# Optimizing a Trainium2 kernel written in Bass

```python
import numpy as np
import jax
import jax.numpy as jnp

def _softmax(x, axis=-1):
    return jax.nn.softmax(x, axis=axis)

def _gelu(x):
    return jax.nn.gelu(x, approximate=True)

def _silu(x):
    return jax.nn.silu(x)

def _sigmoid(x):
    return jax.nn.sigmoid(x)

def _layernorm(x, axis=-1, eps=1e-05):
    m = jnp.mean(x, axis=axis, keepdims=True)
    v = jnp.var(x, axis=axis, keepdims=True)
    return (x - m) / jnp.sqrt(v + eps)

def _scatter_add(tgt, idx, src, axis=0):
    return tgt.at[idx].add(src)

def _segment_sum(src, seg, n):
    return jax.ops.segment_sum(src, seg, n)
kernel_name = 'mk_prb_d2_jaxref_r8_2e6dd8'

def setup_inputs(seed: int=0):
    np.random.seed(seed)
    _w = jnp.asarray

    def _L0_attn_setup():
        import jax, jax.numpy as jnp
        import numpy as np
        B, L, DM, H, HD, K = (4, 256, 128, 16, 64, 64)
        BASE_LR = 1.0
        EPS = 1e-06

        def _ttt_forward(hidden_states, wq, wk, wv, wo, W1, b1, theta, theta_bias, alpha, gamma, beta):
            Bs, Ls, _ = hidden_states.shape
            n_chunks = Ls // K

            def proj(w):
                return (hidden_states @ w).reshape(Bs, Ls, H, HD).transpose(0, 2, 1, 3)
            xq, xk, xv = (proj(wq), proj(wk), proj(wv))

            def to_chunks(x):
                return x.reshape(Bs, H, n_chunks, K, HD).transpose(2, 0, 1, 3, 4)
            cq, ck, cv = (to_chunks(xq), to_chunks(xk), to_chunks(xv))
            token_eta = jnp.clip(1.0 / jnp.arange(1, K + 1, dtype=jnp.float32) + alpha, 0.0)[None, None, :, None]
            g = gamma[None]
            be = beta[None]
            tb = theta_bias.reshape(1, H, 1, 1)
            W0 = jnp.broadcast_to(W1[None], (Bs, H, HD, HD))
            b0 = jnp.broadcast_to(b1[None], (Bs, H, 1, HD))

            def step(carry, inp):
                W, bb = carry
                xq_c, xk_c, xv_c = inp
                lr = jax.nn.sigmoid(jnp.einsum('bhkc,hcd->bhkd', xk_c, theta) + tb)
                eta = token_eta * (BASE_LR * lr / HD)
                Z1 = xk_c @ W + bb
                mu = Z1.mean(-1, keepdims=True)
                std = jnp.sqrt(Z1.var(-1, keepdims=True) + EPS)
                x_hat = (Z1 - mu) / std
                y = g * x_hat + be
                grad_output = y - (xv_c - xk_c)
                gxh = grad_output * g
                grad_x = (HD * gxh - gxh.sum(-1, keepdims=True) - x_hat * (gxh * x_hat).sum(-1, keepdims=True)) / (HD * std)
                dW = jnp.einsum('bhkc,bhkd->bhcd', eta * xk_c, grad_x)
                db = (eta * grad_x).sum(-2, keepdims=True)
                Wn, bn = (W - dW, bb - db)
                Zq = xq_c @ Wn + bn
                mu2 = Zq.mean(-1, keepdims=True)
                std2 = jnp.sqrt(Zq.var(-1, keepdims=True) + EPS)
                out = xq_c + g * ((Zq - mu2) / std2) + be
                return ((Wn, bn), out)
            _, outs = jax.lax.scan(step, (W0, b0), (cq, ck, cv))
            out = outs.transpose(1, 2, 0, 3, 4).reshape(Bs, H, Ls, HD)
            out = out.transpose(0, 2, 1, 3).reshape(Bs, Ls, H * HD)
            return out @ wo
        key = jax.random.key(seed)
        ks = jax.random.split(key, 8)
        s = 0.02
        return {'hidden_states': jax.random.normal(ks[0], (B, L, DM), jnp.float32), 'wq': jax.random.normal(ks[1], (DM, H * HD), jnp.float32) * s, 'wk': jax.random.normal(ks[2], (DM, H * HD), jnp.float32) * s, 'wv': jax.random.normal(ks[3], (DM, H * HD), jnp.float32) * s, 'wo': jax.random.normal(ks[4], (H * HD, DM), jnp.float32) * s, 'W1': jax.random.normal(ks[5], (H, HD, HD), jnp.float32) * s, 'b1': jnp.zeros((H, 1, HD), jnp.float32), 'theta': jax.random.normal(ks[6], (H, HD, 1), jnp.float32) * s, 'theta_bias': jnp.zeros((H, 1, 1), jnp.float32), 'alpha': jnp.zeros((K,), jnp.float32), 'gamma': jnp.ones((H, 1, HD), jnp.float32), 'beta': jnp.zeros((H, 1, HD), jnp.float32)}
    _L0_attn_in = _L0_attn_setup()

    def _L0_ffn_setup():
        import jax, jax.numpy as jnp
        import numpy as np
        K = 32
        key = jax.random.key(seed)
        ks = jax.random.split(key, 9)
        B, S, D, O, E = (8, 256, 128, 128, 16)

        def xavier(k_, shape):
            fan_in, fan_out = (shape[-2], shape[-1])
            lim = (6.0 / (fan_in + fan_out)) ** 0.5
            return jax.random.uniform(k_, shape, jnp.float32, -lim, lim)
        return {'x': jax.random.normal(ks[0], (B, S, D), jnp.float32), 'Wg': xavier(ks[1], (D, E)), 'bg': jnp.zeros((E,), jnp.float32), 'w1': xavier(ks[2], (E, D, O)), 'b1': xavier(ks[3], (E, 1)), 'w2': xavier(ks[4], (E, O, O)), 'b2': xavier(ks[5], (E, 1)), 'w3': xavier(ks[6], (E, O, O)), 'b3': xavier(ks[7], (E, 1))}
    _L0_ffn_in = _L0_ffn_setup()

    def _L1_attn_setup():
        import jax, jax.numpy as jnp
        import numpy as np
        D_MODEL = 128
        NUM_HEADS = 16
        HEAD_DIM = D_MODEL // NUM_HEADS
        EPS = 1e-08
        key = jax.random.key(seed)
        ks = jax.random.split(key, 6)
        B, T = (4, 256)
        s = 0.02
        return {'x': jax.random.normal(ks[0], (B, T, D_MODEL), dtype=jnp.float32), 'Wq': jax.random.normal(ks[1], (D_MODEL, D_MODEL), dtype=jnp.float32) * s, 'Wk': jax.random.normal(ks[2], (D_MODEL, D_MODEL), dtype=jnp.float32) * s, 'Wv': jax.random.normal(ks[3], (D_MODEL, D_MODEL), dtype=jnp.float32) * s, 'Wo': jax.random.normal(ks[4], (D_MODEL, D_MODEL), dtype=jnp.float32) * s, 'bo': jnp.zeros((D_MODEL,), dtype=jnp.float32)}
    _L1_attn_in = _L1_attn_setup()

    def _L1_ffn_setup():
        import jax, jax.numpy as jnp
        import numpy as np
        B, S, H, F, E, R, TOPK = (4, 256, 128, 512, 4, 4, 2)

        def _more_forward(x, Wg, bg, W1, b1, W2, b2):
            b, s, h = x.shape
            cur = x
            for r in range(R):
                flat = cur.reshape(-1, h)
                logits = flat @ Wg[r] + bg[r]
                vals, idx = jax.lax.top_k(logits, TOPK)
                w = jax.nn.softmax(vals, axis=-1)
                cw = jnp.sum(jax.nn.one_hot(idx, E, dtype=flat.dtype) * w[..., None], axis=1)
                hmid = jax.nn.gelu(jnp.einsum('nh,ehf->enf', flat, W1) + b1[:, None, :])
                y = jnp.einsum('enf,efh->enh', hmid, W2) + b2[:, None, :]
                out = jnp.einsum('ne,enh->nh', cw, y)
                cur = cur + out.reshape(b, s, h)
            return cur
        key = jax.random.key(seed)
        ks = jax.random.split(key, 8)
        scale = 0.02
        return {'x': jax.random.normal(ks[0], (B, S, H), dtype=jnp.float32), 'Wg': jax.random.normal(ks[1], (R, H, E), dtype=jnp.float32) * scale, 'bg': jnp.zeros((R, E), dtype=jnp.float32), 'W1': jax.random.normal(ks[2], (E, H, F), dtype=jnp.float32) * scale, 'b1': jnp.zeros((E, F), dtype=jnp.float32), 'W2': jax.random.normal(ks[3], (E, F, H), dtype=jnp.float32) * scale, 'b2': jnp.zeros((E, H), dtype=jnp.float32)}
    _L1_ffn_in = _L1_ffn_setup()
    _d = {'L0_attn_hidden_states': _L0_attn_in['hidden_states'], 'L0_attn_wq': _L0_attn_in['wq'], 'L0_attn_wk': _L0_attn_in['wk'], 'L0_attn_wv': _L0_attn_in['wv'], 'L0_attn_wo': _L0_attn_in['wo'], 'L0_attn_W1': _L0_attn_in['W1'], 'L0_attn_b1': _L0_attn_in['b1'], 'L0_attn_theta': _L0_attn_in['theta'], 'L0_attn_theta_bias': _L0_attn_in['theta_bias'], 'L0_attn_alpha': _L0_attn_in['alpha'], 'L0_attn_gamma': _L0_attn_in['gamma'], 'L0_attn_beta': _L0_attn_in['beta'], 'L0_ffn_Wg': _L0_ffn_in['Wg'], 'L0_ffn_bg': _L0_ffn_in['bg'], 'L0_ffn_w1': _L0_ffn_in['w1'], 'L0_ffn_b1': _L0_ffn_in['b1'], 'L0_ffn_w2': _L0_ffn_in['w2'], 'L0_ffn_b2': _L0_ffn_in['b2'], 'L0_ffn_w3': _L0_ffn_in['w3'], 'L0_ffn_b3': _L0_ffn_in['b3'], 'L1_attn_Wq': _L1_attn_in['Wq'], 'L1_attn_Wk': _L1_attn_in['Wk'], 'L1_attn_Wv': _L1_attn_in['Wv'], 'L1_attn_Wo': _L1_attn_in['Wo'], 'L1_attn_bo': _L1_attn_in['bo'], 'L1_ffn_Wg': _L1_ffn_in['Wg'], 'L1_ffn_bg': _L1_ffn_in['bg'], 'L1_ffn_W1': _L1_ffn_in['W1'], 'L1_ffn_b1': _L1_ffn_in['b1'], 'L1_ffn_W2': _L1_ffn_in['W2'], 'L1_ffn_b2': _L1_ffn_in['b2']}
    _x0 = _d['L0_attn_hidden_states']
    _d['L0_attn_hidden_states'] = jax.random.normal(jax.random.fold_in(jax.random.key(seed), 1), (4, 512, 128), dtype=_x0.dtype)
    del _x0
    return _d

def reference(L0_attn_hidden_states, L0_attn_wq, L0_attn_wk, L0_attn_wv, L0_attn_wo, L0_attn_W1, L0_attn_b1, L0_attn_theta, L0_attn_theta_bias, L0_attn_alpha, L0_attn_gamma, L0_attn_beta, L0_ffn_Wg, L0_ffn_bg, L0_ffn_w1, L0_ffn_b1, L0_ffn_w2, L0_ffn_b2, L0_ffn_w3, L0_ffn_b3, L1_attn_Wq, L1_attn_Wk, L1_attn_Wv, L1_attn_Wo, L1_attn_bo, L1_ffn_Wg, L1_ffn_bg, L1_ffn_W1, L1_ffn_b1, L1_ffn_W2, L1_ffn_b2):

    def _L0_attn_ref(hidden_states, wq, wk, wv, wo, W1, b1, theta, theta_bias, alpha, gamma, beta):
        import jax, jax.numpy as jnp
        import numpy as np
        B, L, DM, H, HD, K = (4, 256, 128, 16, 64, 64)
        BASE_LR = 1.0
        EPS = 1e-06

        def _ttt_forward(hidden_states, wq, wk, wv, wo, W1, b1, theta, theta_bias, alpha, gamma, beta):
            Bs, Ls, _ = hidden_states.shape
            n_chunks = Ls // K

            def proj(w):
                return (hidden_states @ w).reshape(Bs, Ls, H, HD).transpose(0, 2, 1, 3)
            xq, xk, xv = (proj(wq), proj(wk), proj(wv))

            def to_chunks(x):
                return x.reshape(Bs, H, n_chunks, K, HD).transpose(2, 0, 1, 3, 4)
            cq, ck, cv = (to_chunks(xq), to_chunks(xk), to_chunks(xv))
            token_eta = jnp.clip(1.0 / jnp.arange(1, K + 1, dtype=jnp.float32) + alpha, 0.0)[None, None, :, None]
            g = gamma[None]
            be = beta[None]
            tb = theta_bias.reshape(1, H, 1, 1)
            W0 = jnp.broadcast_to(W1[None], (Bs, H, HD, HD))
            b0 = jnp.broadcast_to(b1[None], (Bs, H, 1, HD))

            def step(carry, inp):
                W, bb = carry
                xq_c, xk_c, xv_c = inp
                lr = jax.nn.sigmoid(jnp.einsum('bhkc,hcd->bhkd', xk_c, theta) + tb)
                eta = token_eta * (BASE_LR * lr / HD)
                Z1 = xk_c @ W + bb
                mu = Z1.mean(-1, keepdims=True)
                std = jnp.sqrt(Z1.var(-1, keepdims=True) + EPS)
                x_hat = (Z1 - mu) / std
                y = g * x_hat + be
                grad_output = y - (xv_c - xk_c)
                gxh = grad_output * g
                grad_x = (HD * gxh - gxh.sum(-1, keepdims=True) - x_hat * (gxh * x_hat).sum(-1, keepdims=True)) / (HD * std)
                dW = jnp.einsum('bhkc,bhkd->bhcd', eta * xk_c, grad_x)
                db = (eta * grad_x).sum(-2, keepdims=True)
                Wn, bn = (W - dW, bb - db)
                Zq = xq_c @ Wn + bn
                mu2 = Zq.mean(-1, keepdims=True)
                std2 = jnp.sqrt(Zq.var(-1, keepdims=True) + EPS)
                out = xq_c + g * ((Zq - mu2) / std2) + be
                return ((Wn, bn), out)
            _, outs = jax.lax.scan(step, (W0, b0), (cq, ck, cv))
            out = outs.transpose(1, 2, 0, 3, 4).reshape(Bs, H, Ls, HD)
            out = out.transpose(0, 2, 1, 3).reshape(Bs, Ls, H * HD)
            return out @ wo
        return _ttt_forward(hidden_states, wq, wk, wv, wo, W1, b1, theta, theta_bias, alpha, gamma, beta)

    def _L0_ffn_ref(x, Wg, bg, w1, b1, w2, b2, w3, b3):
        import jax, jax.numpy as jnp
        import numpy as np
        K = 32
        B, S, D = x.shape
        E, _, O = w1.shape
        logits = jnp.einsum('bsd,de->bse', x, Wg) + bg
        probs = jax.nn.softmax(logits, axis=-2)
        pv = jnp.transpose(probs, (0, 2, 1))
        vals, idx = jax.lax.top_k(pv, K)
        bidx = jnp.arange(B)[:, None, None]
        tok = x[bidx, idx]
        b1b = b1[None, :, None, :]
        b2b = b2[None, :, None, :]
        b3b = b3[None, :, None, :]
        h = jax.nn.relu(jnp.einsum('bekd,edo->beko', tok, w1) + b1b)
        h = jax.nn.relu(jnp.einsum('bekd,edo->beko', h, w2) + b2b)
        h = jnp.einsum('bekd,edo->beko', h, w3) + b3b
        out = h * vals[..., None]
        outputs = jnp.zeros((B, S, O), x.dtype).at[bidx, idx].add(out)
        return outputs

    def _L1_attn_ref(x, Wq, Wk, Wv, Wo, bo):
        import jax, jax.numpy as jnp
        import numpy as np
        D_MODEL = 128
        NUM_HEADS = 16
        HEAD_DIM = D_MODEL // NUM_HEADS
        EPS = 1e-08
        B, T, _ = x.shape
        H, D = (NUM_HEADS, HEAD_DIM)
        scale = jnp.sqrt(jnp.asarray(D, dtype=x.dtype))
        q = (x @ Wq.T).reshape(B, T, H, D).transpose(0, 2, 1, 3)
        k = (x @ Wk.T).reshape(B, T, H, D).transpose(0, 2, 1, 3)
        v = (x @ Wv.T).reshape(B, T, H, D).transpose(0, 2, 1, 3)
        s = jnp.einsum('bhtd,bhsd->bhts', q, k) / scale
        m = jnp.max(s, axis=-1, keepdims=True)
        e = jnp.exp(s - m)
        num = jnp.einsum('bhts,bhsd->bhtd', e, v)
        den = jnp.sum(e, axis=-1, keepdims=True) + EPS
        out = (num / den).transpose(0, 2, 1, 3).reshape(B, T, H * D)
        return out @ Wo.T + bo

    def _L1_ffn_ref(x, Wg, bg, W1, b1, W2, b2):
        import jax, jax.numpy as jnp
        import numpy as np
        B, S, H, F, E, R, TOPK = (4, 256, 128, 512, 4, 4, 2)

        def _more_forward(x, Wg, bg, W1, b1, W2, b2):
            b, s, h = x.shape
            cur = x
            for r in range(R):
                flat = cur.reshape(-1, h)
                logits = flat @ Wg[r] + bg[r]
                vals, idx = jax.lax.top_k(logits, TOPK)
                w = jax.nn.softmax(vals, axis=-1)
                cw = jnp.sum(jax.nn.one_hot(idx, E, dtype=flat.dtype) * w[..., None], axis=1)
                hmid = jax.nn.gelu(jnp.einsum('nh,ehf->enf', flat, W1) + b1[:, None, :])
                y = jnp.einsum('enf,efh->enh', hmid, W2) + b2[:, None, :]
                out = jnp.einsum('ne,enh->nh', cw, y)
                cur = cur + out.reshape(b, s, h)
            return cur
        return _more_forward(x, Wg, bg, W1, b1, W2, b2)
    x = L0_attn_hidden_states
    xn = _layernorm(x, axis=-1)
    x = x + _L0_attn_ref(xn, L0_attn_wq, L0_attn_wk, L0_attn_wv, L0_attn_wo, L0_attn_W1, L0_attn_b1, L0_attn_theta, L0_attn_theta_bias, L0_attn_alpha, L0_attn_gamma, L0_attn_beta) + _L0_ffn_ref(xn, L0_ffn_Wg, L0_ffn_bg, L0_ffn_w1, L0_ffn_b1, L0_ffn_w2, L0_ffn_b2, L0_ffn_w3, L0_ffn_b3)
    xn = _layernorm(x, axis=-1)
    x = x + _L1_attn_ref(xn, L1_attn_Wq, L1_attn_Wk, L1_attn_Wv, L1_attn_Wo, L1_attn_bo) + _L1_ffn_ref(xn, L1_ffn_Wg, L1_ffn_bg, L1_ffn_W1, L1_ffn_b1, L1_ffn_W2, L1_ffn_b2)
    return x

_drawn_inputs = setup_inputs


def setup_inputs(seed=0):
    import zlib

    import numpy as np

    out = dict(_drawn_inputs(seed))
    spreads = {'L0_attn_b1': (0.0, 0.1),
     'L0_attn_theta_bias': (0.0, 2.0),
     'L0_attn_alpha': (0.0, 0.581),
     'L0_attn_gamma': (1.0, 0.2),
     'L0_attn_beta': (0.0, 0.459),
     'L0_ffn_bg': (0.0, 2.0),
     'L1_attn_bo': (0.0, 2.0),
     'L1_ffn_bg': (0.0, 0.8),
     'L1_ffn_b1': (0.0, 2.0),
     'L1_ffn_b2': (0.0, 0.648)}
    factors = {'L0_attn_theta': 64.0,
     'L0_ffn_Wg': 4.699,
     'L0_ffn_w1': 7.368,
     'L0_ffn_b1': 8.0,
     'L0_ffn_w2': 6.395,
     'L0_ffn_b2': 8.0,
     'L0_ffn_w3': 4.841,
     'L0_ffn_b3': 158.589,
     'L1_attn_Wq': 46.986,
     'L1_attn_Wk': 45.806,
     'L1_attn_Wv': 37.14,
     'L1_attn_Wo': 34.051,
     'L0_attn_wk': 3.595,
     'L0_attn_wv': 5.431,
     'L0_attn_W1': 3.662,
     'L1_ffn_Wg': 7.142,
     'L1_ffn_W1': 7.755,
     'L1_ffn_W2': 4.921}
    for name, (base, spread) in spreads.items():
        noise = np.random.default_rng([zlib.crc32(name.encode()), seed]).standard_normal(out[name].shape)
        drawn = base * np.exp(spread * noise) if base else spread * noise
        out[name] = jnp.asarray(drawn.astype(out[name].dtype))
    for name, factor in factors.items():
        out[name] = (out[name] * factor).astype(out[name].dtype)
    return out
```

```python
from contextlib import ExitStack

import concourse.bass as bass
from concourse import mybir

F32 = mybir.dt.float32
F32R = mybir.dt.float32r
ALU = mybir.AluOpType
ACT = mybir.ActivationFunctionType
AX_X = mybir.AxisListType.X

P = 128
B, S = 4, 512
NT = S // P
H, HD = 16, 64
NP = H // 2
K = 64
NC = S // K
D = H * HD
W = NP * HD
E0, TOP0 = 16, 32
AH, AD = 16, 8
QH = 4
NQ = AH // QH
E1, F1, R1 = 4, 512, 4
NF = F1 // P

CONST = {}


def constants(np):
    cols, at = [], 0

    def put(name, a):
        nonlocal at
        full = np.zeros((P, a.shape[1]), np.float32)
        full[:a.shape[0]] = a
        cols.append(full)
        CONST[name] = (at, a.shape[0], a.shape[1])
        at += a.shape[1]

    part = np.arange(P)
    put("ident", np.eye(P))
    half = (part[None, :] // K == np.arange(2)[:, None]).astype(np.float32)
    put("half", half)
    put("half_t", half.T)
    mean = np.zeros((P, NP, H))
    spread = np.zeros((H, NP, P))
    for p in range(NP):
        for hh in range(2):
            mean[hh * HD:(hh + 1) * HD, p, 2 * p + hh] = 1.0 / HD
            spread[2 * p + hh, p, hh * HD:(hh + 1) * HD] = 1.0
    put("mean", mean.reshape(P, NP * H))
    put("spread", spread.reshape(H, NP * P))
    put("token_rate", (1.0 / (part % K + 1))[:, None])
    put("slots", np.tile(np.arange(1, TOP0 + 1)[None], (P, 1)))
    low = (np.arange(E1)[None, :] < np.arange(E1)[:, None]).astype(np.float32)
    put("lower", np.tile(low.reshape(1, -1), (P, 1)))
    row = part % 32
    put("q_minus", -(((row >= 8) & (row < 16)) | (row == 25)).astype(np.float32)[:, None])
    put("k_minus", (-((row >= 16) & (row < 24)).astype(np.float32)
                    + ((row == 24) | (row == 25)))[:, None])
    put("k_ones", ((row == 24) | (row == 25)).astype(np.float32)[:, None])
    put("ln_eps", np.full((P, 1), 1e-5))
    put("ttt_eps", np.full((P, 1), 1e-6))
    return np.concatenate(cols, 1).astype(np.float32)


def build(nc, A, out, const_d, dbg=None):
    with ExitStack() as ctx:
        def sb(name, shape, dt=F32):
            return ctx.enter_context(nc.sbuf_tensor(name, shape, dt))

        def sem(name):
            return ctx.enter_context(nc.semaphore(name))

        bank = [ctx.enter_context(nc.psum_tensor(f"bank{n}", [P, 512], F32)) for n in range(8)]

        cst = sb("cst", [P, const_d.shape[1]])
        x1 = sb("x1", [P, B * NT, P])
        xsq = x1
        W2 = sb("W2", [P, E1, NF, P])
        w4 = sb("w4", [P, 4, P])
        b1r = sb("b1r", [E1 * NF, P])
        b2r = sb("b2r", [E1, P])
        boB = sb("boB", [P, P])
        Wg1 = sb("Wg1", [P, R1, E1])
        bgB = sb("bgB", [P, R1, E1])

        first_layer = ExitStack()

        def sb(name, shape, dt=F32):
            return first_layer.enter_context(nc.sbuf_tensor(name, shape, dt))

        PIECE = B * W
        arena = sb("arena", [P, 10 * PIECE])

        def piece(k, n=PIECE, off=0):
            return arena[:, k * PIECE + off:k * PIECE + off + n]

        def C(name):
            at, rows, width = CONST[name]
            return cst[0:rows, at:at + width]

        ident, half, half_t = C("ident"), C("half"), C("half_t")
        mean = C("mean").rearrange("p (a h) -> p a h", a=NP)
        spread = C("spread").rearrange("p (a c) -> p a c", a=NP)

        x = sb("x", [P, B * NT, P])
        xn = sb("xn", [P, B * NT, P])
        st = sb("st", [P, 4, B * NT])
        xnT = sb("xnT", [P, B * S])
        wq = sb("wq", [P, D])
        wk = sb("wk", [P, D])
        wv = piece(7, D, D)
        wo = piece(8, D).rearrange("p (a c) -> p a c", a=NP)
        wog = sb("wog", [P, NP, P])
        wqT = piece(6, D).rearrange("p (a c) -> p a c", a=NP)
        gam = sb("gam", [P, NP])
        bet = sb("bet", [P, NP])
        gamB = piece(6, D, D)
        gg = sb("gg", [P, W])
        gb2 = piece(8, D, D).rearrange("p (k w) -> p k w", k=2)[0:2]
        gbeta = sb("gbeta", [2, W])
        wu = sb("wu", [P, D])
        th = piece(7, D)
        Th = sb("Th", [P, H])
        tbA = sb("tbA", [P, H])
        tb = sb("tb", [P, NP])
        alpha = sb("alpha", [P, 1])
        rate = sb("rate", [P, 1])
        eta = sb("eta", [P, NC, B, NP])
        Wst = sb("Wst", [P, B, NP, HD])
        Bst = sb("Bst", [2, B, W])
        m0 = sb("m0", [P, 2, NP])
        Wqo = sb("Wqo", [P, P])
        bo0 = sb("bo0", [P, 1])
        attnT = sb("attnT", [P, B * S])

        xnc = sb("xnc", [P, B, K])
        kT = piece(0).rearrange("p (b a c) -> p b a c", b=B, a=NP)
        qT = piece(1).rearrange("p (b a c) -> p b a c", b=B, a=NP)
        XK = piece(2).rearrange("p (b a c) -> p b a c", b=B, a=NP)
        U = piece(3).rearrange("p (b w) -> p b w", b=B)
        sqz = piece(4, PIECE // 2).rearrange("p (b w) -> p b w", b=2)
        xh = piece(5).rearrange("p (b w) -> p b w", b=B)
        t1 = piece(6).rearrange("p (b w) -> p b w", b=B)
        gx = piece(7).rearrange("p (b w) -> p b w", b=B)
        gw = piece(8).rearrange("p (b w) -> p b w", b=B)
        sm = sb("sm", [P, B, 7, NP])
        zq = piece(9, PIECE // 2).rearrange("p (b w) -> p b w", b=2)
        sq2 = piece(4, PIECE // 2, PIECE // 2).rearrange("p (b w) -> p b w", b=2)
        rq = sb("rq", [H, B, 2, K])
        Am = piece(9, PIECE // 2, PIECE // 2).rearrange("p (b w) -> p b w", b=2)

        BE = B * E0
        wg0 = sb("wg0", [P, E0])
        wgP = sb("wgP", [P, B, BE])
        bg0 = sb("bg0", [BE, 1])
        ew = [sb(f"ew{n}", [P, E0, P]) for n in range(3)]
        eb = sb("eb", [P, 3, E0])
        b3s = sb("b3s", [P, E0 // 4])
        lgt = piece(9, S)[0:BE]
        wrk = piece(9, 2 * S, 2 * S).rearrange("p (k s) -> p k s", k=2)[0:BE]
        m8 = sb("m8", [BE, 4, 8])
        es = sb("es", [BE, 4])
        rkp = piece(5, 2 * S).rearrange("p (k s) -> p k s", k=2)[0:BE]
        rpT = sb("rpT", [P, 2, NT, BE])
        OH = piece(0, 2 * PIECE).rearrange("p (q t k) -> p q t k", q=2, t=NT)
        WP = piece(2).rearrange("p (t k) -> p t k", t=NT)
        WPT = piece(3, 4 * PIECE).rearrange("p (b g s) -> p b g s", b=B, g=E0 // 4)
        tokT = piece(7).rearrange("p (b e k) -> p b e k", b=B, e=E0)
        h1 = piece(8).rearrange("p (e s) -> p e s", e=E0)
        h2 = piece(0).rearrange("p (e s) -> p e s", e=E0)
        o3 = piece(1).rearrange("p (g b d) -> p g b d", g=E0 // 4, b=B)
        first_layer.close()

        def sb(name, shape, dt=F32):
            return ctx.enter_context(nc.sbuf_tensor(name, shape, dt))

        QW = QH * 32
        W1r = sb("W1r", [P, E1, F1])
        W1h = sb("W1h", [P, E1, F1], F32R)
        W1l = sb("W1l", [P, E1, F1], F32R)
        wr = sb("wr", [P, 2, NQ, QW])
        wrh = sb("wrh", [P, 2, NQ, QW], F32R)
        wrl = sb("wrl", [P, 2, NQ, QW], F32R)
        wT4 = sb("wT4", [P, 4, P])
        b1c = sb("b1c", [P, E1 * NF])
        xn2 = sb("xn2", [P, B * NT, P])
        st2 = sb("st2", [P, 4, B * NT])
        xn2T = sb("xn2T", [P, B * S])
        cur = sb("cur", [P, NT, P])
        curT = sb("curT", [P, S])
        xH = sb("xH", [P, S], F32R)
        xL = sb("xL", [P, S], F32R)
        cH = sb("cH", [P, S], F32R)
        cL = sb("cL", [P, S], F32R)
        hi = sb("hi", [P, 2, S], F32R)
        kx = sb("kx", [P, 2, S], F32R)
        qx = sb("qx", [P, S], F32R)
        qm = sb("qm", [P, S], F32R)
        Mt = sb("Mt", [P, NT, QW])
        Vx = sb("Vx", [P, NT, AH, 32])
        ex = sb("ex", [P, 4, S])
        hb = sb("hb", [P, 4, S])
        ob = sb("ob", [P, S])
        den = sb("den", [P, 2, NT, QH])
        an = sb("an", [P, NT, P])
        aT = sb("aT", [P, S])
        lg = sb("lg", [P, NT, E1])
        lgx = sb("lgx", [P, 3, NT, E1 * E1])
        gt = sb("gt", [P, 8, NT * E1])
        cw = sb("cw", [P, NT, E1])
        cwT = sb("cwT", [E1, S])
        fin = sb("fin", [P, NT, P])
        sq_2 = sb("sq_2", [P, B * NT, P])
        ld_2, ld_1 = sem("ld_2"), sem("ld_1")
        l2_v, l2_a, l2_g = sem("l2_v"), sem("l2_a"), sem("l2_g")
        t2_p, t2_a, w2p, w2a, w2v = sem("t2_p"), sem("t2_a"), sem("w2p"), sem("w2a"), sem("w2v")
        N_L1 = ("cur_p", "cur_a", "cs_v", "cc_v", "pr_p", "pr_a", "pr_v", "v_p", "v_v", "s1_p", "s1_v", "mt_v", "h_p", "h_a", "w_p", "y_v",
                "pv_p", "o_a", "o_p", "o_v", "lg_p2", "lg_v2", "z_v", "e_a", "cw_v", "ct_p", "ct_a", "cb_p", "cb_v", "at2_p", "at2_a", "ao_p",
                "fin_v", "out_d", "v1")
        L_ = {n: sem("L" + n) for n in N_L1}
        ld_m = sem("ld_m")
        wg_v, lg_p, lg_v, ex_a, rk_v, rT_p, rT_a = (sem(n) for n in ("wg_v", "lg_p", "lg_v", "ex_a", "rk_v", "rT_p", "rT_a"))
        oh_v, wp_g, mj_p, mj_a, sc_p, x1_v = (sem(n) for n in ("oh_v", "wp_g", "mj_p", "mj_a", "sc_p", "x1_v"))
        ld_x, ld_c, ld_w, ld_s = sem("ld_x"), sem("ld_c"), sem("ld_w"), sem("ld_s")
        ln_sq, ln_sd, ln_xn = sem("ln_sq"), sem("ln_sd"), sem("ln_xn")
        tr_n, tr_c = sem("tr_n"), sem("tr_c")
        vs = sem("vs")
        gs = sem("gs")
        prep_v, prep_g, prep_a, prep_p = sem("prep_v"), sem("prep_g"), sem("prep_a"), sem("prep_p")
        lr_p, lr_v, lr_a, eta_v = sem("lr_p"), sem("lr_v"), sem("lr_a"), sem("eta_v")
        state_v = sem("state_v")
        N_UNIT = ("xnc_g", "pj_p", "pj_a", "z_p", "sqz_a", "ss_v", "sd_a", "xh_v", "t_g", "gx_v", "q_g", "s2_v",
                  "v_g", "w_v", "gw_g", "w1_v", "dw_p", "up_v", "zq_p", "zq_a", "var_p", "sdq_a", "rq_v",
                  "bc_p", "A_v", "at_p", "at_a", "s1_v", "a_v", "c_v", "zs_a")
        U_ = {n: sem(n) for n in N_UNIT}
        BASE = 1
        done = sem("done")

        block = ctx.enter_context(nc.Block())

        w3 = lambda t: t.rearrange("p (a h c) -> p a h c", a=NP, h=2)

        @block.sync
        def _(sp):
            for one in (*U_.values(), *L_.values()):
                sp.sem_inc(one, BASE)
            sp.dma_start(x[:, :, :], A["L0_attn_hidden_states"].rearrange("b (t p) d -> p (b t) d", p=P)).then_inc(ld_x, 16)
            sp.dma_start(wk[:, :], A["L0_attn_wk"]).then_inc(ld_w, 16)
            sp.dma_start(wv[:, :], A["L0_attn_wv"]).then_inc(ld_w, 16)
            sp.dma_start(wq[:, :], A["L0_attn_wq"]).then_inc(ld_w, 16)
            sp.dma_start(wo[:, :, :], A["L0_attn_wo"].rearrange("(a q) n -> q a n", q=P)).then_inc(ld_w, 16)
            for hh in range(2):
                src = A["L0_attn_W1"].rearrange("(a h) c d -> h c a d", h=2)[hh]
                sp.dma_start(Wst[hh * 64:hh * 64 + 64, 0, :, :], src).then_inc(ld_w, 16)
            sp.dma_start(wg0[:, :], A["L0_ffn_Wg"]).then_inc(ld_m, 16)
            for b in range(B):
                sp.dma_start(bg0[b * E0:(b + 1) * E0, :], A["L0_ffn_bg"].rearrange("(e o) -> e o", o=1)).then_inc(ld_m, 16)
            for n in range(3):
                sp.dma_start(ew[n][:, :, :], A[f"L0_ffn_w{n + 1}"].rearrange("e d o -> d e o")).then_inc(ld_m, 16)
                sp.dma_start(eb[:, n, :], A[f"L0_ffn_b{n + 1}"].rearrange("e o -> o e").broadcast_to([P, E0])).then_inc(ld_m, 16)
            sp.dma_start(W2[:, :, :, :], A["L1_ffn_W2"].rearrange("e (a q) h -> q e a h", q=P)).then_inc(ld_2, 16)
            for n, name in enumerate(("Wq", "Wk", "Wv", "Wo")):
                sp.dma_start(w4[:, n, :], A["L1_attn_" + name]).then_inc(ld_2, 16)
            sp.dma_start(b1r[:, :], A["L1_ffn_b1"].rearrange("e (a q) -> (e a) q", q=P)).then_inc(ld_2, 16)
            sp.dma_start(b2r[:, :], A["L1_ffn_b2"]).then_inc(ld_2, 16)
            sp.dma_start(boB[:, :], A["L1_attn_bo"].rearrange("(a q) -> a q", a=1).broadcast_to([P, P])).then_inc(ld_2, 16)
            sp.dma_start(Wg1[:, :, :], A["L1_ffn_Wg"].rearrange("r h e -> h r e")).then_inc(ld_2, 16)
            sp.dma_start(bgB[:, :, :].rearrange("p r e -> p (r e)"), A["L1_ffn_bg"].rearrange("(a r) e -> a (r e)", a=1).broadcast_to([P, R1 * E1])).then_inc(ld_2, 16)
            sp.wait_ge(x1_v, B)
            sp.dma_start(W1r[:, :, :], A["L1_ffn_W1"].rearrange("e h f -> h e f")).then_inc(ld_1, 16)
            out_v = out.rearrange("b (t p) d -> p b t d", p=P)
            with sp.Fori(0, B) as i:
                sp.wait_ge(L_["fin_v"], i + 1 + BASE)
                sp.dma_start(out_v[:, bass.ds(i, 1), :, :].rearrange("p o t d -> p (o t) d"), fin[:, :, :]).then_inc(L_["out_d"], 16)
            sp.wait_ge(L_["out_d"], 16 * B + BASE)

        N_W, N_S, N_M = 6, 16, 5 + 6
        N_2 = 10

        @block.scalar
        def _(act):
            act.dma_start(cst[:, :], const_d).then_inc(ld_c, 16)
            g = A["L0_attn_gamma"].rearrange("h a d -> a (h d)")
            act.dma_start(gamB[:, :], g.broadcast_to([P, D])).then_inc(ld_s, 16)
            act.dma_start(th[:, :], A["L0_attn_theta"].rearrange("h d a -> a (h d)").broadcast_to([P, D])).then_inc(ld_s, 16)
            for hh in range(2):
                gr = A["L0_attn_gamma"].rearrange("(a h) o d -> h o a d", h=2)[hh]
                br = A["L0_attn_beta"].rearrange("(a h) o d -> h o a d", h=2)[hh]
                b1 = A["L0_attn_b1"].rearrange("(a h) o d -> h o a d", h=2)[hh]
                act.dma_start(gb2[hh:hh + 1, 0, :].rearrange("q (a d) -> q a d", a=NP), gr).then_inc(ld_s, 16)
                act.dma_start(gb2[hh:hh + 1, 1, :].rearrange("q (a d) -> q a d", a=NP), br).then_inc(ld_s, 16)
                act.dma_start(Bst[hh:hh + 1, 0, :].rearrange("q (a d) -> q a d", a=NP), b1).then_inc(ld_s, 16)
                act.dma_start(gam[hh * 64:hh * 64 + 64, :], gr[0].rearrange("a d -> d a"), allow_slow_non_contiguous=True).then_inc(ld_s, 16)
                act.dma_start(bet[hh * 64:hh * 64 + 64, :], br[0].rearrange("a d -> d a"), allow_slow_non_contiguous=True).then_inc(ld_s, 16)
                tr = A["L0_attn_theta_bias"].rearrange("h o d -> o (h d)")
                act.dma_start(tbA[hh * 64:hh * 64 + 64, :], tr.broadcast_to([64, H])).then_inc(ld_s, 16)
                act.dma_start(alpha[hh * 64:hh * 64 + 64, :], A["L0_attn_alpha"].rearrange("(k o) -> k o", o=1)).then_inc(ld_s, 16)
            act.wait_ge(ln_xn, 1)
            act.activation(xsq[:, :, :], xn[:, :, :], ACT.Square).then_inc(ln_sq, 1)
            act.wait_ge(ln_xn, 2)
            act.wait_ge(ld_c, 16)
            act.activation(st[:, 2, :], st[:, 1, :], ACT.Sqrt, bias=C("ln_eps"), scale=1.0 / P).then_inc(ln_sd, 1)
            for n in range(4):
                act.wait_ge(tr_n, n + 1)
                act.activation(xnT[:, n * 512:(n + 1) * 512], bank[n][:, :], ACT.Copy).then_inc(tr_c, 1)
            act.wait_ge(lr_v, 1)
            act.activation(eta[:, :, :, :], eta[:, :, :, :], ACT.Sigmoid).then_inc(lr_a, 1)
            act.wait_ge(prep_p, 1)
            for n in range(2):
                act.activation(wqT[:, 4 * n:4 * n + 4, :], bank[5 + n][:, :], ACT.Copy).then_inc(prep_a, 1)
            act.wait_ge(prep_p, 2)
            act.activation(Wqo[:, :], bank[7][:, 0:P], ACT.Copy).then_inc(prep_a, 1)
            act.activation(bo0[:, :], bank[7][:, P:P + 1], ACT.Copy).then_inc(prep_a, 1)
            act.wait_ge(lg_v, 2)
            act.activation(rkp[:, 1, :], lgt[:, :], ACT.Exp, bias=es[:, 0:1], accum_out=es[:, 1:2]).then_inc(ex_a, 1)
            act.wait_ge(rT_p, 1)
            act.activation(rpT[:, :, :, :], bank[1][:, :].rearrange("p (k t r) -> p k t r", k=2, t=NT), ACT.Copy).then_inc(rT_a, 1)

            def evac(dst, m, n):
                act.wait_ge(U_["pj_p"], n + BASE)
                act.activation(dst, bank[2 + m % 2][:, :], ACT.Copy).then_inc(U_["pj_a"], 1)

            for b in range(B):
                evac(kT[:, b, :, :], b, b + 1)

            def chunk(i, last):
                def sqz_(b):
                    act.wait_ge(U_["z_p"], 4 * i + b + 1 + BASE)
                    act.activation(sqz[:, b % 2, :], bank[b % 2][:, :], ACT.Square).then_inc(U_["sqz_a"], 1)

                def xku(b):
                    if b == 0:
                        act.wait_ge(U_["dw_p"], 4 * i + BASE)
                    evac(XK[:, b, :, :], 2 * b, 16 * i + 4 + 2 * b + 1)
                    evac(U[:, b, :], 2 * b + 1, 16 * i + 4 + 2 * b + 2)

                def std(b):
                    act.wait_ge(U_["ss_v"], 4 * i + b + 1 + BASE)
                    act.activation(sm[:, b, 1, :], sm[:, b, 0, :], ACT.Sqrt, bias=C("ttt_eps"), scale=1.0 / HD).then_inc(U_["sd_a"], 1)

                sqz_(0)
                sqz_(1)
                xku(0)
                std(0)
                xku(1)
                std(1)
                sqz_(2)
                sqz_(3)
                xku(2)
                std(2)
                xku(3)
                std(3)
                for b in range(B):
                    evac(qT[:, b, :, :], b, 16 * i + 12 + b + 1)
                if not last:
                    for b in range(B):
                        evac(kT[:, b, :, :], b, 16 * i + 16 + b + 1)

                def zqs(b):
                    act.wait_ge(U_["zq_p"], 4 * i + b + 1 + BASE)
                    if b >= 2:
                        act.wait_ge(U_["var_p"], 4 * i + b - 1 + BASE)
                        act.wait_ge(U_["A_v"], 4 * i + b - 1 + BASE)
                    act.activation(sq2[:, b % 2, :], bank[b % 2][:, :], ACT.Square).then_inc(U_["zs_a"], 1)
                    act.wait_ge(U_["A_v"], 4 * i + BASE)
                    act.activation(zq[:, b % 2, :], bank[b % 2][:, :], ACT.Copy).then_inc(U_["zq_a"], 1)

                def stdq(b):
                    act.wait_ge(U_["var_p"], 4 * i + b + 1 + BASE)
                    act.activation(rq[:, b, 0, :], bank[7][0:H, b * K:(b + 1) * K], ACT.Sqrt, bias=C("ttt_eps")[0:H, :]).then_inc(U_["sdq_a"], 1)

                def att(b):
                    act.wait_ge(U_["at_p"], 4 * i + b + 1 + BASE)
                    act.activation(attnT[:, bass.ds(b * S + i * K, K)], bank[7][:, 256 + b * K:256 + (b + 1) * K], ACT.Identity,
                                   bias=bo0[:, :]).then_inc(U_["at_a"], 1)

                zqs(0)
                zqs(1)
                stdq(0)
                zqs(2)
                stdq(1)
                zqs(3)
                stdq(2)
                att(0)
                stdq(3)
                att(1)
                att(2)
                att(3)

            act.wait_ge(prep_a, 4)
            with act.Fori(0, NC - 1) as i:
                chunk(i, False)
            chunk(NC - 1, True)

            n = 0
            for b in range(B):
                act.wait_ge(mj_p, n + 1)
                act.activation(tokT[:, b, :, :], bank[n % 4][:, :].rearrange("p (e k) -> p e k", e=E0), ACT.Copy).then_inc(mj_a, 1)
                n += 1
                for g in range(E0 // 4):
                    act.wait_ge(mj_p, n + 1)
                    act.activation(WPT[:, b, g, :], bank[n % 4][:, :], ACT.Copy).then_inc(mj_a, 1)
                    n += 1
            for k, h in enumerate((h1, h2)):
                for g in range(E0 // 4):
                    act.wait_ge(mj_p, n + 1)
                    for j in range(4):
                        last = act.activation(h[:, 4 * g + j, :], bank[n % 4][:, j * P:(j + 1) * P], ACT.Relu, bias=eb[:, k, 4 * g + j:4 * g + j + 1])
                    last.then_inc(mj_a, 1)
                    n += 1
            for g in range(E0 // 4):
                act.wait_ge(mj_p, n + 1)
                act.activation(o3[:, g, :, :], bank[n % 4][:, :].rearrange("p (b d) -> p b d", b=B), ACT.Identity, bias=b3s[:, g:g + 1]).then_inc(mj_a, 1)
                n += 1


            act.wait_ge(l2_v, 1)
            act.activation(sq_2[:, :, :], xn2[:, :, :], ACT.Square).then_inc(l2_a, 1)
            act.wait_ge(l2_v, 2)
            act.activation(st2[:, 2, :], st2[:, 1, :], ACT.Sqrt, bias=C("ln_eps"), scale=1.0 / P).then_inc(l2_a, 1)
            act.wait_ge(w2p, 1)
            act.activation(wT4[:, :, :], bank[0][:, :].rearrange("p (n c) -> p n c", n=4), ACT.Copy).then_inc(w2a, 1)
            act.activation(b1c[:, :], bank[1][:, 0:E1 * NF], ACT.Copy).then_inc(w2a, 1)
            for b in range(B):
                act.wait_ge(t2_p, b + 1)
                act.activation(xn2T[:, b * S:(b + 1) * S], bank[2 + b][:, :], ACT.Copy).then_inc(t2_a, 1)
            act.wait_ge(t2_a, B)
            act.sem_inc(L_["h_a"], 2)
            act.sem_inc(L_["pr_a"], 1)

            def batch(i):
                pr, hj = [0], [0]

                def part():
                    n = pr[0]
                    pr[0] += 1
                    is_k = n in (0, 2, 5, 8)
                    act.wait_ge(L_["pr_p"], 12 * i + n + 1 + BASE)
                    if is_k:
                        last = act.activation(hi[:, n % 2, :], bank[5 + n % 2][:, :], ACT.Identity, bias=C("k_ones"))
                    else:
                        last = act.activation(hi[:, n % 2, :], bank[5 + n % 2][:, :], ACT.Copy)
                    last.then_inc(L_["pr_a"], 1)

                def take(fn, dst, **kw):
                    n = hj[0]
                    hj[0] += 1
                    act.wait_ge(L_["h_p"], 8 * 16 * i + n + 1 + BASE)
                    act.activation(dst, bank[n % 2][:, :], fn, **kw).then_inc(L_["h_a"], 1)

                def gate(r):
                    act.wait_ge(L_["z_v"], R1 * i + r + 1 + BASE)
                    act.activation(gt[:, 1, :], gt[:, 0, :], ACT.Exp).then_inc(L_["e_a"], 1)

                def turned(r):
                    act.wait_ge(L_["ct_p"], R1 * i + r + 1 + BASE)
                    act.activation(cwT[:, :], bank[7][0:E1, :], ACT.Copy).then_inc(L_["ct_a"], 1)

                def hidden():
                    for n in range(E1 * NF):
                        if n >= 4:
                            act.wait_ge(L_["w_p"], WP * i + hid[0] * 16 + n - 3 + BASE)
                        elif hid[0]:
                            act.wait_ge(L_["w_p"], WP * i + hid[0] * 16 - 3 + n + BASE)
                        take(ACT.Gelu_apprx_tanh, hb[:, n % 4, :], bias=b1c[:, n:n + 1])
                    hid[0] += 1

                WP, hid = 16 * R1, [0]
                act.activation(curT[:, :], xn2T[:, bass.ds(i * S, S)], ACT.Copy).then_inc(L_["cur_a"], 1)
                part()
                part()
                gate(0)
                turned(0)
                hidden()
                for j in range(NQ):
                    for _ in range(3 if j < NQ - 1 else 1):
                        part()
                    if j < NQ - 1:
                        act.wait_ge(L_["cur_p"], (R1 - 1) * i + j + 1 + BASE)
                        act.activation(curT[:, :], bank[7][:, :], ACT.Copy).then_inc(L_["cur_a"], 1)
                    for n in range(16):
                        m = 16 * j + n
                        if m >= 4:
                            act.wait_ge(L_["pv_p"], 64 * i + m - 3 + BASE)
                        take(ACT.Exp, ex[:, n % 4, :], scale=float(AD) ** -0.5)
                        if n == 8 and j < NQ - 1:
                            gate(j + 1)
                        if n == 14 and j < NQ - 1:
                            turned(j + 1)
                    act.wait_ge(L_["pv_p"], 64 * i + 16 * (j + 1) + BASE)
                    act.activation(ob[:, :], bank[2][:, :], ACT.Copy).then_inc(L_["o_a"], 1)
                    if j < NQ - 1:
                        hidden()
                act.wait_ge(L_["at2_p"], i + 1 + BASE)
                act.activation(aT[:, :], bank[7][:, :], ACT.Copy).then_inc(L_["at2_a"], 1)

            with act.Fori(0, B) as i:
                batch(i)

        @block.vector
        def _(dve):
            n = [0]

            def link(ins):
                n[0] += 1
                ins.then_inc(vs, 1)
                dve.wait_ge(vs, n[0])

            dve.wait_ge(ld_x, 16)
            bc = lambda t: t.unsqueeze(2).broadcast_to([P, B * NT, P])
            link(dve.tensor_reduce(st[:, 0, :], x[:, :, :], AX_X, ALU.add))
            link(dve.tensor_scalar(st[:, 3, :], st[:, 0, :], 1.0 / P, None, ALU.mult))
            dve.tensor_tensor(xn[:, :, :], x[:, :, :], bc(st[:, 3, :]), ALU.subtract).then_inc(ln_xn, 1)
            dve.wait_ge(ln_sq, 1)
            dve.tensor_reduce(st[:, 1, :], xsq[:, :, :], AX_X, ALU.add).then_inc(ln_xn, 1)
            dve.wait_ge(ln_sd, 1)
            link(dve.reciprocal(st[:, 3, :], st[:, 2, :]))
            for b in range(B):
                dve.tensor_tensor(xn[:, b * NT:(b + 1) * NT, :], xn[:, b * NT:(b + 1) * NT, :],
                                  st[:, 3, b * NT:(b + 1) * NT].unsqueeze(2).broadcast_to([P, NT, P]), ALU.mult).then_inc(ln_xn, 1)
            dve.wait_ge(ld_w, 16 * N_W)
            dve.wait_ge(ld_s, 16 * N_S)
            for hh in range(2):
                r = slice(hh * 64, hh * 64 + 64)
                link(dve.tensor_copy(tb[r, :], tbA[r, :].rearrange("p (a h) -> p h a", h=2)[:, hh, :]))
            link(dve.tensor_tensor(th[:, :], th[:, :], wk[:, :], ALU.mult))
            dve.tensor_reduce(Th[:, :], th[:, :].rearrange("p (h c) -> p h c", h=H), AX_X, ALU.add).then_inc(prep_v, 1)
            link(dve.tensor_tensor(wu[:, :], wk[:, :], wv[:, :], ALU.subtract))
            dve.tensor_tensor(wu[:, :], wu[:, :], gamB[:, :], ALU.mult).then_inc(prep_v, 1)
            for hh in range(2):
                g4 = w3(gamB[:, :])[hh * 64:hh * 64 + 64, :, hh, :]
                last = dve.tensor_tensor(gg[hh * 64:hh * 64 + 64, :].rearrange("p (a c) -> p a c", a=NP), g4, g4, ALU.mult)
            last.then_inc(prep_v, 1)
            dve.tensor_tensor(gbeta[:, :], gb2[:, 0, :], gb2[:, 1, :], ALU.mult).then_inc(prep_v, 1)
            dve.tensor_tensor(wog[:, :, :], wo[:, :, :], gam[:, :].unsqueeze(2).broadcast_to([P, NP, P]), ALU.mult).then_inc(prep_v, 1)
            link(dve.tensor_reduce(m0[:, 0, :], Wst[:, 0, :, :], AX_X, ALU.add))
            link(dve.tensor_scalar(m0[:, 1, :], m0[:, 0, :], 1.0 / HD, None, ALU.mult))
            link(dve.tensor_tensor(Wst[:, 0, :, :], Wst[:, 0, :, :], m0[:, 1, :].unsqueeze(2).broadcast_to([P, NP, HD]), ALU.subtract))
            b0 = Bst[:, 0, :].rearrange("p (a c) -> p a c", a=NP)
            link(dve.tensor_reduce(m0[0:2, 0, :], b0, AX_X, ALU.add))
            link(dve.tensor_scalar(m0[0:2, 1, :], m0[0:2, 0, :], 1.0 / HD, None, ALU.mult))
            link(dve.tensor_tensor(b0, b0, m0[0:2, 1, :].unsqueeze(2).broadcast_to([2, NP, HD]), ALU.subtract))
            for b in range(1, B):
                dve.tensor_copy(Wst[:, b, :, :], Wst[:, 0, :, :]).then_inc(state_v, 1)
                dve.tensor_copy(Bst[:, b, :], Bst[:, 0, :]).then_inc(state_v, 1)
            link(dve.tensor_scalar(rate[:, :], alpha[:, :], C("token_rate"), 0.0, ALU.add, ALU.max))
            link(dve.tensor_scalar(rate[:, :], rate[:, :], 1.0 / HD, None, ALU.mult))
            dve.wait_ge(lr_p, 1)
            dve.tensor_tensor(eta[:, :, :, :].rearrange("p i b a -> p (i b) a"), bank[4][:, 0:NC * B * NP].rearrange("p (i a) -> p i a", a=NP),
                              tb[:, :].unsqueeze(1).broadcast_to([P, NC * B, NP]), ALU.add).then_inc(lr_v, 1)
            dve.wait_ge(lr_a, 1)
            dve.tensor_scalar(eta[:, :, :, :], eta[:, :, :, :], rate[:, :], None, ALU.mult).then_inc(eta_v, 1)
            dve.wait_ge(eta_v, 1)
            dve.wait_ge(ld_m, 16 * N_M)
            link(dve.memset(wgP[:, :, :], 0.0))
            for b in range(B):
                last = dve.tensor_copy(wgP[:, b, b * E0:(b + 1) * E0], wg0[:, :])
            last.then_inc(wg_v, 1)
            for j in range(4):
                r = slice(32 * j, 32 * j + 32)
                dve.tensor_copy(b3s[r, :], eb[r, 2, :].rearrange("p (g j) -> p j g", j=4)[:, j, :])
            link(dve.memset(wrk[:, 1, :], 1.0))
            dve.wait_ge(lg_p, 1)
            dve.tensor_scalar(lgt[:, :], bank[0][0:BE, :], bg0[:, :], None, ALU.add).then_inc(lg_v, 1)
            dve.wait_ge(lg_v, 1)
            for k in range(TOP0 // 8):
                left = lgt[:, :] if k == 0 else wrk[:, 0, :]
                link(dve.max(m8[:, k, :], left))
                if k == 0:
                    dve.tensor_scalar(es[:, 0:1], m8[:, 0, 0:1], -1.0, None, ALU.mult).then_inc(lg_v, 1)
                link(dve.match_replace(wrk[:, 0, :], m8[:, k, :], left, -3.0e38))
            dve.wait_ge(ex_a, 1)
            link(dve.tensor_tensor(wrk[:, 0, :], lgt[:, :], wrk[:, 0, :], ALU.not_equal))
            link(dve.tensor_tensor_scan(lgt[:, :], wrk[:, 1, :], wrk[:, 0, :], 0.0, ALU.mult, ALU.add))
            dve.tensor_tensor(rkp[:, 0, :], lgt[:, :], wrk[:, 0, :], ALU.mult).then_inc(rk_v, 1)
            link(dve.reciprocal(es[:, 2:3], es[:, 1:2]))
            dve.tensor_scalar(rkp[:, 1, :], rkp[:, 1, :], es[:, 2:3], None, ALU.mult).then_inc(rk_v, 1)
            g3 = lambda t: t.rearrange("p (a c) -> p a c", a=NP)
            per = lambda t: t.unsqueeze(2).broadcast_to([P, NP, HD])

            def chunk(i):
                def X(b):
                    u = 4 * i + b + 1
                    dve.wait_ge(U_["sqz_a"], u + BASE)
                    dve.tensor_reduce(sm[:, b, 0, :], g3(sqz[:, b % 2, :]), AX_X, ALU.add).then_inc(U_["ss_v"], 1)
                    dve.wait_ge(U_["sd_a"], u + BASE)
                    dve.reciprocal(sm[:, b, 2, :], sm[:, b, 1, :]).then_inc(U_["s1_v"], 1)
                    dve.wait_ge(U_["s1_v"], u + BASE)
                    dve.tensor_tensor(g3(xh[:, b, :]), g3(bank[b % 2][:, :]), per(sm[:, b, 2, :]), ALU.mult).then_inc(U_["xh_v"], 1)

                def G(b):
                    u = 4 * i + b + 1
                    dve.wait_ge(U_["t_g"], u + BASE)
                    dve.wait_ge(U_["pj_a"], 16 * i + 4 + 2 * b + 2 + BASE)
                    dve.tensor_tensor(gx[:, b, :], t1[:, b, :], U[:, b, :], ALU.add).then_inc(U_["gx_v"], 1)
                    dve.tensor_tensor(sm[:, b, 3, :], eta[:, bass.ds(i, 1), b, :].rearrange("p o a -> p (o a)"), sm[:, b, 2, :], ALU.mult).then_inc(U_["a_v"], 1)
                    dve.wait_ge(U_["gx_v"], u + BASE)
                    dve.tensor_reduce(sm[:, b, 4, :], g3(gx[:, b, :]), AX_X, ALU.add).then_inc(U_["c_v"], 1)
                    dve.wait_ge(U_["c_v"], 3 * (4 * i + b) + 1 + BASE)
                    dve.tensor_scalar(sm[:, b, 5, :], sm[:, b, 4, :], 1.0 / HD, None, ALU.mult).then_inc(U_["c_v"], 1)
                    dve.wait_ge(U_["c_v"], 3 * (4 * i + b) + 2 + BASE)
                    dve.tensor_tensor(g3(gw[:, b, :]), g3(gx[:, b, :]), per(sm[:, b, 5, :]), ALU.subtract).then_inc(U_["c_v"], 1)

                def R(b):
                    u = 4 * i + b + 1
                    dve.wait_ge(U_["q_g"], u + BASE)
                    dve.tensor_reduce(sm[:, b, 6, :], g3(t1[:, b, :]), AX_X, ALU.add).then_inc(U_["w1_v"], 1)
                    dve.wait_ge(U_["w1_v"], u + BASE)
                    dve.tensor_scalar(sm[:, b, 4, :], sm[:, b, 6, :], 1.0 / HD, None, ALU.mult).then_inc(U_["s2_v"], 1)

                def Wd(b):
                    u = 4 * i + b + 1
                    dve.wait_ge(U_["v_g"], u + BASE)
                    dve.wait_ge(U_["c_v"], 3 * (4 * i + b) + 3 + BASE)
                    dve.tensor_tensor(gw[:, b, :], gw[:, b, :], t1[:, b, :], ALU.subtract).then_inc(U_["w_v"], 1)

                def up(b):
                    dve.wait_ge(U_["dw_p"], 4 * i + b + 1 + BASE)
                    dve.tensor_tensor(Wst[:, b, :, :], Wst[:, b, :, :], g3(bank[4][:, :]), ALU.subtract).then_inc(U_["up_v"], 1)
                    dve.tensor_tensor(Bst[:, b, :], Bst[:, b, :], bank[5][0:2, :], ALU.subtract).then_inc(U_["up_v"], 1)

                def rqv(b):
                    dve.wait_ge(U_["sdq_a"], 4 * i + b + 1 + BASE)
                    dve.reciprocal(rq[:, b, 1, :], rq[:, b, 0, :]).then_inc(U_["rq_v"], 1)

                def Av(b):
                    dve.wait_ge(U_["bc_p"], 4 * i + b + 1 + BASE)
                    dve.wait_ge(U_["zq_a"], 4 * i + b + 1 + BASE)
                    dve.tensor_tensor(Am[:, b % 2, :], bank[6][:, :], zq[:, b % 2, :], ALU.mult).then_inc(U_["A_v"], 1)

                X(0), X(1), G(0), X(2), G(1), R(0), X(3), G(2), R(1), Wd(0), G(3), R(2), Wd(1), R(3), Wd(2), Wd(3)
                up(0), up(1), up(2), rqv(0), up(3), Av(0), rqv(1), Av(1), rqv(2), rqv(3), Av(2), Av(3)

            with dve.Fori(0, NC) as i:
                chunk(i)
            for b in range(B):
                if b >= 2:
                    dve.wait_ge(wp_g, b - 1)
                    dve.wait_ge(mj_p, 5 * (b - 2) + 1)
                for t in range(NT):
                    last = dve.tensor_tensor(OH[:, b % 2, t, :].rearrange("p (e k) -> p e k", e=E0),
                                             rpT[:, 0, t, b * E0:(b + 1) * E0].unsqueeze(2).broadcast_to([P, E0, TOP0]),
                                             C("slots").unsqueeze(1).broadcast_to([P, E0, TOP0]), ALU.is_equal)
                last.then_inc(oh_v, 1)
            for b in range(B):
                dve.wait_ge(sc_p, b + 1)
                dve.tensor_tensor(x1[:, b * NT:(b + 1) * NT, :], bank[4 + b][:, :].rearrange("p (t d) -> p t d", t=NT),
                                  x[:, b * NT:(b + 1) * NT, :], ALU.add).then_inc(x1_v, 1)


            tok = lambda t: t.unsqueeze(2).broadcast_to([P, B * NT, P])
            dve.wait_ge(x1_v, B)
            dve.wait_ge(ld_2, 16 * N_2)
            link(dve.tensor_reduce(st2[:, 0, :], x1[:, :, :], AX_X, ALU.add))
            link(dve.tensor_scalar(st2[:, 3, :], st2[:, 0, :], 1.0 / P, None, ALU.mult))
            dve.tensor_tensor(xn2[:, :, :], x1[:, :, :], tok(st2[:, 3, :]), ALU.subtract).then_inc(l2_v, 1)
            dve.wait_ge(ld_1, 16)
            dve.tensor_copy(W1h[:, :, :], W1r[:, :, :]).then_inc(w2v, 1)
            dve.wait_ge(l2_a, 1)
            dve.tensor_reduce(st2[:, 1, :], sq_2[:, :, :], AX_X, ALU.add).then_inc(l2_v, 1)
            dve.wait_ge(w2v, 1)
            dve.tensor_tensor(W1l[:, :, :], W1r[:, :, :], W1h[:, :, :], ALU.subtract).then_inc(w2v, 1)
            dve.wait_ge(l2_a, 2)
            link(dve.reciprocal(st2[:, 3, :], st2[:, 2, :]))
            dve.wait_ge(l2_v, 2)
            dve.tensor_tensor(xn2[:, :, :], xn2[:, :, :], tok(st2[:, 3, :]), ALU.mult).then_inc(l2_v, 1)
            dve.memset(Mt[:, :, :], 0.0)
            dve.memset(Vx[:, :, :, :], 0.0).then_inc(w2v, 1)
            link(dve.memset(wr[:, :, :, :], 0.0))
            dve.wait_ge(w2a, 2)
            for k in range(2):
                last = dve.tensor_copy(wr[:, k, :, :].rearrange("p q (j c) -> p (q j) c", c=32)[:, :, 0:24].rearrange("p h (c d) -> p h c d", d=AD),
                                       wT4[:, k, :].rearrange("p (h d) -> p h d", d=AD).unsqueeze(2).broadcast_to([P, AH, 3, AD]))
            link(last)
            link(dve.tensor_copy(wrh[:, :, :, :], wr[:, :, :, :]))
            dve.tensor_tensor(wrl[:, :, :, :], wr[:, :, :, :], wrh[:, :, :, :], ALU.subtract).then_inc(w2v, 1)
            dve.wait_ge(w2v, 3)
            dve.memset(Vx[:, :, :, AD:AD + 1], 1.0).then_inc(w2v, 1)
            dve.wait_ge(w2v, 5)
            for name, v in (("pr_v", 2), ("s1_v", 2)):
                dve.sem_inc(L_[name], v)

            def batch(i):
                n1, pr, s1 = [0], [0], [0]

                def link(ins):
                    n1[0] += 1
                    ins.then_inc(L_["v1"], 1)
                    dve.wait_ge(L_["v1"], V1 * i + n1[0] + BASE)

                def split(H_, L_2, k):
                    dve.wait_ge(L_["cur_a"], R1 * i + k + 1 + BASE)
                    link(dve.tensor_copy(H_[:, :], curT[:, :]))
                    dve.tensor_tensor(L_2[:, :], curT[:, :], H_[:, :], ALU.subtract).then_inc(L_["cs_v"], 1)

                def part():
                    n = pr[0]
                    pr[0] += 1
                    is_k = n in (0, 2, 5, 8)
                    dst = kx[:, (0, 0, 1, 1, 1, 0, 0, 0, 1, 1, 1, 1)[n], :] if is_k else (qm if n in (4, 7, 10, 11) else qx)[:, :]
                    dve.wait_ge(L_["pr_a"], 12 * i + n + 2 + BASE)
                    dve.scalar_tensor_tensor(out=dst, in0=hi[:, n % 2, :], scalar=C("k_minus" if is_k else "q_minus"),
                                             in1=bank[5 + n % 2][:, :], op0=ALU.mult, op1=ALU.add).then_inc(L_["pr_v"], 1)

                def smax():
                    n = s1[0]
                    s1[0] += 1
                    t, h = n % 16 // QH, n % QH
                    dve.wait_ge(L_["s1_p"], 64 * i + n + 1 + BASE)
                    dve.tensor_reduce(Mt[:, t, 32 * h + 24:32 * h + 25], bank[3 + n % 2][:, :], AX_X, ALU.max, negate=True).then_inc(L_["s1_v"], 1)

                def maxima(j):
                    dve.wait_ge(L_["s1_v"], 64 * i + 16 * (j + 1) + 2 + BASE)
                    m = Mt[:, :, :].rearrange("p t (h c) -> p t h c", c=32)
                    dve.tensor_copy(m[:, :, :, 25:26], m[:, :, :, 24:25]).then_inc(L_["mt_v"], 1)

                def gate(r):
                    n = R1 * i + r + 1
                    dve.wait_ge(L_["lg_p2"], n + BASE)
                    b16 = bank[7][:, 0:NT * E1].rearrange("p (t e) -> p t e", e=E1)
                    dve.tensor_tensor(lg[:, :, :], b16, bgB[:, r, :].unsqueeze(1).broadcast_to([P, NT, E1]), ALU.add).then_inc(L_["lg_v2"], 1)
                    dve.wait_ge(L_["lg_v2"], n + BASE)
                    other = lg[:, :, :].unsqueeze(2).broadcast_to([P, NT, E1, E1])
                    own = lg[:, :, :].unsqueeze(3).broadcast_to([P, NT, E1, E1])
                    sq = lambda k: lgx[:, k, :, :].rearrange("p t (e f) -> p t e f", e=E1)
                    g2 = lambda k: gt[:, k, :]
                    g3_ = lambda k: gt[:, k, :].rearrange("p (t e) -> p t e", e=E1)
                    one = lambda k: gt[:, k, 0:NT]
                    per = lambda k: gt[:, k, 0:NT].unsqueeze(2).broadcast_to([P, NT, E1])
                    dve.tensor_tensor(sq(0), other, own, ALU.is_gt)
                    link(dve.tensor_tensor(sq(1), other, own, ALU.is_equal))
                    link(dve.tensor_reduce(one(2), lg[:, :, :], AX_X, ALU.max))
                    dve.tensor_tensor(g3_(0), lg[:, :, :], per(2), ALU.subtract).then_inc(L_["z_v"], 1)
                    link(dve.tensor_tensor(lgx[:, 2, :, :], lgx[:, 1, :, :], C("lower").unsqueeze(1).broadcast_to([P, NT, E1 * E1]), ALU.mult))
                    link(dve.tensor_tensor(lgx[:, 1, :, :], lgx[:, 0, :, :], lgx[:, 2, :, :], ALU.add))
                    link(dve.tensor_reduce(g3_(3), sq(1), AX_X, ALU.add))
                    link(dve.tensor_scalar(g2(4), g2(3), 2.0, None, ALU.is_lt))
                    dve.wait_ge(L_["e_a"], n + BASE)
                    link(dve.tensor_tensor(g2(5), g2(1), g2(4), ALU.mult))
                    link(dve.tensor_reduce(one(6), g3_(5), AX_X, ALU.add))
                    link(dve.reciprocal(one(7), one(6)))
                    dve.tensor_tensor(cw[:, :, :], g3_(5), per(7), ALU.mult).then_inc(L_["cw_v"], 1)

                def bias(r):
                    dve.wait_ge(L_["cb_p"], R1 * i + r + 1 + BASE)
                    dve.wait_ge(L_["cc_v"], i + 1 + BASE)
                    if r:
                        dve.wait_ge(L_["y_v"], 16 * i + 4 * r + BASE)
                    dve.tensor_tensor(cur[:, :, :], bank[7][:, :].rearrange("p (t d) -> p t d", t=NT), cur[:, :, :], ALU.add).then_inc(L_["cb_v"], 1)

                def expert(r, e):
                    dve.wait_ge(L_["w_p"], 64 * i + 16 * r + 4 * e + 4 + BASE)
                    dve.wait_ge(L_["cb_v"], R1 * i + r + 1 + BASE)
                    if e:
                        dve.wait_ge(L_["y_v"], 16 * i + 4 * r + e + BASE)
                    for t in range(NT):
                        last = dve.scalar_tensor_tensor(out=cur[:, t, :], in0=bank[2][:, t * P:(t + 1) * P], scalar=cw[:, t, e:e + 1],
                                                        in1=cur[:, t, :], op0=ALU.mult, op1=ALU.add)
                    last.then_inc(L_["y_v"], 1)

                dve.tensor_copy(cur[:, :, :], xn2[:, bass.ds(i * NT, NT), :]).then_inc(L_["cc_v"], 1)
                split(xH, xL, 0)
                part()
                part()
                dve.wait_ge(L_["v_p"], i + 1 + BASE)
                dve.tensor_copy(Vx[:, :, :, 0:AD], bank[7][:, :].rearrange("p (t h d) -> p t h d", t=NT, d=AD)).then_inc(L_["v_v"], 1)
                gate(0)
                bias(0)
                for n in range(16):
                    smax()
                    if n % 4 == 0 and n:
                        expert(0, n // 4 - 1)
                expert(0, E1 - 1)
                maxima(0)
                for j in range(NQ):
                    for _ in range(3 if j < NQ - 1 else 1):
                        part()
                    if j < NQ - 1:
                        split(cH, cL, j + 1)
                    if j < NQ - 1:
                        for n in range(16):
                            smax()
                            if n == 6:
                                gate(j + 1)
                        maxima(j + 1)
                    n = NQ * i + j + 1
                    dve.wait_ge(L_["o_p"], n + BASE)
                    o4 = bank[7][:, :].rearrange("p (t h c) -> p t h c", t=NT, c=32)
                    link(dve.tensor_scalar(den[:, 0, :, :], o4[:, :, :, AD:AD + 1].rearrange("p t h o -> p t (h o)"), 1e-8, None, ALU.add))
                    link(dve.reciprocal(den[:, 1, :, :], den[:, 0, :, :]))
                    dve.tensor_tensor(an[:, :, j * 32:(j + 1) * 32].rearrange("p t (h d) -> p t h d", d=AD), o4[:, :, :, 0:AD],
                                      den[:, 1, :, :].unsqueeze(3).broadcast_to([P, NT, QH, AD]), ALU.mult).then_inc(L_["o_v"], 1)
                    if j < NQ - 1:
                        bias(j + 1)
                        for e in range(E1):
                            expert(j + 1, e)
                dve.wait_ge(L_["ao_p"], i + 1 + BASE)
                dve.wait_ge(L_["y_v"], 16 * i + 16 + BASE)
                dve.wait_ge(L_["out_d"], 16 * i + BASE)
                link(dve.tensor_tensor(fin[:, :, :], bank[7][:, :].rearrange("p (t d) -> p t d", t=NT), cur[:, :, :], ALU.add))
                link(dve.tensor_tensor(fin[:, :, :], fin[:, :, :], boB[:, :].unsqueeze(1).broadcast_to([P, NT, P]), ALU.add))
                dve.tensor_tensor(fin[:, :, :], fin[:, :, :], x1[:, bass.ds(i * NT, NT), :], ALU.add).then_inc(L_["fin_v"], 1)
                assert n1[0] == V1, n1[0]

            V1 = 4 + 4 * 9 + 2 * 4 + 2
            with dve.Fori(0, B) as i:
                batch(i)

        @block.gpsimd
        def _(pool):
            def xc(i):
                pool.tensor_copy(xnc[:, :, :], xnT[:, :].rearrange("p (b s) -> p b s", b=B)[:, :, bass.ds(i * K, K)]).then_inc(U_["xnc_g"], 1)

            pool.wait_ge(tr_c, 4)
            pool.wait_ge(prep_v, 3)
            g3 = lambda t: t.rearrange("p (a c) -> p a c", a=NP)
            per = lambda t: t.unsqueeze(2).broadcast_to([P, NP, HD])

            def chunk(i):
                pool.wait_ge(U_["pj_p"], 16 * i + 4 + BASE)
                xc(i)

                def t(b):
                    pool.wait_ge(U_["xh_v"], 4 * i + b + 1 + BASE)
                    pool.tensor_tensor(t1[:, b, :], xh[:, b, :], gg[:, :], ALU.mult).then_inc(U_["t_g"], 1)

                def q(b):
                    pool.wait_ge(U_["gx_v"], 4 * i + b + 1 + BASE)
                    pool.tensor_tensor(t1[:, b, :], gx[:, b, :], xh[:, b, :], ALU.mult).then_inc(U_["q_g"], 1)

                def v(b):
                    pool.wait_ge(U_["s2_v"], 4 * i + b + 1 + BASE)
                    pool.tensor_tensor(g3(t1[:, b, :]), g3(xh[:, b, :]), per(sm[:, b, 4, :]), ALU.mult).then_inc(U_["v_g"], 1)

                def wa(b):
                    pool.wait_ge(U_["w_v"], 4 * i + b + 1 + BASE)
                    pool.tensor_tensor(g3(gw[:, b, :]), g3(gw[:, b, :]), per(sm[:, b, 3, :]), ALU.mult).then_inc(U_["gw_g"], 1)

                t(0), t(1), q(0), t(2), q(1), v(0), t(3), q(2), v(1), wa(0), q(3), v(2), wa(1), v(3), wa(2), wa(3)

            with pool.Fori(0, NC) as i:
                chunk(i)
            for b in range(B):
                pool.wait_ge(oh_v, b + 1)
                if b:
                    pool.wait_ge(mj_p, 5 * b)
                for t in range(NT):
                    last = pool.tensor_tensor(WP[:, t, :].rearrange("p (e k) -> p e k", e=E0), OH[:, b % 2, t, :].rearrange("p (e k) -> p e k", e=E0),
                                              rpT[:, 1, t, b * E0:(b + 1) * E0].unsqueeze(2).broadcast_to([P, E0, TOP0]), ALU.mult)
                last.then_inc(wp_g, 1)

        @block.tensor
        def _(pe):
            pe.wait_ge(ld_c, 16)
            for b in range(B):
                pe.wait_ge(ln_xn, 3 + b)
                for t in range(NT):
                    last = pe.transpose(bank[b][:, t * P:(t + 1) * P], xn[:, b * NT + t, :], ident)
                last.then_inc(tr_n, 1)
            pe.wait_ge(tr_c, 4)
            pe.wait_ge(prep_v, 1)
            for i in range(NC):
                for b in range(B):
                    for hh in range(2):
                        last = pe.matmul(bank[4][hh * 64:hh * 64 + 64, (i * B + b) * NP:(i * B + b + 1) * NP],
                                         xnT[:, b * S + i * K:b * S + (i + 1) * K],
                                         Th[:, :].rearrange("p (a h) -> p h a", h=2)[:, hh, :], start=True, stop=True, skip_group_check=True)
            last.then_inc(lr_p, 1)
            pe.wait_ge(ld_w, 16 * N_W)
            pe.wait_ge(ld_s, 16 * N_S)
            for a in range(NP):
                last = pe.transpose(bank[5 + a // 4][:, a % 4 * P:(a % 4 + 1) * P], wq[:, a * P:(a + 1) * P], ident)
            last.then_inc(prep_p, 1)
            pe.wait_ge(prep_a, 2)
            for a in range(NP):
                pe.matmul(bank[7][:, 0:P], wqT[:, a, :], wo[:, a, :], start=(a == 0), stop=(a == NP - 1))
            for a in range(NP):
                last = pe.matmul(bank[7][:, P:P + 1], wo[:, a, :], bet[:, a:a + 1], start=(a == 0), stop=(a == NP - 1))
            last.then_inc(prep_p, 1)

            pe.wait_ge(wg_v, 1)
            for b in range(B):
                last = pe.matmul(bank[0][0:BE, :], wgP[:, b, :], xnT[:, b * S:(b + 1) * S], start=(b == 0), stop=(b == B - 1))
            last.then_inc(lg_p, 1)
            pe.wait_ge(rk_v, 2)
            for k in range(2):
                for t in range(NT):
                    last = pe.transpose(bank[1][:, (k * NT + t) * BE:(k * NT + t + 1) * BE], rkp[:, k, t * P:(t + 1) * P], ident[0:BE, 0:BE])
            last.then_inc(rT_p, 1)

            def fill(k, n, parts, bias=None):
                if n is not None:
                    pe.wait_ge(U_["pj_a"], n + BASE)
                to = bank[2 + k % 2]
                if bias is not None:
                    pe.matmul(to[:, :], half, bias, start=True, stop=False, skip_group_check=True)
                for dst, lhs, rhs in parts:
                    last = pe.matmul(dst(to), lhs, rhs, start=(bias is None), stop=True, skip_group_check=True)
                last.then_inc(U_["pj_p"], 1)

            def heads(w, b, at):
                return [(lambda to, a=a: to[:, a * K:(a + 1) * K], w[:, a * P:(a + 1) * P], xnT[:, bass.ds(at, K)]) for a in range(NP)]

            def tokens(w, b):
                return [(lambda to, hh=hh: to[hh * 64:hh * 64 + 64, :], xnc[:, b, :], w3(w[:, :])[:, :, hh, :]) for hh in range(2)]

            for b in range(B):
                fill(b, None if b < 2 else b - 1, heads(wk, b, b * S))
            pe.wait_ge(state_v, 2 * (B - 1))
            pe.wait_ge(prep_v, 5)
            pe.wait_ge(prep_a, 4)

            def chunk(i, last_chunk):
                def blocks(to, lhs, rhs, start):
                    for a in range(NP):
                        for hh in range(2):
                            r = slice(hh * 64, hh * 64 + 64)
                            last = pe.matmul(to[r, a * 64:a * 64 + 64], lhs(r, a), rhs(r, a), start=start, stop=True, skip_group_check=True)
                    return last

                def Z(b):
                    pe.wait_ge(U_["pj_a"], 16 * i + b + 1 + BASE)
                    if b == 0:
                        pe.wait_ge(U_["up_v"], 8 * i + BASE)
                    if b < 2:
                        pe.wait_ge(U_["zq_a"], 4 * i + BASE)
                    else:
                        pe.wait_ge(U_["xh_v"], 4 * i + b - 1 + BASE)
                    to = bank[b % 2]
                    pe.matmul(to[:, :], half, Bst[:, b, :], start=True, stop=False, skip_group_check=True)
                    blocks(to, lambda r, a: kT[r, b, a, :], lambda r, a: Wst[r, b, a, :], False).then_inc(U_["z_p"], 1)

                def xku(b):
                    if b == 0:
                        pe.wait_ge(U_["xnc_g"], i + 1 + BASE)
                    fill(0, 16 * i + 3 + 2 * b, tokens(wk, b))
                    fill(1, 16 * i + 4 + 2 * b, tokens(wu, b), gbeta[:, :])

                def dW(b):
                    pe.wait_ge(U_["gw_g"], 4 * i + b + 1 + BASE)
                    pe.wait_ge(U_["up_v"], 8 * i + 2 * b + BASE)
                    pe.matmul(bank[5][0:2, :], half_t, gw[:, b, :], start=True, stop=True)
                    blocks(bank[4], lambda r, a: XK[r, b, a, :], lambda r, a: gw[r, b, a * 64:a * 64 + 64], True).then_inc(U_["dw_p"], 1)

                def Zq(b):
                    pe.wait_ge(U_["up_v"], 8 * i + 2 * b + 2 + BASE)
                    pe.wait_ge(U_["pj_a"], 16 * i + 13 + b + BASE)
                    if b < 2:
                        pe.wait_ge(U_["xh_v"], 4 * i + b + 3 + BASE)
                    else:
                        pe.wait_ge(U_["zq_a"], 4 * i + b - 1 + BASE)
                    for a in range(NP):
                        for hh in range(2):
                            r = slice(hh * 64, hh * 64 + 64)
                            to = bank[b % 2][r, a * 64:a * 64 + 64]
                            pe.matmul(to, Bst[:, b, a * 64:a * 64 + 64], half[:, r], start=True, stop=False, skip_group_check=True)
                            last = pe.matmul(to, Wst[r, b, a, :], qT[r, b, a, :], start=False, stop=True, skip_group_check=True)
                    last.then_inc(U_["zq_p"], 1)

                def var(b):
                    pe.wait_ge(U_["zs_a"], 4 * i + b + 1 + BASE)
                    if b in (1, 2):
                        pe.wait_ge(U_["sdq_a"], 4 * i + b + BASE)
                    else:
                        pe.wait_ge(U_["at_a"], 4 * i + b // 3 + BASE)
                    for a in range(NP):
                        last = pe.matmul(bank[7][0:H, b * K:(b + 1) * K], mean[:, a, :], sq2[:, b % 2, a * K:(a + 1) * K],
                                         start=(a == 0), stop=(a == NP - 1), skip_group_check=True)
                    last.then_inc(U_["var_p"], 1)

                def bcast(b):
                    pe.wait_ge(U_["rq_v"], 4 * i + b + 1 + BASE)
                    pe.wait_ge(U_["A_v"], 4 * i + b + BASE)
                    for a in range(NP):
                        last = pe.matmul(bank[6][:, a * K:(a + 1) * K], spread[:, a, :], rq[:, b, 1, :], start=True, stop=True, skip_group_check=True)
                    last.then_inc(U_["bc_p"], 1)

                def att(b):
                    pe.wait_ge(U_["A_v"], 4 * i + b + 1 + BASE)
                    if b < 2:
                        pe.wait_ge(U_["sdq_a"], 4 * i + 3 + b + BASE)
                    else:
                        pe.wait_ge(U_["at_a"], 4 * i + b + BASE)
                    to = bank[7][:, 256 + b * K:256 + (b + 1) * K]
                    for a in range(NP):
                        pe.matmul(to, wog[:, a, :], Am[:, b % 2, a * K:(a + 1) * K], start=(a == 0), stop=False, skip_group_check=True)
                    pe.matmul(to, Wqo[:, :], xnT[:, bass.ds(b * S + i * K, K)], start=False, stop=True, skip_group_check=True).then_inc(U_["at_p"], 1)

                Z(0), Z(1), xku(0), xku(1), Z(2), Z(3), xku(2), xku(3)
                for b in range(B):
                    fill(b, 16 * i + 11 + b, heads(wq, b, b * S + i * K))
                if not last_chunk:
                    for b in range(B):
                        fill(b, 16 * i + 15 + b, heads(wk, b, b * S + (i + 1) * K))
                dW(0), dW(1), Zq(0), dW(2), Zq(1), var(0), dW(3), Zq(2), var(1), bcast(0), Zq(3), var(2), bcast(1), att(0)
                var(3), bcast(2), att(1), bcast(3), att(2), att(3)

            with pe.Fori(0, NC - 1) as i:
                chunk(i, False)
            chunk(NC - 1, True)

            jobs = [0]

            def job(parts):
                n = jobs[0]
                jobs[0] += 1
                if n >= 4:
                    pe.wait_ge(mj_a, n - 3)
                for dst, lhs, rhs, start, stop in parts:
                    last = pe.matmul(bank[n % 4][dst], lhs, rhs, start=start, stop=stop, skip_group_check=True)
                last.then_inc(mj_p, 1)

            pe.wait_ge(U_["at_a"], 4 * NC + BASE)
            for b in range(B):
                pe.wait_ge(oh_v, b + 1)
                job([((slice(0, P), slice(0, S)), xn[:, b * NT + t, :], OH[:, b % 2, t, :], t == 0, t == NT - 1) for t in range(NT)])
                pe.wait_ge(wp_g, b + 1)
                for g in range(E0 // 4):
                    n = jobs[0]
                    jobs[0] += 1
                    if n >= 4:
                        pe.wait_ge(mj_a, n - 3)
                    for t in range(NT):
                        last = pe.transpose(bank[n % 4][:, t * P:(t + 1) * P], WP[:, t, g * P:(g + 1) * P], ident)
                    last.then_inc(mj_p, 1)
            n0 = jobs[0]
            pe.wait_ge(ld_m, 16 * N_M)
            pe.wait_ge(mj_a, n0)
            for g in range(E0 // 4):
                job([((slice(0, P), slice(j * P, (j + 1) * P)), ew[0][:, 4 * g + j, :], tokT[:, :, 4 * g + j, :], True, True) for j in range(4)])
            for g in range(E0 // 4):
                pe.wait_ge(mj_a, n0 + g + 1)
                job([((slice(0, P), slice(j * P, (j + 1) * P)), ew[1][:, 4 * g + j, :], h1[:, 4 * g + j, :], True, True) for j in range(4)])
            for g in range(E0 // 4):
                pe.wait_ge(mj_a, n0 + 4 + g + 1)
                job([((slice(32 * j, 32 * j + 32), slice(b * P, (b + 1) * P)), h2[:, 4 * g + j, b * 32:(b + 1) * 32], ew[2][:, 4 * g + j, :], True, True)
                     for b in range(B) for j in range(4)])
            pe.wait_ge(mj_a, n0 + 12)
            for b in range(B):
                for t in range(NT):
                    to = bank[4 + b][:, t * P:(t + 1) * P]
                    pe.matmul(to, attnT[:, b * S + t * P:b * S + (t + 1) * P], ident, start=True, stop=False, skip_group_check=True)
                    for g in range(E0 // 4):
                        last = pe.matmul(to, WPT[:, b, g, t * P:(t + 1) * P], o3[:, g, b, :], start=False, stop=(g == E0 // 4 - 1), skip_group_check=True)
                last.then_inc(sc_p, 1)

            pe.wait_ge(ld_2, 16 * N_2)
            for n in range(4):
                pe.transpose(bank[0][:, n * P:(n + 1) * P], w4[:, n, :], ident)
            pe.transpose(bank[1][:, 0:E1 * NF], b1r[:, :], ident[0:E1 * NF, 0:E1 * NF]).then_inc(w2p, 1)
            pe.wait_ge(l2_v, 3)
            pe.wait_ge(x1_v, B)
            for b in range(B):
                for t in range(NT):
                    last = pe.transpose(bank[2 + b][:, t * P:(t + 1) * P], xn2[:, b * NT + t, :], ident)
                last.then_inc(t2_p, 1)
            pe.wait_ge(t2_a, B)
            pe.wait_ge(w2v, 5)
            pe.wait_ge(w2a, 2)

            def mm3(to, lh, ll, rh, rl, start=True, stop=True):
                pe.matmul(to, lh, rh, start=start, stop=False, skip_group_check=True)
                pe.matmul(to, ll, rh, start=False, stop=False, skip_group_check=True)
                return pe.matmul(to, lh, rl, start=False, stop=stop, skip_group_check=True)

            def batch(i):
                pr, s1, hj, pv, wj, yj = [0], [0], [0], [0], [0], [0]

                def project(kind, j, maxima=False):
                    n = pr[0]
                    pr[0] += 1
                    pe.wait_ge(L_["pr_v"], 12 * i + n + 1 + BASE)
                    to = bank[5 + n % 2]
                    last = mm3(to[:, :], wrh[:, kind, j, :], wrl[:, kind, j, :], xH[:, :], xL[:, :], stop=not maxima)
                    if maxima:
                        pe.wait_ge(L_["mt_v"], NQ * i + j + 1 + BASE)
                        for t in range(NT):
                            last = pe.matmul(to[:, t * P:(t + 1) * P], Mt[:, t, :], ident, start=False, stop=True, skip_group_check=True)
                    last.then_inc(L_["pr_p"], 1)

                def scores():
                    n = s1[0]
                    s1[0] += 1
                    j, t, h = n // 16, n % 16 // QH, n % QH
                    r = slice(32 * h, 32 * h + 32)
                    if n % 16 == 0:
                        pe.wait_ge(L_["pr_v"], 12 * i + (2, 4, 7, 10)[j] + 2 + BASE)
                    pe.wait_ge(L_["s1_v"], 64 * i + n + 1 + BASE)
                    pe.matmul(bank[3 + n % 2][:, :], qx[r, t * P:(t + 1) * P], kx[r, j % 2, :], start=True, stop=True).then_inc(L_["s1_p"], 1)

                def turned_scores(j, n):
                    m = hj[0]
                    hj[0] += 1
                    t, h = n // QH, n % QH
                    r = slice(32 * h, 32 * h + 32)
                    if n == 0:
                        pe.wait_ge(L_["pr_v"], 12 * i + (5, 8, 11, 12)[j] + 2 + BASE)
                    pe.wait_ge(L_["h_a"], 128 * i + m + 1 + BASE)
                    pe.matmul(bank[m % 2][:, :], kx[r, j % 2, t * P:(t + 1) * P], qm[r, :], start=True, stop=True).then_inc(L_["h_p"], 1)

                def values(j, n):
                    t, h = n // QH, n % QH
                    if n == 0:
                        pe.wait_ge(L_["v_v"], i + 1 + BASE)
                        pe.wait_ge(L_["y_v"], 16 * i + 4 * (j + 1) + BASE)
                    pe.wait_ge(L_["h_a"], 128 * i + 32 * j + 16 + n + 3 + BASE)
                    pe.matmul(bank[2][32 * h:32 * h + 32, :], Vx[:, t, QH * j + h, :], ex[:, n % 4, :], start=(t == 0), stop=(t == NT - 1),
                              skip_group_check=True).then_inc(L_["pv_p"], 1)

                def hidden(r, n):
                    m = hj[0]
                    hj[0] += 1
                    e, a = n // NF, n % NF
                    h_, l_ = (xH, xL) if r == 0 else (cH, cL)
                    if n == 0:
                        pe.wait_ge(L_["cs_v"], R1 * i + r + 1 + BASE)
                    pe.wait_ge(L_["h_a"], 128 * i + m + 1 + BASE)
                    c = slice(a * P, (a + 1) * P)
                    mm3(bank[m % 2][:, :], W1h[:, e, c], W1l[:, e, c], h_[:, :], l_[:, :]).then_inc(L_["h_p"], 1)

                def outputs(r, n):
                    e, a = n // NF, n % NF
                    if n == 0 and r:
                        pe.wait_ge(L_["o_a"], NQ * i + r + BASE)
                    elif n == 0:
                        pe.wait_ge(L_["o_a"], NQ * i + BASE)
                    if a == 0:
                        pe.wait_ge(L_["y_v"], 16 * i + 4 * r + e + BASE)
                    pe.wait_ge(L_["h_a"], 128 * i + 32 * r + n + 3 + BASE)
                    for t in range(NT):
                        last = pe.matmul(bank[2][:, t * P:(t + 1) * P], hb[:, n % 4, t * P:(t + 1) * P], W2[:, e, a, :],
                                         start=(a == 0 and t == 0), stop=(a == NF - 1), skip_group_check=True)
                    last.then_inc(L_["w_p"], 1)

                def logits(r):
                    if r:
                        pe.wait_ge(L_["cur_a"], R1 * i + r + 1 + BASE)
                    else:
                        pe.wait_ge(L_["v_v"], i + 1 + BASE)
                    for t in range(NT):
                        last = pe.matmul(bank[7][:, t * E1:(t + 1) * E1], curT[:, t * P:(t + 1) * P], Wg1[:, r, :], start=True, stop=True, skip_group_check=True)
                    last.then_inc(L_["lg_p2"], 1)

                def turn_weights(r):
                    pe.wait_ge(L_["cw_v"], R1 * i + r + 1 + BASE)
                    for t in range(NT):
                        last = pe.transpose(bank[7][0:E1, t * P:(t + 1) * P], cw[:, t, :], ident)
                    last.then_inc(L_["ct_p"], 1)

                def biases(r):
                    pe.wait_ge(L_["ct_a"], R1 * i + r + 1 + BASE)
                    if r:
                        pe.wait_ge(L_["o_v"], NQ * i + r + BASE)
                    for t in range(NT):
                        last = pe.matmul(bank[7][:, t * P:(t + 1) * P], cwT[:, t * P:(t + 1) * P], b2r[:, :], start=True, stop=True, skip_group_check=True)
                    last.then_inc(L_["cb_p"], 1)

                pe.wait_ge(L_["cs_v"], R1 * i + 1 + BASE)
                project(1, 0)
                project(0, 0)
                pe.wait_ge(L_["fin_v"], i + BASE)
                for t in range(NT):
                    last = pe.matmul(bank[7][:, t * P:(t + 1) * P], curT[:, t * P:(t + 1) * P], wT4[:, 2, :], start=True, stop=True, skip_group_check=True)
                last.then_inc(L_["v_p"], 1)
                logits(0)
                turn_weights(0)
                biases(0)

                def mlp(r, with_scores):
                    for n in range(E1 * NF + 1):
                        if n < E1 * NF:
                            hidden(r, n)
                            if with_scores:
                                scores()
                        if n:
                            outputs(r, n - 1)

                mlp(0, True)
                for j in range(NQ):
                    if j < NQ - 1:
                        project(1, j + 1)
                        project(0, j + 1)
                    project(0, j, maxima=True)
                    if j < NQ - 1:
                        pe.wait_ge(L_["y_v"], 16 * i + 4 * (j + 1) + BASE)
                        pe.wait_ge(L_["cb_v"], R1 * i + j + 1 + BASE)
                        for t in range(NT):
                            last = pe.transpose(bank[7][:, t * P:(t + 1) * P], cur[:, t, :], ident)
                        last.then_inc(L_["cur_p"], 1)
                    for n in range(17):
                        if n < 16:
                            turned_scores(j, n)
                        if n < 16 and j < NQ - 1:
                            scores()
                        if n:
                            values(j, n - 1)
                        if n == 3 and j < NQ - 1:
                            logits(j + 1)
                        if n == 13 and j < NQ - 1:
                            turn_weights(j + 1)
                    pe.wait_ge(L_["o_a"], NQ * i + j + 1 + BASE)
                    if j < NQ - 1:
                        pe.wait_ge(L_["ct_a"], R1 * i + j + 2 + BASE)
                    for t in range(NT):
                        last = pe.transpose(bank[7][:, t * P:(t + 1) * P], ob[:, t * P:(t + 1) * P], ident)
                    last.then_inc(L_["o_p"], 1)
                    if j < NQ - 1:
                        biases(j + 1)
                        mlp(j + 1, False)
                pe.wait_ge(L_["o_v"], NQ * (i + 1) + BASE)
                for t in range(NT):
                    last = pe.transpose(bank[7][:, t * P:(t + 1) * P], an[:, t, :], ident)
                last.then_inc(L_["at2_p"], 1)
                pe.wait_ge(L_["at2_a"], i + 1 + BASE)
                for t in range(NT):
                    last = pe.matmul(bank[7][:, t * P:(t + 1) * P], aT[:, t * P:(t + 1) * P], wT4[:, 3, :], start=True, stop=True, skip_group_check=True)
                last.then_inc(L_["ao_p"], 1)

            with pe.Fori(0, B) as i:
                batch(i)


_INS = ["L0_attn_hidden_states", "L0_attn_wq", "L0_attn_wk", "L0_attn_wv", "L0_attn_wo", "L0_attn_W1", "L0_attn_b1", "L0_attn_theta",
        "L0_attn_theta_bias", "L0_attn_alpha", "L0_attn_gamma", "L0_attn_beta", "L0_ffn_Wg", "L0_ffn_bg", "L0_ffn_w1", "L0_ffn_b1",
        "L0_ffn_w2", "L0_ffn_b2", "L0_ffn_w3", "L0_ffn_b3", "L1_attn_Wq", "L1_attn_Wk", "L1_attn_Wv", "L1_attn_Wo", "L1_attn_bo",
        "L1_ffn_Wg", "L1_ffn_bg", "L1_ffn_W1", "L1_ffn_b1", "L1_ffn_W2", "L1_ffn_b2"]


def kernel(**inputs):
    import numpy as _np
    import concourse.bacc as _bacc
    from concourse import mybir as _mybir
    from concourse.bass_utils import run_bass_kernel_spmd as _run

    nc = _bacc.Bacc("TRN2", target_bir_lowering=False, num_devices=1)
    arrays, aps = {}, {}
    for name in _INS:
        a = _np.ascontiguousarray(inputs[name])
        arrays[f"in_{name}"] = a
        aps[name] = nc.dram_tensor(f"in_{name}", a.shape, _mybir.dt.from_np(a.dtype), kind="ExternalInput").ap()
    c = constants(_np)
    arrays["constants"] = c
    const_d = nc.dram_tensor("constants", c.shape, _mybir.dt.float32, kind="ExternalInput").ap()
    out = nc.dram_tensor("out_0", (B, S, P), _mybir.dt.float32, kind="ExternalOutput").ap()
    build(nc, aps, out, const_d)
    r = _run(nc, [arrays], core_ids=[0])
    return r.results[0]["out_0"]
```

```python
from contextlib import ExitStack

import concourse.bass as bass
from concourse import mybir

F32 = mybir.dt.float32
F32R = mybir.dt.float32r
ALU = mybir.AluOpType
ACT = mybir.ActivationFunctionType
AX_X = mybir.AxisListType.X

P = 128
B, S = 4, 512
NT = S // P
H, HD = 16, 64
NP = H // 2
K = 64
NC = S // K
D = H * HD
W = NP * HD
E0, TOP0 = 16, 32
AH, AD = 16, 8
QH = 4
NQ = AH // QH
E1, F1, R1 = 4, 512, 4
NF = F1 // P

CONST = {}


def constants(np):
    cols, at = [], 0

    def put(name, a):
        nonlocal at
        full = np.zeros((P, a.shape[1]), np.float32)
        full[:a.shape[0]] = a
        cols.append(full)
        CONST[name] = (at, a.shape[0], a.shape[1])
        at += a.shape[1]

    part = np.arange(P)
    put("ident", np.eye(P))
    half = (part[None, :] // K == np.arange(2)[:, None]).astype(np.float32)
    put("half", half)
    put("half_t", half.T)
    put("token_rate", (1.0 / (part % K + 1))[:, None])
    put("slots", np.tile(np.arange(1, TOP0 + 1)[None], (P, 1)))
    low = (np.arange(E1)[None, :] < np.arange(E1)[:, None]).astype(np.float32)
    put("lower", np.tile(low.reshape(1, -1), (P, 1)))
    row = part % 32
    put("q_minus", -(((row >= 8) & (row < 16)) | (row == 25)).astype(np.float32)[:, None])
    put("k_minus", (-((row >= 16) & (row < 24)).astype(np.float32)
                    + ((row == 24) | (row == 25)))[:, None])
    put("k_ones", ((row == 24) | (row == 25)).astype(np.float32)[:, None])
    put("even", ((part // 32) % 2 == 0).astype(np.float32)[:, None])
    put("odd", ((part // 32) % 2 == 1).astype(np.float32)[:, None])
    put("ln_eps", np.full((P, 1), 1e-5))
    put("ttt_eps", np.full((P, 1), 1e-6))
    return np.concatenate(cols, 1).astype(np.float32)


def build(nc, A, out, const_d, dbg=None):
    with ExitStack() as ctx:
        def sb(name, shape, dt=F32):
            return ctx.enter_context(nc.sbuf_tensor(name, shape, dt))

        def sem(name):
            return ctx.enter_context(nc.semaphore(name))

        bank = [ctx.enter_context(nc.psum_tensor(f"bank{n}", [P, 512], F32)) for n in range(8)]

        cst = sb("cst", [P, const_d.shape[1]])
        x = sb("x", [P, B * NT, P])
        x1 = x
        w4 = sb("w4", [P, 4, P])
        b1r = sb("b1r", [E1 * NF, P])
        b2r = sb("b2r", [E1, P])
        boB = sb("boB", [P, P])
        Wg1 = sb("Wg1", [P, R1, E1])
        bgB = sb("bgB", [P, R1, E1])

        first_layer = ExitStack()

        def sb(name, shape, dt=F32):
            return first_layer.enter_context(nc.sbuf_tensor(name, shape, dt))

        PIECE = B * W
        arena = sb("arena", [P, 10 * PIECE])

        def piece(k, n=PIECE, off=0):
            return arena[:, k * PIECE + off:k * PIECE + off + n]

        def C(name):
            at, rows, width = CONST[name]
            return cst[0:rows, at:at + width]

        ident, half, half_t = C("ident"), C("half"), C("half_t")

        xn = sb("xn", [P, B * NT, P])
        st = sb("st", [P, 4, B * NT])
        xnT = sb("xnT", [P, B * S])
        xsq = piece(0).rearrange("p (t d) -> p t d", d=P)
        wq = piece(1, D)
        wk = piece(1, D, D)
        wu = piece(5, D, D)
        W1s = piece(3, NP * HD).rearrange("p (a d) -> p a d", a=NP)
        wkh, wkl, wqh, wql, wuh, wul = (sb(n, [P, D], F32R) for n in ("wkh", "wkl", "wqh", "wql", "wuh", "wul"))
        wv = piece(7, D, D)
        wo = piece(8, D).rearrange("p (a c) -> p a c", a=NP)
        wog = sb("wog", [P, NP, P])
        wqT = piece(6, D).rearrange("p (a c) -> p a c", a=NP)
        gam = sb("gam", [P, NP])
        bet = sb("bet", [P, NP])
        gamB = piece(6, D, D)
        gg = sb("gg", [P, D])
        gb2 = piece(4).rearrange("p (k w) -> p k w", k=2)[0:64]
        gbr = sb("gbr", [64, D], F32R)
        ones = sb("ones", [64, P], F32R)
        th = piece(7, D)
        Th = sb("Th", [P, H])
        tb = sb("tb", [P, H])
        alpha = sb("alpha", [P, 1])
        rate = sb("rate", [P, 1])
        eta = sb("eta", [P, NC, 2, H])
        Wbd = sb("Wbd", [P, B, NP, P])
        Bst = sb("Bst", [2, 2, D])
        m0 = sb("m0", [P, 2, NP])
        mb = sb("mb", [2, 2, 2 * H])
        Wqo = sb("Wqo", [P, P])
        bo0 = sb("bo0", [P, 1])
        attnT = sb("attnT", [P, B * S])

        xch, xcl = (sb(n, [P, B * K], F32R) for n in ("xch", "xcl"))
        kT = piece(0).rearrange("p (a b c) -> p a b c", a=NP, b=B)
        qT = piece(1).rearrange("p (a b c) -> p a b c", a=NP, b=B)
        XK, U, xh, t1, gx, gw = (piece(n).rearrange("p (u w) -> p u w", u=4) for n in (2, 3, 5, 6, 7, 8))
        sqz = piece(4, PIECE // 2).rearrange("p (u w) -> p u w", u=2)
        sq2 = piece(4, PIECE // 2, PIECE // 2).rearrange("p (u w) -> p u w", u=2)
        sm = sb("sm", [P, 4, 7, 8])
        rq = sb("rq", [P, 4, 3, 8])
        Am = piece(9, PIECE // 2).rearrange("p (u w) -> p u w", u=2)
        AT = piece(9, PIECE // 2, PIECE // 2).rearrange("p (u w) -> p u w", u=2)

        BE = B * E0
        wg0 = sb("wg0", [P, E0])
        wgP = sb("wgP", [P, B, BE])
        bg0 = sb("bg0", [BE, 1])
        ew = [sb(f"ew{n}", [P, E0, P]) for n in range(2)] + [piece(9).rearrange("p (e o) -> p e o", e=E0)]
        eb = sb("eb", [P, 3, E0])
        b3s = sb("b3s", [P, E0 // 4])
        lgt = piece(9, S)[0:BE]
        wrk = piece(9, 2 * S, 2 * S).rearrange("p (k s) -> p k s", k=2)[0:BE]
        m8 = sb("m8", [BE, 4, 8])
        es = sb("es", [BE, 4])
        rkp = attnT[0:BE, 0:2 * S].rearrange("p (k s) -> p k s", k=2)
        rpT = sb("rpT", [P, 2, NT, BE])
        OH = piece(0, 2 * PIECE).rearrange("p (q t k) -> p q t k", q=2, t=NT)
        WP = piece(2).rearrange("p (t k) -> p t k", t=NT)
        WPT = piece(3, 4 * PIECE).rearrange("p (b g s) -> p b g s", b=B, g=E0 // 4)
        tokT = piece(7).rearrange("p (b e k) -> p b e k", b=B, e=E0)
        h1 = piece(8).rearrange("p (e s) -> p e s", e=E0)
        h2 = piece(0).rearrange("p (e s) -> p e s", e=E0)
        o3 = piece(1).rearrange("p (g b d) -> p g b d", g=E0 // 4, b=B)
        first_layer.close()

        def sb(name, shape, dt=F32):
            return ctx.enter_context(nc.sbuf_tensor(name, shape, dt))

        QW = QH * 32
        ex = sb("ex", [P, 8, S])
        hd = sb("hd", [P, 8, S])
        W2 = sb("W2", [P, E1, NF, P])
        W1r = ex[:, 0:4, :]
        sq_2 = ex[:, 4:8, :].rearrange("p n (t d) -> p (n t) d", d=P)
        W1h = sb("W1h", [P, E1, F1], F32R)
        W1l = sb("W1l", [P, E1, F1], F32R)
        wr = hd[:, 0:2, :].rearrange("p k (q c) -> p k q c", q=NQ)
        wrh = sb("wrh", [P, 2, NQ, QW], F32R)
        wrl = sb("wrl", [P, 2, NQ, QW], F32R)
        wT4 = sb("wT4", [P, 4, P])
        b1c = sb("b1c", [P, E1 * NF])
        xn2 = sb("xn2", [P, B * NT, P])
        st2 = sb("st2", [P, 4, B * NT])
        xn2T = sb("xn2T", [P, B * S])
        cur = sb("cur", [P, NT, P])
        curT = sb("curT", [P, S])
        xH = sb("xH", [P, S], F32R)
        xL = sb("xL", [P, S], F32R)
        cH = sb("cH", [P, S], F32R)
        cL = sb("cL", [P, S], F32R)
        hi = sb("hi", [P, 2, S], F32R)
        kx = sb("kx", [P, 2, S], F32R)
        qf = sb("qf", [P, S])
        qx = sb("qx", [P, 2, S], F32R)
        qm = sb("qm", [P, 2, S], F32R)
        Mt = sb("Mt", [P, NT, QW])
        Vx = sb("Vx", [P, NT, AH, 32])
        Vs = sb("Vs", [P, NT, P])
        ob = sb("ob", [P, S])
        den = sb("den", [P, 2, NT, QH])
        an = sb("an", [P, NT, P])
        aT = sb("aT", [P, S])
        lg = sb("lg", [P, NT, E1])
        lgx = sb("lgx", [P, 3, NT, E1 * E1])
        gt = sb("gt", [P, 8, NT * E1])
        cw = sb("cw", [P, NT, E1])
        cwT = sb("cwT", [E1, S])
        fin = sb("fin", [P, NT, P])
        ld_2, ld_1 = sem("ld_2"), sem("ld_1")
        l2_v, l2_a, l2_g = sem("l2_v"), sem("l2_a"), sem("l2_g")
        t2_p, t2_a, w2p, w2a, w2v = sem("t2_p"), sem("t2_a"), sem("w2p"), sem("w2a"), sem("w2v")
        N_L1 = ("cur_p", "cur_a", "cs_v", "xs_v", "cc_v", "pr_p", "pr_a", "pr_v", "qs_v", "v_p", "v_v", "vx_v", "s1_p", "s1_v", "mt_v",
                "tq_p", "tq_a", "h_p", "h_a", "w_p", "y_v",
                "pv_p", "o_a", "o_p", "o_v", "lg_p2", "lg_v2", "z_v", "e_a", "cw_v", "ct_p", "ct_a", "cb_p", "cb_v", "at2_p", "at2_a", "ao_p",
                "fin_v", "out_d", "v1")
        L_ = {n: sem("L" + n) for n in N_L1}
        ld_m = sem("ld_m")
        wg_v, lg_p, lg_v, ex_a, rk_v, rT_p, rT_a = (sem(n) for n in ("wg_v", "lg_p", "lg_v", "ex_a", "rk_v", "rT_p", "rT_a"))
        oh_v, wp_g, mj_p, mj_a, sc_p, x1_v = (sem(n) for n in ("oh_v", "wp_g", "mj_p", "mj_a", "sc_p", "x1_v"))
        ld_x, ld_c, ld_w, ld_s = sem("ld_x"), sem("ld_c"), sem("ld_w"), sem("ld_s")
        ln_sq, ln_sd, ln_xn = sem("ln_sq"), sem("ln_sd"), sem("ln_xn")
        tr_n, tr_c = sem("tr_n"), sem("tr_c")
        vs = sem("vs")
        gs = sem("gs")
        prep_v, prep_g, prep_a, prep_p = sem("prep_v"), sem("prep_g"), sem("prep_a"), sem("prep_p")
        lr_p, lr_v, lr_a, eta_v = sem("lr_p"), sem("lr_v"), sem("lr_a"), sem("eta_v")
        state_v = sem("state_v")
        N_UNIT = ("pj_p", "pj_a", "z_p", "sqz_a", "ss_v", "sd_a", "s1_v", "xh_v", "t_g", "gx_v", "a_v", "c_v", "q_g", "w1_v", "s2_v", "v_g",
                  "w_v", "gw_g", "dw_p", "up_v", "zq_p", "zs_a", "sq_v", "sdq_a", "rq_v", "A_v", "at_p", "at_a", "att_p", "att_a", "xc_a", "xc_v")
        U_ = {n: sem(n) for n in N_UNIT}
        m0_v = sem("m0_v")
        z_g, ld_e, ld_k = sem("z_g"), sem("ld_e"), sem("ld_k")

        block = ctx.enter_context(nc.Block())

        @block.sync
        def _(sp):
            sp.dma_start(x[:, :, :], A["L0_attn_hidden_states"].rearrange("b (t p) d -> p (b t) d", p=P)).then_inc(ld_x, 16)
            sp.dma_start(wk[:, :], A["L0_attn_wk"]).then_inc(ld_w, 16)
            sp.dma_start(wv[:, :], A["L0_attn_wv"]).then_inc(ld_w, 16)
            sp.dma_start(wq[:, :], A["L0_attn_wq"]).then_inc(ld_w, 16)
            sp.dma_start(wo[:, :, :], A["L0_attn_wo"].rearrange("(a q) n -> q a n", q=P)).then_inc(ld_w, 16)
            for hh in range(2):
                src = A["L0_attn_W1"].rearrange("(a h) c d -> h c a d", h=2)[hh]
                sp.dma_start(W1s[hh * 64:hh * 64 + 64, :, :], src).then_inc(ld_w, 16)
            sp.dma_start(wg0[:, :], A["L0_ffn_Wg"]).then_inc(ld_m, 16)
            for b in range(B):
                sp.dma_start(bg0[b * E0:(b + 1) * E0, :], A["L0_ffn_bg"].rearrange("(e o) -> e o", o=1)).then_inc(ld_m, 16)
            for n in range(3):
                if n < 2:
                    sp.dma_start(ew[n][:, :, :], A[f"L0_ffn_w{n + 1}"].rearrange("e d o -> d e o")).then_inc(ld_m, 16)
                sp.dma_start(eb[:, n, :], A[f"L0_ffn_b{n + 1}"].rearrange("e o -> o e").broadcast_to([P, E0])).then_inc(ld_m, 16)
            for n, name in enumerate(("Wq", "Wk", "Wv", "Wo")):
                sp.dma_start(w4[:, n, :], A["L1_attn_" + name]).then_inc(ld_2, 16)
            sp.dma_start(b1r[:, :], A["L1_ffn_b1"].rearrange("e (a q) -> (e a) q", q=P)).then_inc(ld_2, 16)
            sp.dma_start(b2r[:, :], A["L1_ffn_b2"]).then_inc(ld_2, 16)
            sp.dma_start(boB[:, :], A["L1_attn_bo"].rearrange("(a q) -> a q", a=1).broadcast_to([P, P])).then_inc(ld_2, 16)
            sp.dma_start(Wg1[:, :, :], A["L1_ffn_Wg"].rearrange("r h e -> h r e")).then_inc(ld_2, 16)
            sp.dma_start(bgB[:, :, :].rearrange("p r e -> p (r e)"), A["L1_ffn_bg"].rearrange("(a r) e -> a (r e)", a=1).broadcast_to([P, R1 * E1])).then_inc(ld_2, 16)
            sp.wait_ge(U_["att_a"], 2 * NC)
            sp.dma_start(ew[2], A["L0_ffn_w3"].rearrange("e d o -> d e o")).then_inc(ld_e, 16)
            sp.wait_ge(x1_v, B)
            sp.dma_start(W2[:, :, :, :], A["L1_ffn_W2"].rearrange("e (a q) h -> q e a h", q=P)).then_inc(ld_k, 16)
            sp.dma_start(W1r[:, :, :], A["L1_ffn_W1"].rearrange("e h f -> h e f")).then_inc(ld_1, 16)
            out_v = out.rearrange("b (t p) d -> p b t d", p=P)
            with sp.Fori(0, B) as i:
                sp.wait_ge(L_["fin_v"], i + 1)
                sp.dma_start(out_v[:, bass.ds(i, 1), :, :].rearrange("p o t d -> p (o t) d"), fin[:, :, :]).then_inc(L_["out_d"], 16)
            sp.wait_ge(L_["out_d"], 16 * B)

        N_W, N_S, N_M = 6, 2 + 4 + 2 + 8, 5 + 5

        def quads(i, r):
            live, before = not (isinstance(i, int) and i == B), not (isinstance(i, int) and i == 0)
            return live, (before if r == 0 else live), (before if r <= 1 else live)

        def counted(n):
            return not isinstance(n, int) or n > 0

        N_2 = 9

        SCORES = {2: 1, 3: 1, 4: 1, 5: 1, 6: 1, 7: 1, 8: 1, 10: 1, 12: 1, 14: 1, 16: 1, 17: 1, 18: 1, 19: 1, 20: 1, 21: 1}

        @block.scalar
        def _(act):
            act.dma_start(cst[:, :], const_d).then_inc(ld_c, 16)
            g = A["L0_attn_gamma"].rearrange("h a d -> a (h d)")
            act.dma_start(gamB[:, :], g.broadcast_to([P, D])).then_inc(ld_s, 16)
            act.dma_start(th[:, :], A["L0_attn_theta"].rearrange("h d a -> a (h d)").broadcast_to([P, D])).then_inc(ld_s, 16)
            act.wait_ge(ln_xn, 1)
            act.activation(xsq[:, :, :], xn[:, :, :], ACT.Square).then_inc(ln_sq, 1)
            act.wait_ge(z_g, 1)
            for r in (0, 32):
                act.dma_start(gb2[r:r + 1, 0, :], g).then_inc(ld_s, 16)
                act.dma_start(gb2[r:r + 1, 1, :], A["L0_attn_beta"].rearrange("h a d -> a (h d)")).then_inc(ld_s, 16)
            for n in range(2):
                act.dma_start(Bst[:, n, :], A["L0_attn_b1"].rearrange("h a d -> a (h d)").broadcast_to([2, D])).then_inc(ld_s, 16)
            for hh in range(2):
                gr = A["L0_attn_gamma"].rearrange("(a h) o d -> h o a d", h=2)[hh]
                br = A["L0_attn_beta"].rearrange("(a h) o d -> h o a d", h=2)[hh]
                act.dma_start(gam[hh * 64:hh * 64 + 64, :], gr[0].rearrange("a d -> d a"), allow_slow_non_contiguous=True).then_inc(ld_s, 16)
                act.dma_start(bet[hh * 64:hh * 64 + 64, :], br[0].rearrange("a d -> d a"), allow_slow_non_contiguous=True).then_inc(ld_s, 16)
                tr = A["L0_attn_theta_bias"].rearrange("h o d -> o (h d)")
                act.dma_start(tb[hh * 64:hh * 64 + 64, :], tr.broadcast_to([64, H])).then_inc(ld_s, 16)
                act.dma_start(alpha[hh * 64:hh * 64 + 64, :], A["L0_attn_alpha"].rearrange("(k o) -> k o", o=1)).then_inc(ld_s, 16)
            act.wait_ge(ln_xn, 2)
            act.wait_ge(ld_c, 16)
            act.activation(st[:, 2, :], st[:, 1, :], ACT.Sqrt, bias=C("ln_eps"), scale=1.0 / P).then_inc(ln_sd, 1)
            for n in range(4):
                act.wait_ge(tr_n, n + 1)
                act.activation(xnT[:, n * 512:(n + 1) * 512], bank[n][:, :], ACT.Copy).then_inc(tr_c, 1)
            act.wait_ge(tr_c, 4)
            act.activation(xch[:, :].rearrange("p (b c) -> p b c", b=B), xnT[:, :].rearrange("p (b s) -> p b s", b=B)[:, :, 0:K], ACT.Copy).then_inc(U_["xc_a"], 1)
            def evac(dst, m, n):
                act.wait_ge(U_["pj_p"], n)
                act.activation(dst, bank[2 + m % 2][:, :], ACT.Copy).then_inc(U_["pj_a"], 1)

            def tokens_of(i):
                act.activation(xch[:, :].rearrange("p (b c) -> p b c", b=B), xnT[:, :].rearrange("p (b s) -> p b s", b=B)[:, :, bass.ds(i * K, K)],
                               ACT.Copy).then_inc(U_["xc_a"], 1)

            def keys(n):
                for m in range(4):
                    evac(kT[:, 2 * m:2 * m + 2, :, :].rearrange("p a b c -> p (a b c)"), m, n + m + 1)

            keys(0)
            act.wait_ge(prep_p, 1)
            for n in range(2):
                act.activation(wqT[:, 4 * n:4 * n + 4, :], bank[5 + n][:, :], ACT.Copy).then_inc(prep_a, 1)
            act.wait_ge(prep_p, 2)
            act.activation(Wqo[:, :], bank[7][:, 0:P], ACT.Copy).then_inc(prep_a, 1)
            act.activation(bo0[:, :], bank[7][:, P:P + 1], ACT.Copy).then_inc(prep_a, 1)
            act.wait_ge(lr_v, 1)
            act.activation(eta[:, :, :, :], eta[:, :, :, :], ACT.Sigmoid).then_inc(lr_a, 1)
            def chunk(i, live=True, before=True, more=True):
                j = i - 1

                def sqz_(u):
                    if live:
                        act.wait_ge(U_["z_p"], 4 * i + u + 1)
                        act.activation(sqz[:, u % 2, :], bank[u % 2][:, :], ACT.Square).then_inc(U_["sqz_a"], 1)

                def xku(u):
                    if live:
                        if u == 0 and before:
                            act.wait_ge(U_["dw_p"], 4 * i)
                        evac(XK[:, u, :], 0, 16 * i + 4 + 2 * u + 1)
                        evac(U[:, u, :], 1, 16 * i + 4 + 2 * u + 2)
                    if not before and u == 2:
                        act.wait_ge(lg_v, 2)
                        act.activation(rkp[:, 1, :], lgt[:, :], ACT.Exp, bias=es[:, 0:1], accum_out=es[:, 1:2]).then_inc(ex_a, 1)

                def std(u):
                    if live:
                        act.wait_ge(U_["ss_v"], 4 * i + u + 1)
                        act.activation(sm[:, u, 1, :], sm[:, u, 0, :], ACT.Sqrt, bias=C("ttt_eps"), scale=1.0 / HD).then_inc(U_["sd_a"], 1)

                def zqs(u):
                    if before:
                        act.wait_ge(U_["zq_p"], 4 * j + u + 1)
                        act.activation(sq2[:, u % 2, :], bank[6][:, :], ACT.Square).then_inc(U_["zs_a"], 1)

                def stdq(u):
                    if before:
                        act.wait_ge(U_["sq_v"], 4 * j + u + 1)
                        act.activation(rq[:, u, 1, :], rq[:, u, 0, :], ACT.Sqrt, bias=C("ttt_eps"), scale=1.0 / HD).then_inc(U_["sdq_a"], 1)

                def turned(u):
                    if before:
                        act.wait_ge(U_["at_p"], 4 * j + u + 1)
                        act.activation(AT[:, u % 2, :], bank[7][:, :], ACT.Copy).then_inc(U_["at_a"], 1)

                def att(g):
                    if before:
                        act.wait_ge(U_["att_p"], 2 * j + g + 1)
                        act.activation(attnT[:, :].rearrange("p (b s) -> p b s", b=B)[:, 2 * g:2 * g + 2, bass.ds(j * K, K)],
                                       bank[7][:, 0:P].rearrange("p (b s) -> p b s", b=2), ACT.Identity, bias=bo0[:, :]).then_inc(U_["att_a"], 1)

                sqz_(0), sqz_(1), std(0), xku(0), std(1), zqs(0), sqz_(2), stdq(0), std(2), xku(1), zqs(1), sqz_(3), stdq(1), std(3)
                xku(2), turned(0), zqs(2), stdq(2), xku(3), turned(1), att(0), zqs(3)
                if not live:
                    stdq(3)
                if live:
                    for m in range(4):
                        if m == 2:
                            stdq(3)
                        evac(qT[:, 2 * m:2 * m + 2, :, :].rearrange("p a b c -> p (a b c)"), m, 16 * i + 12 + m + 1)
                turned(2)
                if more:
                    tokens_of(i + 1)
                turned(3), att(1)
                if not before:
                    act.wait_ge(rT_p, 1)
                    act.activation(rpT[:, :, :, :], bank[7][:, :].rearrange("p (k t r) -> p k t r", k=2, t=NT), ACT.Copy).then_inc(rT_a, 1)
                if more:
                    keys(16 * i + 16)

            chunk(0, before=False)
            with act.Fori(1, NC - 1) as i:
                chunk(i)
            chunk(NC - 1, more=False)
            chunk(NC, live=False, more=False)

            n = 0
            for b in range(B):
                act.wait_ge(mj_p, n + 1)
                act.activation(tokT[:, b, :, :], bank[n % 4][:, :].rearrange("p (e k) -> p e k", e=E0), ACT.Copy).then_inc(mj_a, 1)
                n += 1
                for g in range(E0 // 4):
                    act.wait_ge(mj_p, n + 1)
                    act.activation(WPT[:, b, g, :], bank[n % 4][:, :], ACT.Copy).then_inc(mj_a, 1)
                    n += 1
            for k, h in enumerate((h1, h2)):
                for g in range(E0 // 4):
                    act.wait_ge(mj_p, n + 1)
                    for j in range(4):
                        last = act.activation(h[:, 4 * g + j, :], bank[n % 4][:, j * P:(j + 1) * P], ACT.Relu, bias=eb[:, k, 4 * g + j:4 * g + j + 1])
                    last.then_inc(mj_a, 1)
                    n += 1
            for g in range(E0 // 4):
                act.wait_ge(mj_p, n + 1)
                act.activation(o3[:, g, :, :], bank[n % 4][:, :].rearrange("p (b d) -> p b d", b=B), ACT.Identity, bias=b3s[:, g:g + 1]).then_inc(mj_a, 1)
                n += 1


            act.wait_ge(l2_v, 1)
            act.activation(sq_2[:, :, :], xn2[:, :, :], ACT.Square).then_inc(l2_a, 1)
            act.wait_ge(l2_v, 2)
            act.activation(st2[:, 2, :], st2[:, 1, :], ACT.Sqrt, bias=C("ln_eps"), scale=1.0 / P).then_inc(l2_a, 1)
            act.wait_ge(w2p, 1)
            act.activation(wT4[:, :, :], bank[0][:, :].rearrange("p (n c) -> p n c", n=4), ACT.Copy).then_inc(w2a, 1)
            act.activation(b1c[:, :], bank[1][:, 0:E1 * NF], ACT.Copy).then_inc(w2a, 1)
            for b in range(B):
                act.wait_ge(t2_p, b + 1)
                act.activation(xn2T[:, b * S:(b + 1) * S], bank[2 + b][:, :], ACT.Copy).then_inc(t2_a, 1)
            act.wait_ge(t2_a, B)

            def round_(i, r):
                live, has1, has2 = quads(i, r)

                def part(k):
                    act.wait_ge(L_["pr_p"], 12 * i + 3 * r + k)
                    n = (3 * r + k + 1) % 2
                    if k == 1:
                        last = act.activation(hi[:, n, :], bank[5][:, :], ACT.Identity, bias=C("k_ones"))
                    else:
                        last = act.activation(hi[:, n, :], bank[5][:, :], ACT.Copy)
                    last.then_inc(L_["pr_a"], 1)

                def exps(n):
                    act.wait_ge(L_["tq_p"], 64 * i + 16 * r - 16 + n + 1)
                    if counted(64 * i + 16 * r - 16 + n - 7):
                        act.wait_ge(L_["pv_p"], 64 * i + 16 * r - 16 + n - 7)
                    act.activation(ex[:, n % 8, :], bank[n % 2][:, :], ACT.Exp, scale=float(AD) ** -0.5).then_inc(L_["tq_a"], 1)

                def gelu(n):
                    act.wait_ge(L_["h_p"], 64 * i + 16 * r + n + 1)
                    if counted(64 * i + 16 * r + n - 7):
                        act.wait_ge(L_["w_p"], 64 * i + 16 * r + n - 7)
                    act.activation(hd[:, n % 8, :], bank[n % 2][:, :], ACT.Gelu_apprx_tanh, bias=b1c[:, n:n + 1]).then_inc(L_["h_a"], 1)

                if has2:
                    act.wait_ge(L_["pv_p"], 64 * i + 16 * r - 16)
                    act.activation(ob[:, :], bank[6][:, :], ACT.Copy).then_inc(L_["o_a"], 1)
                if live and r:
                    act.wait_ge(L_["cur_p"], 3 * i + r)
                    act.activation(curT[:, :], bank[7][:, :], ACT.Copy).then_inc(L_["cur_a"], 1)
                elif live:
                    act.activation(curT[:, :], xn2T[:, bass.ds(i * S, S)], ACT.Copy).then_inc(L_["cur_a"], 1)
                if has1:
                    part(0)
                for n in range(8 if live else 0):
                    gelu(n)
                    if n == 2:
                        part(1)
                    if n == 5:
                        part(2)
                if live:
                    act.wait_ge(L_["z_v"], 4 * i + r + 1)
                    act.activation(gt[:, 1, :], gt[:, 0, :], ACT.Exp).then_inc(L_["e_a"], 1)
                for n in range(8):
                    if has1:
                        exps(n)
                    if n == 2 and live:
                        act.wait_ge(L_["ct_p"], 4 * i + r + 1)
                        act.activation(cwT[:, :], bank[7][0:E1, :], ACT.Copy).then_inc(L_["ct_a"], 1)
                for n in range(8, 16):
                    if live:
                        gelu(n)
                    if n == 10 and r == 1 and has2:
                        act.wait_ge(L_["at2_p"], i)
                        act.activation(aT[:, :], bank[7][:, :], ACT.Copy).then_inc(L_["at2_a"], 1)
                for n in range(8, 16 if has1 else 8):
                    exps(n)

            for r in range(R1):
                round_(0, r)
            with act.Fori(1, B) as i:
                for r in range(R1):
                    round_(i, r)
            for r in range(2):
                round_(B, r)

        @block.vector
        def _(dve):
            n = [0]

            def link(ins):
                n[0] += 1
                ins.then_inc(vs, 1)
                dve.wait_ge(vs, n[0])

            dve.wait_ge(ld_x, 16)
            bc = lambda t: t.unsqueeze(2).broadcast_to([P, B * NT, P])
            link(dve.tensor_reduce(st[:, 0, :], x[:, :, :], AX_X, ALU.add))
            link(dve.tensor_scalar(st[:, 3, :], st[:, 0, :], 1.0 / P, None, ALU.mult))
            dve.tensor_tensor(xn[:, :, :], x[:, :, :], bc(st[:, 3, :]), ALU.subtract).then_inc(ln_xn, 1)
            dve.memset(wrk[:, 1, :], 1.0)
            link(dve.memset(wgP[:, :, :], 0.0))
            dve.wait_ge(ld_w, 16 * N_W)
            dve.tensor_copy(wkh[:, :], wk[:, :])
            link(dve.tensor_copy(wqh[:, :], wq[:, :]))
            dve.tensor_tensor(wkl[:, :], wk[:, :], wkh[:, :], ALU.subtract).then_inc(prep_v, 1)
            dve.wait_ge(ln_sq, 1)
            dve.tensor_reduce(st[:, 1, :], xsq[:, :, :], AX_X, ALU.add).then_inc(ln_xn, 1)
            dve.wait_ge(ln_sd, 1)
            link(dve.reciprocal(st[:, 3, :], st[:, 2, :]))
            for b in range(B):
                dve.tensor_tensor(xn[:, b * NT:(b + 1) * NT, :], xn[:, b * NT:(b + 1) * NT, :],
                                  st[:, 3, b * NT:(b + 1) * NT].unsqueeze(2).broadcast_to([P, NT, P]), ALU.mult).then_inc(ln_xn, 1)
            dve.wait_ge(ld_m, 16 * N_M)
            for b in range(B):
                last = dve.tensor_copy(wgP[:, b, b * E0:(b + 1) * E0], wg0[:, :])
            last.then_inc(wg_v, 1)
            for j in range(4):
                r = slice(32 * j, 32 * j + 32)
                dve.tensor_copy(b3s[r, :], eb[r, 2, :].rearrange("p (g j) -> p j g", j=4)[:, j, :])
            link(dve.tensor_reduce(m0[:, 0, 0:NP], W1s[:, :, :], AX_X, ALU.add))
            dve.tensor_scalar(m0[:, 1, 0:NP], m0[:, 0, 0:NP], 1.0 / HD, None, ALU.mult).then_inc(m0_v, 1)
            dve.wait_ge(ld_s, 16 * N_S)
            link(dve.tensor_tensor(th[:, :], th[:, :], wk[:, :], ALU.mult))
            dve.tensor_reduce(Th[:, :], th[:, :].rearrange("p (h c) -> p h c", h=H), AX_X, ALU.add).then_inc(prep_v, 1)
            dve.wait_ge(U_["xc_a"], 1)
            dve.tensor_tensor(xcl[:, :].rearrange("p (b c) -> p b c", b=B), xnT[:, :].rearrange("p (b s) -> p b s", b=B)[:, :, 0:K],
                              xch[:, :].rearrange("p (b c) -> p b c", b=B), ALU.subtract).then_inc(U_["xc_v"], 1)
            b0 = Bst[:, :, :].rearrange("p g (h c) -> p (g h) c", h=H)
            link(dve.tensor_reduce(mb[:, 0, :], b0, AX_X, ALU.add))
            link(dve.tensor_scalar(mb[:, 1, :], mb[:, 0, :], 1.0 / HD, None, ALU.mult))
            dve.tensor_tensor(b0, b0, mb[:, 1, :].unsqueeze(2).broadcast_to([2, 2 * H, HD]), ALU.subtract).then_inc(state_v, 1)
            dve.wait_ge(z_g, 2)
            dve.wait_ge(m0_v, 1)
            for b in range(B):
                dve.tensor_tensor(Wbd[0:64, b, :, 0:64], W1s[0:64, :, :], m0[0:64, 1, 0:NP].unsqueeze(2).broadcast_to([64, NP, HD]),
                                  ALU.subtract).then_inc(state_v, 1)
            link(dve.tensor_tensor(wu[:, :], wk[:, :], wv[:, :], ALU.subtract))
            link(dve.tensor_tensor(wu[:, :], wu[:, :], gamB[:, :], ALU.mult))
            link(dve.tensor_copy(wuh[:, :], wu[:, :]))
            dve.tensor_tensor(wul[:, :], wu[:, :], wuh[:, :], ALU.subtract)
            link(dve.tensor_scalar(ones[:, :], ident[0:64, :], 0.0, 1.0, ALU.mult, ALU.add))
            link(dve.tensor_tensor(gb2[:, 0, :], gb2[:, 0, :], gb2[:, 1, :], ALU.mult))
            link(dve.tensor_copy(gbr[:, :], gb2[:, 0, :]))
            dve.tensor_tensor(gbr[32:33, :], gb2[32:33, 0, :], gbr[32:33, :], ALU.subtract).then_inc(prep_v, 1)
            link(dve.tensor_scalar(rate[:, :], alpha[:, :], C("token_rate"), 0.0, ALU.add, ALU.max))
            link(dve.tensor_scalar(rate[:, :], rate[:, :], 1.0 / HD, None, ALU.mult))
            dve.wait_ge(lr_p, 1)
            dve.tensor_tensor(eta[:, :, :, :].rearrange("p i g h -> p (i g) h"), bank[4][:, 0:NC * 2 * H].rearrange("p (i h) -> p i h", h=H),
                              tb[:, :].unsqueeze(1).broadcast_to([P, NC * 2, H]), ALU.add).then_inc(lr_v, 1)
            dve.tensor_tensor(wql[:, :], wq[:, :], wqh[:, :], ALU.subtract).then_inc(prep_v, 1)
            dve.wait_ge(lr_a, 1)
            dve.tensor_scalar(eta[:, :, :, :], eta[:, :, :, :], rate[:, :], None, ALU.mult).then_inc(eta_v, 1)
            dve.wait_ge(eta_v, 1)

            def choice(step):
                if step == 0:
                    dve.wait_ge(lg_p, 1)
                    dve.tensor_scalar(lgt[:, :], bank[7][0:BE, :], bg0[:, :], None, ALU.add).then_inc(lg_v, 1)
                    dve.wait_ge(lg_v, 1)
                elif step <= TOP0 // 8:
                    k = step - 1
                    left = lgt[:, :] if k == 0 else wrk[:, 0, :]
                    link(dve.max(m8[:, k, :], left))
                    if k == 0:
                        dve.tensor_scalar(es[:, 0:1], m8[:, 0, 0:1], -1.0, None, ALU.mult).then_inc(lg_v, 1)
                    link(dve.match_replace(wrk[:, 0, :], m8[:, k, :], left, -3.0e38))
                elif step == 5:
                    dve.wait_ge(ex_a, 1)
                    link(dve.tensor_tensor(wrk[:, 0, :], lgt[:, :], wrk[:, 0, :], ALU.not_equal))
                    link(dve.tensor_tensor_scan(lgt[:, :], wrk[:, 1, :], wrk[:, 0, :], 0.0, ALU.mult, ALU.add))
                else:
                    dve.tensor_tensor(rkp[:, 0, :], lgt[:, :], wrk[:, 0, :], ALU.mult).then_inc(rk_v, 1)
                    link(dve.reciprocal(es[:, 2:3], es[:, 1:2]))
                    dve.tensor_scalar(rkp[:, 1, :], rkp[:, 1, :], es[:, 2:3], None, ALU.mult).then_inc(rk_v, 1)

            g3 = lambda t: t.rearrange("p (h c) -> p h c", h=8)
            per = lambda t: t.unsqueeze(2).broadcast_to([P, 8, HD])

            def chunk(i, live=True, before=True, more=True):
                j = i - 1

                def Xa(u):
                    if live:
                        dve.wait_ge(U_["sqz_a"], 4 * i + u + 1)
                        dve.tensor_reduce(sm[:, u, 0, :], g3(sqz[:, u % 2, :]), AX_X, ALU.add).then_inc(U_["ss_v"], 1)

                def Xb(u):
                    if live:
                        n = 4 * i + u + 1
                        dve.wait_ge(U_["sd_a"], n)
                        dve.reciprocal(sm[:, u, 2, :], sm[:, u, 1, :]).then_inc(U_["s1_v"], 1)
                        dve.wait_ge(U_["s1_v"], n)
                        dve.tensor_tensor(g3(xh[:, u, :]), g3(bank[u % 2][:, :]), per(sm[:, u, 2, :]), ALU.mult).then_inc(U_["xh_v"], 1)

                def G(u):
                    if live:
                        n = 4 * i + u + 1
                        dve.wait_ge(U_["t_g"], n)
                        dve.wait_ge(U_["pj_a"], 16 * i + 4 + 2 * u + 2)
                        dve.tensor_tensor(gx[:, u, :], t1[:, u, :], U[:, u, :], ALU.add).then_inc(U_["gx_v"], 1)
                        rates = eta[:, bass.ds(i, 1), u // 2, :].rearrange("p o h -> p (o h)")[:, 8 * (u % 2):8 * (u % 2) + 8]
                        dve.tensor_tensor(sm[:, u, 3, :], rates, sm[:, u, 2, :], ALU.mult).then_inc(U_["a_v"], 1)
                        dve.wait_ge(U_["gx_v"], n)
                        dve.tensor_reduce(sm[:, u, 4, :], g3(gx[:, u, :]), AX_X, ALU.add).then_inc(U_["c_v"], 1)
                        dve.wait_ge(U_["c_v"], 12 * i + 3 * u + 1)
                        dve.tensor_scalar(sm[:, u, 5, :], sm[:, u, 4, :], 1.0 / HD, None, ALU.mult).then_inc(U_["c_v"], 1)
                        dve.wait_ge(U_["c_v"], 12 * i + 3 * u + 2)
                        dve.tensor_tensor(g3(gw[:, u, :]), g3(gx[:, u, :]), per(sm[:, u, 5, :]), ALU.subtract).then_inc(U_["c_v"], 1)

                def R(u):
                    if live:
                        n = 4 * i + u + 1
                        dve.wait_ge(U_["q_g"], n)
                        dve.tensor_reduce(sm[:, u, 6, :], g3(t1[:, u, :]), AX_X, ALU.add).then_inc(U_["w1_v"], 1)
                        dve.wait_ge(U_["w1_v"], n)
                        dve.tensor_scalar(sm[:, u, 4, :], sm[:, u, 6, :], 1.0 / HD, None, ALU.mult).then_inc(U_["s2_v"], 1)

                def Wd(u):
                    if live:
                        dve.wait_ge(U_["v_g"], 4 * i + u + 1)
                        dve.wait_ge(U_["c_v"], 12 * i + 3 * u + 3)
                        dve.tensor_tensor(gw[:, u, :], gw[:, u, :], t1[:, u, :], ALU.subtract).then_inc(U_["w_v"], 1)

                def up(u):
                    if live:
                        g, hf = u // 2, u % 2
                        dve.wait_ge(U_["dw_p"], 4 * i + u + 1)
                        for k in range(2):
                            for hh in range(2):
                                r = slice(64 * hh, 64 * hh + 64)
                                st_ = Wbd[r, 2 * g + k, 4 * hf:4 * hf + 4, r]
                                dve.tensor_tensor(st_, st_, bank[(4, 0)[u % 2] + k][r, :].rearrange("p (a c) -> p a c", a=4)[:, :, r], ALU.subtract)
                        bb = Bst[:, g, 512 * hf:512 * hf + 512]
                        dve.tensor_tensor(bb, bb, bank[6 + u % 2][0:2, :], ALU.subtract).then_inc(U_["up_v"], 1)

                def Qa(u):
                    if before:
                        dve.wait_ge(U_["zs_a"], 4 * j + u + 1)
                        dve.tensor_reduce(rq[:, u, 0, :], g3(sq2[:, u % 2, :]), AX_X, ALU.add).then_inc(U_["sq_v"], 1)

                def Qb(u):
                    if before:
                        dve.wait_ge(U_["sdq_a"], 4 * j + u + 1)
                        dve.reciprocal(rq[:, u, 2, :], rq[:, u, 1, :]).then_inc(U_["rq_v"], 1)
                        dve.wait_ge(U_["rq_v"], 4 * j + u + 1)
                        dve.tensor_tensor(g3(Am[:, u % 2, :]), g3(bank[6][:, :]), per(rq[:, u, 2, :]), ALU.mult).then_inc(U_["A_v"], 1)

                step = (lambda n: None) if before else choice
                Xa(0), Xa(1), Xb(0), Xb(1), step(0), step(1), Qa(0), G(0), Xa(2), Qb(0), Xb(2), step(2), Qa(1), G(1), Xa(3), Qb(1), Xb(3)
                step(3), R(0), Qa(2), G(2), step(4), R(1), Qb(2), Wd(0), Qa(3), G(3), Qb(3), step(5), step(6)
                if more:
                    dve.wait_ge(U_["xc_a"], i + 2)
                    dve.tensor_tensor(xcl[:, :].rearrange("p (b c) -> p b c", b=B), xnT[:, :].rearrange("p (b s) -> p b s", b=B)[:, :, bass.ds((i + 1) * K, K)],
                                      xch[:, :].rearrange("p (b c) -> p b c", b=B), ALU.subtract).then_inc(U_["xc_v"], 1)
                R(2), Wd(1), up(0), R(3), Wd(2), up(1), Wd(3), up(2), up(3)

            chunk(0, before=False)
            with dve.Fori(1, NC - 1) as i:
                chunk(i)
            chunk(NC - 1, more=False)
            chunk(NC, live=False, more=False)
            for b in range(B):
                if b >= 2:
                    dve.wait_ge(wp_g, b - 1)
                    dve.wait_ge(mj_p, 5 * (b - 2) + 1)
                for t in range(NT):
                    last = dve.tensor_tensor(OH[:, b % 2, t, :].rearrange("p (e k) -> p e k", e=E0),
                                             rpT[:, 0, t, b * E0:(b + 1) * E0].unsqueeze(2).broadcast_to([P, E0, TOP0]),
                                             C("slots").unsqueeze(1).broadcast_to([P, E0, TOP0]), ALU.is_equal)
                last.then_inc(oh_v, 1)
            for b in range(B):
                dve.wait_ge(sc_p, b + 1)
                dve.tensor_tensor(x1[:, b * NT:(b + 1) * NT, :], bank[4 + b][:, :].rearrange("p (t d) -> p t d", t=NT),
                                  x[:, b * NT:(b + 1) * NT, :], ALU.add).then_inc(x1_v, 1)


            tok = lambda t: t.unsqueeze(2).broadcast_to([P, B * NT, P])
            dve.wait_ge(x1_v, B)
            dve.wait_ge(ld_2, 16 * N_2)
            link(dve.tensor_reduce(st2[:, 0, :], x1[:, :, :], AX_X, ALU.add))
            link(dve.tensor_scalar(st2[:, 3, :], st2[:, 0, :], 1.0 / P, None, ALU.mult))
            dve.tensor_tensor(xn2[:, :, :], x1[:, :, :], tok(st2[:, 3, :]), ALU.subtract).then_inc(l2_v, 1)
            dve.wait_ge(ld_1, 16)
            dve.tensor_copy(W1h[:, :, :], W1r[:, :, :]).then_inc(w2v, 1)
            dve.wait_ge(l2_a, 1)
            dve.tensor_reduce(st2[:, 1, :], sq_2[:, :, :], AX_X, ALU.add).then_inc(l2_v, 1)
            dve.wait_ge(w2v, 1)
            dve.tensor_tensor(W1l[:, :, :], W1r[:, :, :], W1h[:, :, :], ALU.subtract).then_inc(w2v, 1)
            dve.wait_ge(l2_a, 2)
            link(dve.reciprocal(st2[:, 3, :], st2[:, 2, :]))
            dve.wait_ge(l2_v, 2)
            dve.tensor_tensor(xn2[:, :, :], xn2[:, :, :], tok(st2[:, 3, :]), ALU.mult).then_inc(l2_v, 1)
            dve.memset(Mt[:, :, :], 0.0)
            dve.memset(Vx[:, :, :, :], 0.0).then_inc(w2v, 1)
            link(dve.memset(wr[:, :, :, :], 0.0))
            dve.wait_ge(w2a, 2)
            for k in range(2):
                last = dve.tensor_copy(wr[:, k, :, :].rearrange("p q (j c) -> p (q j) c", c=32)[:, :, 0:24].rearrange("p h (c d) -> p h c d", d=AD),
                                       wT4[:, k, :].rearrange("p (h d) -> p h d", d=AD).unsqueeze(2).broadcast_to([P, AH, 3, AD]))
            link(last)
            link(dve.tensor_copy(wrh[:, :, :, :], wr[:, :, :, :]))
            dve.tensor_tensor(wrl[:, :, :, :], wr[:, :, :, :], wrh[:, :, :, :], ALU.subtract).then_inc(w2v, 1)
            dve.wait_ge(w2v, 3)
            dve.memset(Vx[:, :, :, AD:AD + 1], 1.0).then_inc(w2v, 1)
            dve.wait_ge(w2v, 5)

            n1 = [0]

            def round_(i, r):
                live, has1, has2 = quads(i, r)
                at = V1 * i + V0 - V1 if not isinstance(i, int) else V0 * min(i, 1) + V1 * max(i - 1, 0)

                def link(ins):
                    n1[0] += 1
                    ins.then_inc(L_["v1"], 1)
                    dve.wait_ge(L_["v1"], at + n1[0])

                def part(k):
                    n = 12 * i + 3 * r + k
                    dve.wait_ge(L_["pr_a"], n)
                    h = hi[:, (3 * r + k + 1) % 2, :]
                    if k == 1:
                        dve.scalar_tensor_tensor(out=kx[:, r % 2, :], in0=h, scalar=C("k_minus"), in1=bank[5][:, :], op0=ALU.mult, op1=ALU.add).then_inc(L_["pr_v"], 1)
                        return
                    if counted(8 * i + 2 * r - 1 + k // 2):
                        dve.wait_ge(L_["qs_v"], 8 * i + 2 * r - 1 + k // 2)
                    dve.scalar_tensor_tensor(out=qf[:, :], in0=h, scalar=C("q_minus"), in1=bank[5][:, :], op0=ALU.mult, op1=ALU.add).then_inc(L_["pr_v"], 1)
                    q = qx if k else qm
                    dve.wait_ge(L_["pr_v"], n)
                    dve.tensor_scalar(q[:, 0, :], qf[:, :], C("even"), None, ALU.mult)
                    dve.tensor_scalar(q[:, 1, :], qf[:, :], C("odd"), None, ALU.mult).then_inc(L_["qs_v"], 1)

                def smax():
                    n = s1[0]
                    s1[0] += 1
                    t, h = n // QH, n % QH
                    dve.wait_ge(L_["s1_p"], 64 * i + 16 * r + n + 1)
                    dve.tensor_reduce(Mt[:, t, 32 * h + 24:32 * h + 25], bank[3][:, :], AX_X, ALU.max, negate=True).then_inc(L_["s1_v"], 1)

                def maxima():
                    dve.wait_ge(L_["s1_v"], 64 * i + 16 * (r + 1))
                    m = Mt[:, :, :].rearrange("p t (h c) -> p t h c", c=32)
                    dve.tensor_copy(m[:, :, :, 25:26], m[:, :, :, 24:25]).then_inc(L_["mt_v"], 1)

                n_g = 4 * i + r + 1
                other = lg[:, :, :].unsqueeze(2).broadcast_to([P, NT, E1, E1])
                own = lg[:, :, :].unsqueeze(3).broadcast_to([P, NT, E1, E1])
                sq = lambda k: lgx[:, k, :, :].rearrange("p t (e f) -> p t e f", e=E1)
                g2 = lambda k: gt[:, k, :]
                g3_ = lambda k: gt[:, k, :].rearrange("p t (e) -> p t e", e=E1) if False else gt[:, k, :].rearrange("p (t e) -> p t e", e=E1)
                one = lambda k: gt[:, k, 0:NT]
                per = lambda k: gt[:, k, 0:NT].unsqueeze(2).broadcast_to([P, NT, E1])

                def best():
                    dve.wait_ge(L_["lg_p2"], n_g)
                    b16 = bank[7][:, 0:NT * E1].rearrange("p (t e) -> p t e", e=E1)
                    dve.tensor_tensor(lg[:, :, :], b16, bgB[:, r, :].unsqueeze(1).broadcast_to([P, NT, E1]), ALU.add).then_inc(L_["lg_v2"], 1)
                    dve.wait_ge(L_["lg_v2"], n_g)
                    dve.tensor_tensor(sq(0), other, own, ALU.is_gt)
                    dve.tensor_tensor(sq(1), other, own, ALU.is_equal)
                    link(dve.tensor_reduce(one(2), lg[:, :, :], AX_X, ALU.max))
                    dve.tensor_tensor(g3_(0), lg[:, :, :], per(2), ALU.subtract).then_inc(L_["z_v"], 1)
                    link(dve.tensor_tensor(lgx[:, 2, :, :], lgx[:, 1, :, :], C("lower").unsqueeze(1).broadcast_to([P, NT, E1 * E1]), ALU.mult))
                    link(dve.tensor_tensor(lgx[:, 1, :, :], lgx[:, 0, :, :], lgx[:, 2, :, :], ALU.add))
                    link(dve.tensor_reduce(g3_(3), sq(1), AX_X, ALU.add))
                    link(dve.tensor_scalar(g2(4), g2(3), 2.0, None, ALU.is_lt))

                def weigh():
                    dve.wait_ge(L_["e_a"], n_g)
                    link(dve.tensor_tensor(g2(5), g2(1), g2(4), ALU.mult))
                    link(dve.tensor_reduce(one(6), g3_(5), AX_X, ALU.add))
                    link(dve.reciprocal(one(7), one(6)))
                    dve.tensor_tensor(cw[:, :, :], g3_(5), per(7), ALU.mult).then_inc(L_["cw_v"], 1)

                def bias():
                    dve.wait_ge(L_["cb_p"], n_g)
                    dve.wait_ge(L_["cc_v"], i + 1)
                    if r:
                        dve.wait_ge(L_["y_v"], 16 * i + 4 * r)
                    dve.tensor_tensor(cur[:, :, :], bank[7][:, :].rearrange("p (t d) -> p t d", t=NT), cur[:, :, :], ALU.add).then_inc(L_["cb_v"], 1)

                def expert(e):
                    dve.wait_ge(L_["w_p"], 64 * i + 16 * r + 4 * e + 4)
                    dve.wait_ge(L_["cb_v"], n_g)
                    if e:
                        dve.wait_ge(L_["y_v"], 16 * i + 4 * r + e)
                    for t in range(NT):
                        last = dve.scalar_tensor_tensor(out=cur[:, t, :], in0=bank[2 + 2 * (e % 2)][:, t * P:(t + 1) * P], scalar=cw[:, t, e:e + 1],
                                                        in1=cur[:, t, :], op0=ALU.mult, op1=ALU.add)
                    last.then_inc(L_["y_v"], 1)

                def outputs():
                    j = (r - 2) % 4
                    dve.wait_ge(L_["o_p"], 4 * i + r - 1)
                    o4 = bank[7][:, :].rearrange("p (t h c) -> p t h c", t=NT, c=32)
                    link(dve.tensor_scalar(den[:, 0, :, :], o4[:, :, :, AD:AD + 1].rearrange("p t h o -> p t (h o)"), 1e-8, None, ALU.add))
                    link(dve.reciprocal(den[:, 1, :, :], den[:, 0, :, :]))
                    dve.tensor_tensor(an[:, :, j * 32:(j + 1) * 32].rearrange("p t (h d) -> p t h d", d=AD), o4[:, :, :, 0:AD],
                                      den[:, 1, :, :].unsqueeze(3).broadcast_to([P, NT, QH, AD]), ALU.mult).then_inc(L_["o_v"], 1)

                s1 = [0]
                if live:
                    dve.wait_ge(L_["cur_a"], n_g)
                    link(dve.tensor_copy(cH[:, :], curT[:, :]))
                    dve.tensor_tensor(cL[:, :], curT[:, :], cH[:, :], ALU.subtract).then_inc(L_["cs_v"], 1)
                if has1:
                    part(0)
                if r == 0 and has1:
                    dve.wait_ge(L_["y_v"], 16 * i)
                    if counted(16 * i - 16):
                        dve.wait_ge(L_["out_d"], 16 * i - 16)
                    link(dve.tensor_tensor(fin[:, :, :], cur[:, :, :], boB[:, :].unsqueeze(1).broadcast_to([P, NT, P]), ALU.add))
                    link(dve.tensor_tensor(fin[:, :, :], fin[:, :, :], x1[:, bass.ds(i * NT - NT, NT), :], ALU.add))
                if r == 0 and live:
                    dve.tensor_copy(cur[:, :, :], xn2[:, bass.ds(i * NT, NT), :]).then_inc(L_["cc_v"], 1)
                    dve.wait_ge(L_["cs_v"], n_g)
                    dve.tensor_copy(xH[:, :], cH[:, :])
                    dve.tensor_copy(xL[:, :], cL[:, :]).then_inc(L_["xs_v"], 1)
                if live:
                    best()
                    part(1)
                if has2:
                    outputs()
                if live:
                    part(2)
                if r == 0 and live:
                    dve.wait_ge(L_["v_p"], i + 1)
                    dve.tensor_copy(Vs[:, :, :], bank[7][:, :].rearrange("p (t d) -> p t d", t=NT)).then_inc(L_["v_v"], 1)
                if r == 1 and live:
                    if counted(64 * i):
                        dve.wait_ge(L_["pv_p"], 64 * i)
                    dve.wait_ge(L_["v_v"], i + 1)
                    dve.tensor_copy(Vx[:, :, :, 0:AD], Vs[:, :, :].rearrange("p t (h d) -> p t h d", d=AD)).then_inc(L_["vx_v"], 1)
                if live:
                    weigh()
                for n in range(24 if live else 0):
                    k = n if n < 8 else n - 8 if n >= 16 else None
                    if k == 3:
                        bias()
                    if k is not None and k % NF == 3:
                        expert(k // NF)
                    for _ in range(SCORES.get(n, 0)):
                        smax()
                    if n == 22:
                        maxima()
                    if n == 13 and r == 1 and has2:
                        result(i, link)
                if not live and r == 1:
                    result(i, link)

            def result(i, link):
                dve.wait_ge(L_["ao_p"], i)
                dve.tensor_tensor(fin[:, :, :], bank[7][:, :].rearrange("p (t d) -> p t d", t=NT), fin[:, :, :], ALU.add).then_inc(L_["fin_v"], 1)

            V0, V1 = 4 * (1 + 5 + 3) + 2 * 2, 4 * (1 + 5 + 3) + 4 * 2 + 2
            for r in range(R1):
                round_(0, r)
            assert n1[0] == V0, n1[0]
            n1[0] = 0
            with dve.Fori(1, B) as i:
                for r in range(R1):
                    round_(i, r)
            assert n1[0] == V1, n1[0]
            n1[0] = 0
            for r in range(2):
                round_(B, r)

        @block.gpsimd
        def _(pool):
            pool.memset(gb2[:, :, :], 0.0).then_inc(z_g, 1)
            pool.memset(Wbd[:, :, :, :], 0.0).then_inc(z_g, 1)
            pool.wait_ge(m0_v, 1)
            pool.wait_ge(z_g, 2)
            for b in range(B):
                pool.tensor_tensor(Wbd[64:128, b, :, 64:128], W1s[64:128, :, :], m0[64:128, 1, 0:NP].unsqueeze(2).broadcast_to([64, NP, HD]),
                                   ALU.subtract).then_inc(prep_g, 1)
            pool.wait_ge(prep_g, B)
            pool.wait_ge(ld_s, 16 * N_S)
            pool.wait_ge(ld_w, 16 * N_W)
            pool.tensor_tensor(gg[:, :], gamB[:, :], gamB[:, :], ALU.mult).then_inc(prep_g, 1)
            pool.tensor_tensor(wog[:, :, :], wo[:, :, :], gam[:, :].unsqueeze(2).broadcast_to([P, NP, P]), ALU.mult).then_inc(prep_g, 1)
            pool.wait_ge(prep_g, B + 1)
            g3 = lambda t: t.rearrange("p (h c) -> p h c", h=8)
            per = lambda t: t.unsqueeze(2).broadcast_to([P, 8, HD])

            def chunk(i):
                def t(u):
                    pool.wait_ge(U_["xh_v"], 4 * i + u + 1)
                    pool.tensor_tensor(t1[:, u, :], xh[:, u, :], gg[:, 512 * (u % 2):512 * (u % 2) + 512], ALU.mult).then_inc(U_["t_g"], 1)

                def q(u):
                    pool.wait_ge(U_["gx_v"], 4 * i + u + 1)
                    pool.tensor_tensor(t1[:, u, :], gx[:, u, :], xh[:, u, :], ALU.mult).then_inc(U_["q_g"], 1)

                def v(u):
                    pool.wait_ge(U_["s2_v"], 4 * i + u + 1)
                    pool.tensor_tensor(g3(t1[:, u, :]), g3(xh[:, u, :]), per(sm[:, u, 4, :]), ALU.mult).then_inc(U_["v_g"], 1)

                def wa(u):
                    pool.wait_ge(U_["w_v"], 4 * i + u + 1)
                    pool.tensor_tensor(g3(gw[:, u, :]), g3(gw[:, u, :]), per(sm[:, u, 3, :]), ALU.mult).then_inc(U_["gw_g"], 1)

                t(0), t(1), q(0), t(2), q(1), v(0), t(3), q(2), v(1), wa(0), q(3), v(2), wa(1), v(3), wa(2), wa(3)

            with pool.Fori(0, NC) as i:
                chunk(i)
            for b in range(B):
                pool.wait_ge(oh_v, b + 1)
                if b:
                    pool.wait_ge(mj_p, 5 * b)
                for t in range(NT):
                    last = pool.tensor_tensor(WP[:, t, :].rearrange("p (e k) -> p e k", e=E0), OH[:, b % 2, t, :].rearrange("p (e k) -> p e k", e=E0),
                                              rpT[:, 1, t, b * E0:(b + 1) * E0].unsqueeze(2).broadcast_to([P, E0, TOP0]), ALU.mult)
                last.then_inc(wp_g, 1)

        @block.tensor
        def _(pe):
            pe.wait_ge(ld_c, 16)
            for b in range(B):
                pe.wait_ge(ln_xn, 3 + b)
                for t in range(NT):
                    last = pe.transpose(bank[b][:, t * P:(t + 1) * P], xn[:, b * NT + t, :], ident)
                last.then_inc(tr_n, 1)
            pe.wait_ge(tr_c, 4)
            pe.wait_ge(prep_v, 2)
            for i in range(NC):
                for b in range(B):
                    last = pe.matmul(bank[4][b % 2 * 64:b % 2 * 64 + 64, (i * 2 + b // 2) * H:(i * 2 + b // 2 + 1) * H],
                                     xnT[:, b * S + i * K:b * S + (i + 1) * K], Th[:, :], start=True, stop=True, skip_group_check=True)
            last.then_inc(lr_p, 1)
            def mm3(to, lh, ll, rh, rl, start=True, stop=True):
                pe.matmul(to, lh, rh, start=start, stop=False, skip_group_check=True)
                pe.matmul(to, ll, rh, start=False, stop=False, skip_group_check=True)
                return pe.matmul(to, lh, rl, start=False, stop=stop, skip_group_check=True)

            def features(m, n, wh, wl):
                if counted(n):
                    pe.wait_ge(U_["pj_a"], n)
                to = bank[2 + m % 2]
                for k in range(2):
                    a = slice((2 * m + k) * P, (2 * m + k + 1) * P)
                    last = mm3(to[:, k * 256:(k + 1) * 256], wh[:, a], wl[:, a], xch[:, :], xcl[:, :])
                last.then_inc(U_["pj_p"], 1)

            pe.wait_ge(prep_v, 2)
            pe.wait_ge(U_["xc_v"], 1)
            for m in range(4):
                features(m, m - 1, wkh, wkl)
            pe.wait_ge(ld_w, 16 * N_W)
            pe.wait_ge(ld_s, 16 * N_S)
            for a in range(NP):
                last = pe.transpose(bank[5 + a // 4][:, a % 4 * P:(a % 4 + 1) * P], wq[:, a * P:(a + 1) * P], ident)
            last.then_inc(prep_p, 1)
            pe.wait_ge(prep_a, 2)
            for a in range(NP):
                pe.matmul(bank[7][:, 0:P], wqT[:, a, :], wo[:, a, :], start=(a == 0), stop=(a == NP - 1))
            for a in range(NP):
                last = pe.matmul(bank[7][:, P:P + 1], wo[:, a, :], bet[:, a:a + 1], start=(a == 0), stop=(a == NP - 1))
            last.then_inc(prep_p, 1)
            pe.wait_ge(state_v, B + 1)
            pe.wait_ge(prep_g, B)

            def chunk(i, live=True, before=True, more=True):
                j = i - 1

                def through(u, T, to):
                    g, hf = u // 2, u % 2
                    pe.matmul(to[:, :], half, Bst[:, g, 512 * hf:512 * hf + 512], start=True, stop=False, skip_group_check=True)
                    for a in range(4):
                        for k in range(2):
                            last = pe.matmul(to[64 * k:64 * k + 64, a * P:(a + 1) * P], T[:, 4 * hf + a, 2 * g + k, :], Wbd[:, 2 * g + k, 4 * hf + a, :],
                                             start=False, stop=True, skip_group_check=True)
                    return last

                def Z(u):
                    if live:
                        if u == 0:
                            pe.wait_ge(U_["pj_a"], 16 * i + 4)
                        if before:
                            pe.wait_ge(U_["up_v"], 4 * i)
                        if counted(4 * i + u - 1):
                            pe.wait_ge(U_["xh_v"], 4 * i + u - 1)
                        through(u, kT, bank[u % 2]).then_inc(U_["z_p"], 1)

                def Zq(u):
                    if before:
                        if u == 0:
                            pe.wait_ge(U_["pj_a"], 16 * j + 16)
                            pe.wait_ge(U_["up_v"], 4 * i)
                        else:
                            pe.wait_ge(U_["A_v"], 4 * j + u)
                        through(u, qT, bank[6]).then_inc(U_["zq_p"], 1)

                def xku(u):
                    if live:
                        g, hf = u // 2, u % 2
                        xs, ws = slice(g * P, (g + 1) * P), slice(hf * 512, (hf + 1) * 512)
                        pe.wait_ge(U_["pj_a"], 16 * i + 3 + 2 * u)
                        mm3(bank[2][:, :], xch[:, xs], xcl[:, xs], wkh[:, ws], wkl[:, ws]).then_inc(U_["pj_p"], 1)
                        pe.wait_ge(U_["pj_a"], 16 * i + 4 + 2 * u)
                        pe.matmul(bank[3][:, :], ones[:, :], gbr[:, ws], start=True, stop=False, skip_group_check=True)
                        mm3(bank[3][:, :], xch[:, xs], xcl[:, xs], wuh[:, ws], wul[:, ws], start=False).then_inc(U_["pj_p"], 1)

                def dW(u):
                    if live:
                        pe.wait_ge(U_["gw_g"], 4 * i + u + 1)
                        if counted(4 * i + u - 1):
                            pe.wait_ge(U_["up_v"], 4 * i + u - 1)
                        if before and u == 0:
                            pe.wait_ge(U_["A_v"], 4 * i)
                        if u == 1:
                            pe.wait_ge(U_["xh_v"], 4 * i + 4)
                            if before:
                                pe.wait_ge(U_["att_a"], 2 * i)
                            else:
                                pe.wait_ge(rT_a, 1)
                        pe.matmul(bank[6 + u % 2][0:2, :], half_t, gw[:, u, :], start=True, stop=True)
                        for a in range(4):
                            for k in range(2):
                                r, c = slice(64 * k, 64 * k + 64), slice(a * P, (a + 1) * P)
                                last = pe.matmul(bank[(4, 0)[u % 2] + k][:, c], XK[r, u, c], gw[r, u, c], start=True, stop=True, skip_group_check=True)
                        last.then_inc(U_["dw_p"], 1)

                def turn(u):
                    if before:
                        pe.wait_ge(U_["A_v"], 4 * j + u + 1)
                        if u % 2:
                            pe.wait_ge(U_["at_a"], 4 * j + u)
                        elif counted(2 * j + u // 2):
                            pe.wait_ge(U_["att_a"], 2 * j + u // 2)
                        for a in range(4):
                            last = pe.transpose(bank[7][:, a * P:(a + 1) * P], Am[:, u % 2, a * P:(a + 1) * P], ident)
                        last.then_inc(U_["at_p"], 1)

                def att(g):
                    if before:
                        pe.wait_ge(U_["at_a"], 4 * j + 2 * g + 2)
                        pe.wait_ge(prep_g, B + 2)
                        pe.wait_ge(prep_a, 4)
                        to = bank[7][:, 0:P]
                        for a in range(NP):
                            pe.matmul(to, wog[:, a, :], AT[:, a // 4, a % 4 * P:(a % 4 + 1) * P], start=(a == 0), stop=False, skip_group_check=True)
                        pe.matmul(to, Wqo[:, :], xnT[:, :].rearrange("p (b s) -> p b s", b=B)[:, 2 * g:2 * g + 2, bass.ds(j * K, K)],
                                  start=False, stop=True, skip_group_check=True).then_inc(U_["att_p"], 1)

                Z(0), Z(1)
                if not before:
                    pe.wait_ge(prep_a, 4)
                    pe.wait_ge(wg_v, 1)
                    for b in range(B):
                        last = pe.matmul(bank[7][0:BE, :], wgP[:, b, :], xnT[:, b * S:(b + 1) * S], start=(b == 0), stop=(b == B - 1))
                    last.then_inc(lg_p, 1)
                    pe.wait_ge(prep_v, 3)
                xku(0), Zq(0), Z(2), xku(1), Zq(1), Z(3), xku(2), turn(0), Zq(2), xku(3), turn(1), att(0), Zq(3)
                if live:
                    if not before:
                        pe.wait_ge(prep_v, 4)
                    for m in range(4):
                        features(m, 16 * i + 11 + m, wqh, wql)
                turn(2), turn(3), att(1)
                if not before:
                    pe.wait_ge(rk_v, 2)
                    for k in range(2):
                        for t in range(NT):
                            last = pe.transpose(bank[7][:, (k * NT + t) * BE:(k * NT + t + 1) * BE], rkp[:, k, t * P:(t + 1) * P], ident[0:BE, 0:BE])
                    last.then_inc(rT_p, 1)
                if more:
                    pe.wait_ge(U_["xc_v"], i + 2)
                for step in (0, 1, "f0", 2, "f1", 3, "f2", "f3"):
                    if step in (0, 1, 2, 3):
                        dW(step)
                    elif more:
                        m = int(step[1])
                        features(m, 16 * i + 15 + m, wkh, wkl)

            chunk(0, before=False)
            with pe.Fori(1, NC - 1) as i:
                chunk(i)
            chunk(NC - 1, more=False)
            chunk(NC, live=False, more=False)

            jobs = [0]

            def job(parts):
                n = jobs[0]
                jobs[0] += 1
                if n >= 4:
                    pe.wait_ge(mj_a, n - 3)
                for dst, lhs, rhs, start, stop in parts:
                    last = pe.matmul(bank[n % 4][dst], lhs, rhs, start=start, stop=stop, skip_group_check=True)
                last.then_inc(mj_p, 1)

            pe.wait_ge(U_["att_a"], 2 * NC)
            for b in range(B):
                pe.wait_ge(oh_v, b + 1)
                job([((slice(0, P), slice(0, S)), xn[:, b * NT + t, :], OH[:, b % 2, t, :], t == 0, t == NT - 1) for t in range(NT)])
                pe.wait_ge(wp_g, b + 1)
                for g in range(E0 // 4):
                    n = jobs[0]
                    jobs[0] += 1
                    if n >= 4:
                        pe.wait_ge(mj_a, n - 3)
                    for t in range(NT):
                        last = pe.transpose(bank[n % 4][:, t * P:(t + 1) * P], WP[:, t, g * P:(g + 1) * P], ident)
                    last.then_inc(mj_p, 1)
            n0 = jobs[0]
            pe.wait_ge(ld_m, 16 * N_M)
            pe.wait_ge(mj_a, n0)
            for g in range(E0 // 4):
                job([((slice(0, P), slice(j * P, (j + 1) * P)), ew[0][:, 4 * g + j, :], tokT[:, :, 4 * g + j, :], True, True) for j in range(4)])
            for g in range(E0 // 4):
                pe.wait_ge(mj_a, n0 + g + 1)
                job([((slice(0, P), slice(j * P, (j + 1) * P)), ew[1][:, 4 * g + j, :], h1[:, 4 * g + j, :], True, True) for j in range(4)])
            pe.wait_ge(ld_e, 16)
            for g in range(E0 // 4):
                pe.wait_ge(mj_a, n0 + 4 + g + 1)
                job([((slice(32 * j, 32 * j + 32), slice(b * P, (b + 1) * P)), h2[:, 4 * g + j, b * 32:(b + 1) * 32], ew[2][:, 4 * g + j, :], True, True)
                     for b in range(B) for j in range(4)])
            pe.wait_ge(mj_a, n0 + 12)
            for b in range(B):
                for t in range(NT):
                    to = bank[4 + b][:, t * P:(t + 1) * P]
                    pe.matmul(to, attnT[:, b * S + t * P:b * S + (t + 1) * P], ident, start=True, stop=False, skip_group_check=True)
                    for g in range(E0 // 4):
                        last = pe.matmul(to, WPT[:, b, g, t * P:(t + 1) * P], o3[:, g, b, :], start=False, stop=(g == E0 // 4 - 1), skip_group_check=True)
                last.then_inc(sc_p, 1)

            pe.wait_ge(ld_2, 16 * N_2)
            for n in range(4):
                pe.transpose(bank[0][:, n * P:(n + 1) * P], w4[:, n, :], ident)
            pe.transpose(bank[1][:, 0:E1 * NF], b1r[:, :], ident[0:E1 * NF, 0:E1 * NF]).then_inc(w2p, 1)
            pe.wait_ge(l2_v, 3)
            pe.wait_ge(x1_v, B)
            for b in range(B):
                for t in range(NT):
                    last = pe.transpose(bank[2 + b][:, t * P:(t + 1) * P], xn2[:, b * NT + t, :], ident)
                last.then_inc(t2_p, 1)
            pe.wait_ge(t2_a, B)
            pe.wait_ge(w2v, 5)
            pe.wait_ge(w2a, 2)

            pe.wait_ge(ld_k, 16)

            def round_(i, r):
                live, has1, has2 = quads(i, r)
                s1 = [0]

                def project(k):
                    n = 12 * i + 3 * r + k
                    if counted(n - 1):
                        pe.wait_ge(L_["pr_v"], n - 1)
                    j = (r - 1) % 4 if k == 0 else r
                    if k and r == 0:
                        pe.wait_ge(L_["xs_v"], i + 1)
                    kind = 1 if k == 1 else 0
                    last = mm3(bank[5][:, :], wrh[:, kind, j, :], wrl[:, kind, j, :], xH[:, :], xL[:, :], stop=(k != 0))
                    if k == 0:
                        pe.wait_ge(L_["mt_v"], 4 * i + r)
                        for t in range(NT):
                            last = pe.matmul(bank[5][:, t * P:(t + 1) * P], Mt[:, t, :], ident, start=False, stop=True, skip_group_check=True)
                    last.then_inc(L_["pr_p"], 1)

                def scores():
                    n = s1[0]
                    s1[0] += 1
                    t, h = n // QH, n % QH
                    rows = slice(64 * (h // 2), 64 * (h // 2) + 64)
                    if n == 0:
                        pe.wait_ge(L_["qs_v"], 8 * i + 2 * r + 1)
                    if counted(64 * i + 16 * r + n):
                        pe.wait_ge(L_["s1_v"], 64 * i + 16 * r + n)
                    pe.matmul(bank[3][:, :], qx[rows, h % 2, t * P:(t + 1) * P], kx[rows, r % 2, :], start=True, stop=True).then_inc(L_["s1_p"], 1)

                def turned_scores(n):
                    t, h = n // QH, n % QH
                    rows = slice(64 * (h // 2), 64 * (h // 2) + 64)
                    if n == 0:
                        pe.wait_ge(L_["qs_v"], 8 * i + 2 * r)
                    if n % 8 > 1:
                        pe.wait_ge(L_["tq_a"], 64 * i + 16 * r - 16 + n - 1)
                    elif live:
                        pe.wait_ge(L_["h_a"], 64 * i + 16 * r + n // 8 * 8 + 7 + n % 8)
                    elif counted(64 * i + 16 * r - 16 + n - 1):
                        pe.wait_ge(L_["tq_a"], 64 * i + 16 * r - 16 + n - 1)
                    pe.matmul(bank[n % 2][:, :], kx[rows, (r - 1) % 2, t * P:(t + 1) * P], qm[rows, h % 2, :], start=True, stop=True).then_inc(L_["tq_p"], 1)

                def values(c, t):
                    j = (r - c) % 4
                    if t == 0:
                        if r == 1 and c == 1:
                            pe.wait_ge(L_["vx_v"], i + 1)
                        if counted(4 * i + r - c):
                            pe.wait_ge(L_["o_a"], 4 * i + r - c)
                    pe.wait_ge(L_["tq_a"], 64 * i + 16 * (r - c) + 4 * t + 4)
                    for h in range(QH):
                        pe.matmul(bank[6][32 * h:32 * h + 32, :], Vx[:, t, QH * j + h, :], ex[:, (4 * t + h) % 8, :], start=(t == 0), stop=(t == NT - 1),
                                  skip_group_check=True).then_inc(L_["pv_p"], 1)

                def hidden(n):
                    m = 64 * i + 16 * r + n
                    e, a = n // NF, n % NF
                    if n == 0:
                        pe.wait_ge(L_["cs_v"], 4 * i + r + 1)
                    if n % 8 > 1 or not has1 and counted(m - 1):
                        pe.wait_ge(L_["h_a"], m - 1)
                    if n % 8 <= 1 and counted(64 * i + 16 * r - 16 + n // 8 * 8 - 1 + n % 8):
                        pe.wait_ge(L_["tq_a"], 64 * i + 16 * r - 16 + n // 8 * 8 - 1 + n % 8)
                    c = slice(a * P, (a + 1) * P)
                    mm3(bank[n % 2][:, :], W1h[:, e, c], W1l[:, e, c], cH[:, :], cL[:, :]).then_inc(L_["h_p"], 1)

                def outputs(n):
                    e, a = n // NF, n % NF
                    if a == 0 and counted(16 * i + 4 * r + e - 1):
                        pe.wait_ge(L_["y_v"], 16 * i + 4 * r + e - 1)
                    pe.wait_ge(L_["h_a"], 64 * i + 16 * r + n + 1)
                    to = bank[2 + 2 * (e % 2)]
                    for t in range(NT):
                        last = pe.matmul(to[:, t * P:(t + 1) * P], hd[:, n % 8, t * P:(t + 1) * P], W2[:, e, a, :],
                                         start=(a == 0 and t == 0), stop=(a == NF - 1), skip_group_check=True)
                    last.then_inc(L_["w_p"], 1)

                def logits():
                    pe.wait_ge(L_["cur_a"], 4 * i + r + 1)
                    if r == 0 and counted(4 * i + r):
                        pe.wait_ge(L_["cb_v"], 4 * i + r)
                    for t in range(NT):
                        last = pe.matmul(bank[7][:, t * P:(t + 1) * P][:, 0:0 + E1] if False else bank[7][:, t * E1:(t + 1) * E1],
                                         curT[:, t * P:(t + 1) * P], Wg1[:, r, :], start=True, stop=True, skip_group_check=True)
                    last.then_inc(L_["lg_p2"], 1)

                def turn_out():
                    pe.wait_ge(L_["o_a"], 4 * i + r - 1)
                    if live:
                        pe.wait_ge(L_["lg_v2"], 4 * i + r + 1)
                    elif r:
                        pe.wait_ge(L_["o_v"], 4 * i + r - 2)
                    else:
                        pe.wait_ge(L_["cb_v"], 4 * i)
                    for t in range(NT):
                        last = pe.transpose(bank[7][:, t * P:(t + 1) * P], ob[:, t * P:(t + 1) * P], ident)
                    last.then_inc(L_["o_p"], 1)

                def turn_weights():
                    pe.wait_ge(L_["cw_v"], 4 * i + r + 1)
                    for t in range(NT):
                        last = pe.transpose(bank[7][0:E1, t * P:(t + 1) * P], cw[:, t, :], ident)
                    last.then_inc(L_["ct_p"], 1)

                def biases():
                    pe.wait_ge(L_["ct_a"], 4 * i + r + 1)
                    for t in range(NT):
                        last = pe.matmul(bank[7][:, t * P:(t + 1) * P], cwT[:, t * P:(t + 1) * P], b2r[:, :], start=True, stop=True, skip_group_check=True)
                    last.then_inc(L_["cb_p"], 1)

                def turn_heads():
                    pe.wait_ge(L_["o_v"], 4 * i)
                    if live:
                        pe.wait_ge(L_["cb_v"], 4 * i + r + 1)
                    for t in range(NT):
                        last = pe.transpose(bank[7][:, t * P:(t + 1) * P], an[:, t, :], ident)
                    last.then_inc(L_["at2_p"], 1)

                def attention_out():
                    pe.wait_ge(L_["at2_a"], i)
                    for t in range(NT):
                        last = pe.matmul(bank[7][:, t * P:(t + 1) * P], aT[:, t * P:(t + 1) * P], wT4[:, 3, :], start=True, stop=True, skip_group_check=True)
                    last.then_inc(L_["ao_p"], 1)

                if has2:
                    values(2, 2)
                    values(2, 3)
                if live and r:
                    pe.wait_ge(L_["y_v"], 16 * i + 4 * r)
                    if r == 2 and counted(i):
                        pe.wait_ge(L_["fin_v"], i)
                    for t in range(NT):
                        last = pe.transpose(bank[7][:, t * P:(t + 1) * P], cur[:, t, :], ident)
                    last.then_inc(L_["cur_p"], 1)
                if has1:
                    project(0)
                for n in range(8 if live else 0):
                    hidden(n)
                    if n == 1:
                        logits()
                    if n == 2:
                        project(1)
                    if n == 4 and has2:
                        turn_out()
                    if n == 5:
                        project(2)
                    if n == 6 and r == 0:
                        pe.wait_ge(L_["o_v" if has2 else "lg_v2"], 4 * i + r - 1 if has2 else 1)
                        for t in range(NT):
                            last = pe.matmul(bank[7][:, t * P:(t + 1) * P], curT[:, t * P:(t + 1) * P], wT4[:, 2, :], start=True, stop=True, skip_group_check=True)
                        last.then_inc(L_["v_p"], 1)
                if has2 and not live:
                    turn_out()
                for n in range(24):
                    k = n if n < 8 else n - 8 if n >= 16 else None
                    if k is not None and has1:
                        turned_scores(k)
                    if k is not None and live:
                        outputs(k)
                    if k is None and live:
                        hidden(n)
                    if n in (9, 13) and has1:
                        values(1, n // 4 - 2)
                    if live and n == 2:
                        if has2:
                            pe.wait_ge(L_["o_v"], 4 * i + r - 1)
                        if r == 0:
                            pe.wait_ge(L_["v_v"], i + 1)
                        turn_weights()
                    if live and n == 3:
                        biases()
                    if live:
                        for _ in range(SCORES.get(n, 0)):
                            scores()
                    if n == 9 and r == 1 and has2:
                        turn_heads()
                    if n == 12 and r == 1 and has2:
                        attention_out()
                if live and r < 3 or has1:
                    pass

            for r in range(R1):
                round_(0, r)
            with pe.Fori(1, B) as i:
                for r in range(R1):
                    round_(i, r)
            for r in range(2):
                round_(B, r)


_INS = ["L0_attn_hidden_states", "L0_attn_wq", "L0_attn_wk", "L0_attn_wv", "L0_attn_wo", "L0_attn_W1", "L0_attn_b1", "L0_attn_theta",
        "L0_attn_theta_bias", "L0_attn_alpha", "L0_attn_gamma", "L0_attn_beta", "L0_ffn_Wg", "L0_ffn_bg", "L0_ffn_w1", "L0_ffn_b1",
        "L0_ffn_w2", "L0_ffn_b2", "L0_ffn_w3", "L0_ffn_b3", "L1_attn_Wq", "L1_attn_Wk", "L1_attn_Wv", "L1_attn_Wo", "L1_attn_bo",
        "L1_ffn_Wg", "L1_ffn_bg", "L1_ffn_W1", "L1_ffn_b1", "L1_ffn_W2", "L1_ffn_b2"]


def kernel(**inputs):
    import numpy as _np
    import concourse.bacc as _bacc
    from concourse import mybir as _mybir
    from concourse.bass_utils import run_bass_kernel_spmd as _run

    nc = _bacc.Bacc("TRN2", target_bir_lowering=False, num_devices=1)
    arrays, aps = {}, {}
    for name in _INS:
        a = _np.ascontiguousarray(inputs[name])
        arrays[f"in_{name}"] = a
        aps[name] = nc.dram_tensor(f"in_{name}", a.shape, _mybir.dt.from_np(a.dtype), kind="ExternalInput").ap()
    c = constants(_np)
    arrays["constants"] = c
    const_d = nc.dram_tensor("constants", c.shape, _mybir.dt.float32, kind="ExternalInput").ap()
    out = nc.dram_tensor("out_0", (B, S, P), _mybir.dt.float32, kind="ExternalOutput").ap()
    build(nc, aps, out, const_d)
    r = _run(nc, [arrays], core_ids=[0])
    return r.results[0]["out_0"]
```

```python
from contextlib import ExitStack

import concourse.bass as bass
from concourse import mybir

F32 = mybir.dt.float32
F32R = mybir.dt.float32r
ALU = mybir.AluOpType
ACT = mybir.ActivationFunctionType
AX_X = mybir.AxisListType.X

P = 128
B, S = 4, 512
NT = S // P
H, HD = 16, 64
NP = H // 2
K = 64
NC = S // K
D = H * HD
W = NP * HD
E0, TOP0 = 16, 32
AH, AD = 16, 8
QH = 4
NQ = AH // QH
E1, F1, R1 = 4, 512, 4
NF = F1 // P

CONST = {}


def constants(np):
    cols, at = [], 0

    def put(name, a):
        nonlocal at
        full = np.zeros((P, a.shape[1]), np.float32)
        full[:a.shape[0]] = a
        cols.append(full)
        CONST[name] = (at, a.shape[0], a.shape[1])
        at += a.shape[1]

    part = np.arange(P)
    put("ident", np.eye(P))
    half = (part[None, :] // K == np.arange(2)[:, None]).astype(np.float32)
    put("half", half)
    put("half_t", half.T)
    put("token_rate", (1.0 / (part % K + 1))[:, None])
    put("slots", np.tile(np.arange(1, TOP0 + 1)[None], (P, 1)))
    low = (np.arange(E1)[None, :] < np.arange(E1)[:, None]).astype(np.float32)
    put("lower", np.tile(low.reshape(1, -1), (P, 1)))
    row = part % 32
    put("q_minus", -(((row >= 8) & (row < 16)) | (row == 25)).astype(np.float32)[:, None])
    put("k_minus", (-((row >= 16) & (row < 24)).astype(np.float32)
                    + ((row == 24) | (row == 25)))[:, None])
    put("k_ones", ((row == 24) | (row == 25)).astype(np.float32)[:, None])
    put("even", ((part // 32) % 2 == 0).astype(np.float32)[:, None])
    put("odd", ((part // 32) % 2 == 1).astype(np.float32)[:, None])
    put("ln_eps", np.full((P, 1), 1e-5))
    put("ttt_eps", np.full((P, 1), 1e-6))
    return np.concatenate(cols, 1).astype(np.float32)


def build(nc, A, out, const_d, dbg=None):
    with ExitStack() as ctx:
        def sb(name, shape, dt=F32):
            return ctx.enter_context(nc.sbuf_tensor(name, shape, dt))

        def sem(name):
            return ctx.enter_context(nc.semaphore(name))

        bank = [ctx.enter_context(nc.psum_tensor(f"bank{n}", [P, 512], F32)) for n in range(8)]

        cst = sb("cst", [P, const_d.shape[1]])
        x = sb("x", [P, B * NT, P])
        x1 = x
        st2 = sb("st2", [P, 4, B * NT])
        xn = sb("xn", [P, B * NT, P])
        x2 = xn2 = xn
        w4 = sb("w4", [P, 4, P])
        b1r = sb("b1r", [E1 * NF, P])
        b2r = sb("b2r", [E1, P])
        boB = sb("boB", [P, P])
        Wg1 = sb("Wg1", [P, R1, E1])
        bgB = sb("bgB", [P, R1, E1])

        first_layer = ExitStack()

        def sb(name, shape, dt=F32):
            return first_layer.enter_context(nc.sbuf_tensor(name, shape, dt))

        PIECE = B * W
        arena = sb("arena", [P, 10 * PIECE])

        def piece(k, n=PIECE, off=0):
            return arena[:, k * PIECE + off:k * PIECE + off + n]

        def C(name):
            at, rows, width = CONST[name]
            return cst[0:rows, at:at + width]

        ident, half, half_t = C("ident"), C("half"), C("half_t")

        st = sb("st", [P, 4, B * NT])
        xnT = sb("xnT", [P, B * S])
        xsq = piece(0).rearrange("p (t d) -> p t d", d=P)
        wq = piece(1, D)
        wk = piece(1, D, D)
        wu = piece(5, D, D)
        W1s = piece(3, NP * HD).rearrange("p (a d) -> p a d", a=NP)
        wkh, wkl, wqh, wql, wuh, wul = (sb(n, [P, D], F32R) for n in ("wkh", "wkl", "wqh", "wql", "wuh", "wul"))
        wv = piece(7, D, D)
        wo = piece(8, D).rearrange("p (a c) -> p a c", a=NP)
        wog = sb("wog", [P, NP, P])
        wqT = piece(6, D).rearrange("p (a c) -> p a c", a=NP)
        gam = sb("gam", [P, NP])
        bet = sb("bet", [P, NP])
        gamB = piece(6, D, D)
        gg = sb("gg", [P, D])
        gb2 = piece(4).rearrange("p (k w) -> p k w", k=2)[0:64]
        gbr = sb("gbr", [64, D], F32R)
        ones = sb("ones", [64, P], F32R)
        th = piece(7, D)
        Th = sb("Th", [P, H])
        tb = sb("tb", [P, H])
        alpha = sb("alpha", [P, 1])
        rate = sb("rate", [P, 1])
        eta = sb("eta", [P, NC, 2, H])
        Wbd = sb("Wbd", [P, B, NP, P])
        Bst = sb("Bst", [2, 2, D])
        m0 = sb("m0", [P, 2, NP])
        mb = sb("mb", [2, 2, 2 * H])
        Wqo = sb("Wqo", [P, P])
        bo0 = sb("bo0", [P, 1])
        attnT = sb("attnT", [P, B * S])

        xch, xcl = (sb(n, [P, B * K], F32R) for n in ("xch", "xcl"))
        kT = piece(0).rearrange("p (a b c) -> p a b c", a=NP, b=B)
        qT = piece(1).rearrange("p (a b c) -> p a b c", a=NP, b=B)
        XK, U, xh, t1, gx, gw = (piece(n).rearrange("p (u w) -> p u w", u=4) for n in (2, 3, 5, 6, 7, 8))
        sqz = piece(4, PIECE // 2).rearrange("p (u w) -> p u w", u=2)
        sq2 = piece(4, PIECE // 2, PIECE // 2).rearrange("p (u w) -> p u w", u=2)
        sm = sb("sm", [P, 4, 7, 8])
        rq = sb("rq", [P, 4, 3, 8])
        Am = piece(9, PIECE // 2).rearrange("p (u w) -> p u w", u=2)
        AT = piece(9, PIECE // 2, PIECE // 2).rearrange("p (u w) -> p u w", u=2)

        BE = B * E0
        wg0 = sb("wg0", [P, E0])
        wgP = sb("wgP", [P, B, BE])
        bg0 = sb("bg0", [BE, 1])
        ew = [sb(f"ew{n}", [P, E0, P]) for n in range(2)] + [piece(9).rearrange("p (e o) -> p e o", e=E0)]
        eb = sb("eb", [P, 3, E0])
        b3s = sb("b3s", [P, E0 // 4])
        lgt = piece(9, S)[0:BE]
        wrk = piece(9, 2 * S, 2 * S).rearrange("p (k s) -> p k s", k=2)[0:BE]
        m8 = sb("m8", [BE, 4, 8])
        es = sb("es", [BE, 4])
        rkp = attnT[0:BE, 0:2 * S].rearrange("p (k s) -> p k s", k=2)
        rpT = sb("rpT", [P, 2, NT, BE])
        OH = piece(0, 2 * PIECE).rearrange("p (q t k) -> p q t k", q=2, t=NT)
        WP = piece(2).rearrange("p (t k) -> p t k", t=NT)
        WPT = piece(3, 4 * PIECE).rearrange("p (b g s) -> p b g s", b=B, g=E0 // 4)
        tokT = piece(7).rearrange("p (b e k) -> p b e k", b=B, e=E0)
        h1 = piece(8).rearrange("p (e s) -> p e s", e=E0)
        h2 = piece(0).rearrange("p (e s) -> p e s", e=E0)
        o3 = piece(1).rearrange("p (g b d) -> p g b d", g=E0 // 4, b=B)
        sq_2 = piece(2).rearrange("p (t d) -> p t d", d=P)
        first_layer.close()

        def sb(name, shape, dt=F32):
            return ctx.enter_context(nc.sbuf_tensor(name, shape, dt))

        QW = QH * 32
        ex = sb("ex", [P, 8, S])
        hd = sb("hd", [P, 8, S])
        W2 = sb("W2", [P, E1, NF, P])
        W1r = ex[:, 0:4, :]
        W1h = sb("W1h", [P, E1, F1], F32R)
        W1l = sb("W1l", [P, E1, F1], F32R)
        wr = hd[:, 0:2, :].rearrange("p k (q c) -> p k q c", q=NQ)
        wrh = sb("wrh", [P, 2, NQ, QW], F32R)
        wrl = sb("wrl", [P, 2, NQ, QW], F32R)
        wT4 = sb("wT4", [P, 4, P])
        b1c = sb("b1c", [P, E1 * NF])
        xn2T = sb("xn2T", [P, B * S])
        cur = sb("cur", [P, NT, P])
        curT = sb("curT", [P, S])
        xH = sb("xH", [P, S], F32R)
        xL = sb("xL", [P, S], F32R)
        cH = sb("cH", [P, S], F32R)
        cL = sb("cL", [P, S], F32R)
        hi = sb("hi", [P, 2, S], F32R)
        kx = sb("kx", [P, 2, S], F32R)
        qf = sb("qf", [P, S])
        qx = sb("qx", [P, 2, S], F32R)
        qm = sb("qm", [P, 2, S], F32R)
        Mt = sb("Mt", [P, NT, QW])
        Vx = sb("Vx", [P, NT, AH, 32])
        Vs = sb("Vs", [P, NT, P])
        ob = sb("ob", [P, S])
        den = sb("den", [P, 2, NT, QH])
        an = sb("an", [P, NT, P])
        aT = sb("aT", [P, S])
        lg = sb("lg", [P, NT, E1])
        lgx = sb("lgx", [P, 3, NT, E1 * E1])
        gt = sb("gt", [P, 8, NT * E1])
        cw = sb("cw", [P, NT, E1])
        cwT = sb("cwT", [E1, S])
        fin = sb("fin", [P, NT, P])
        l2_loaded, w1_loaded = sem("l2_loaded"), sem("w1_loaded")
        l2_norm_step, l2_squares = sem("l2_norm_step"), sem("l2_squares")
        xn2_turned, xn2_turned_taken, l2_w_turned, l2_w_taken, l2_w_split = sem("xn2_turned"), sem("xn2_turned_taken"), sem("l2_w_turned"), sem("l2_w_taken"), sem("l2_w_split")
        N_ROUNDS = ("cur_turned", "cur_taken", "cur_split", "xn_split", "cur_set", "rows_ready", "rows_high", "rows_taken", "q_masked",
            "v_ready", "v_taken", "v_spread", "scores_ready", "score_max", "maxima_ready", "turned_ready", "exps_ready", "hidden_ready",
            "gelu_ready", "outputs_ready", "expert_added", "values_summed", "heads_taken", "heads_turned", "heads_divided",
            "logits_ready", "logits_taken", "logits_shifted", "gate_exp", "gates_ready", "gates_turned", "gates_taken", "bias_ready",
            "bias_added", "att_turned", "att_turned_taken", "att_out", "result_ready", "result_stored", "own_step")
        ROUND = {n: sem("rounds_" + n) for n in N_ROUNDS}
        moe_loaded = sem("moe_loaded")
        wg_ready, choice_logits, choice_step, choice_exp, ranks_ready, ranks_turned, ranks_taken = (sem(n) for n in (
            "wg_ready", "choice_logits", "choice_step", "choice_exp", "ranks_ready", "ranks_turned", "ranks_taken"))
        onehot_ready, weighted_ready, job_done, job_taken, scattered, x1_ready = (sem(n) for n in (
            "onehot_ready", "weighted_ready", "job_done", "job_taken", "scattered", "x1_ready"))
        x_loaded, consts_loaded, weights_loaded, small_loaded = sem("x_loaded"), sem("consts_loaded"), sem("weights_loaded"), sem("small_loaded")
        squares_ready, dev_ready, norm_step = sem("squares_ready"), sem("dev_ready"), sem("norm_step")
        xn_turned, xn_turned_taken = sem("xn_turned"), sem("xn_turned_taken")
        v_step = sem("v_step")
        prep_dve, prep_pool, prep_act, prep_pe = sem("prep_dve"), sem("prep_pool"), sem("prep_act"), sem("prep_pe")
        rates_raw, rates_biased, rates_sigmoid, eta_ready = sem("rates_raw"), sem("rates_biased"), sem("rates_sigmoid"), sem("eta_ready")
        state_ready = sem("state_ready")
        N_CHUNKS = ("proj_ready", "proj_taken", "z_ready", "z_squared", "z_sumsq", "z_dev", "z_rdev", "xhat_ready", "scaled_ready", "gx_ready",
            "rate_ready", "gx_centred", "gx_xhat", "gx_xhat_sum", "gx_xhat_mean", "xhat_part", "grad_less", "grad_ready", "dw_ready",
            "state_updated", "zq_ready", "zq_squared", "zq_sumsq", "zq_dev", "zq_rdev", "normed_ready", "normed_turned", "turned_taken",
            "att_ready", "att_taken", "tokens_high", "tokens_low")
        CHUNK = {n: sem("chunks_" + n) for n in N_CHUNKS}
        w_mean_ready, l2_pool_step, l2_sumsq = sem("w_mean_ready"), sem("l2_pool_step"), sem("l2_sumsq")
        zeros_ready, w3_loaded, w2_loaded = sem("zeros_ready"), sem("w3_loaded"), sem("w2_loaded")

        block = ctx.enter_context(nc.Block())

        @block.sync
        def _(sp):
            sp.dma_start(x[:, :, :], A["L0_attn_hidden_states"].rearrange("b (t p) d -> p (b t) d", p=P)).then_inc(x_loaded, 16)
            sp.dma_start(wk[:, :], A["L0_attn_wk"]).then_inc(weights_loaded, 16)
            sp.dma_start(wv[:, :], A["L0_attn_wv"]).then_inc(weights_loaded, 16)
            sp.dma_start(wq[:, :], A["L0_attn_wq"]).then_inc(weights_loaded, 16)
            sp.dma_start(wo[:, :, :], A["L0_attn_wo"].rearrange("(a q) n -> q a n", q=P)).then_inc(weights_loaded, 16)
            for hh in range(2):
                src = A["L0_attn_W1"].rearrange("(a h) c d -> h c a d", h=2)[hh]
                sp.dma_start(W1s[hh * 64:hh * 64 + 64, :, :], src).then_inc(weights_loaded, 16)
            sp.wait_ge(zeros_ready, 1)
            for r in (0, 32):
                sp.dma_start(gb2[r:r + 1, 0, :], A["L0_attn_gamma"].rearrange("h a d -> a (h d)")).then_inc(small_loaded, 16)
                sp.dma_start(gb2[r:r + 1, 1, :], A["L0_attn_beta"].rearrange("h a d -> a (h d)")).then_inc(small_loaded, 16)
            for n in range(2):
                sp.dma_start(Bst[:, n, :], A["L0_attn_b1"].rearrange("h a d -> a (h d)").broadcast_to([2, D])).then_inc(small_loaded, 16)
            sp.dma_start(wg0[:, :], A["L0_ffn_Wg"]).then_inc(moe_loaded, 16)
            for b in range(B):
                sp.dma_start(bg0[b * E0:(b + 1) * E0, :], A["L0_ffn_bg"].rearrange("(e o) -> e o", o=1)).then_inc(moe_loaded, 16)
            for n in range(3):
                if n < 2:
                    sp.dma_start(ew[n][:, :, :], A[f"L0_ffn_w{n + 1}"].rearrange("e d o -> d e o")).then_inc(moe_loaded, 16)
                sp.dma_start(eb[:, n, :], A[f"L0_ffn_b{n + 1}"].rearrange("e o -> o e").broadcast_to([P, E0])).then_inc(moe_loaded, 16)
            for n, name in enumerate(("Wq", "Wk", "Wv", "Wo")):
                sp.dma_start(w4[:, n, :], A["L1_attn_" + name]).then_inc(l2_loaded, 16)
            sp.dma_start(b1r[:, :], A["L1_ffn_b1"].rearrange("e (a q) -> (e a) q", q=P)).then_inc(l2_loaded, 16)
            sp.dma_start(b2r[:, :], A["L1_ffn_b2"]).then_inc(l2_loaded, 16)
            sp.dma_start(boB[:, :], A["L1_attn_bo"].rearrange("(a q) -> a q", a=1).broadcast_to([P, P])).then_inc(l2_loaded, 16)
            sp.dma_start(Wg1[:, :, :], A["L1_ffn_Wg"].rearrange("r h e -> h r e")).then_inc(l2_loaded, 16)
            sp.dma_start(bgB[:, :, :].rearrange("p r e -> p (r e)"), A["L1_ffn_bg"].rearrange("(a r) e -> a (r e)", a=1).broadcast_to([P, R1 * E1])).then_inc(l2_loaded, 16)
            sp.wait_ge(CHUNK["att_taken"], 2 * NC)
            sp.dma_start(ew[2], A["L0_ffn_w3"].rearrange("e d o -> d e o")).then_inc(w3_loaded, 16)
            sp.wait_ge(x1_ready, B)
            sp.dma_start(W1r[:, :, :], A["L1_ffn_W1"].rearrange("e h f -> h e f")).then_inc(w1_loaded, 16)
            sp.dma_start(W2[:, :, :, :], A["L1_ffn_W2"].rearrange("e (a q) h -> q e a h", q=P)).then_inc(w2_loaded, 16)
            out_v = out.rearrange("b (t p) d -> p b t d", p=P)
            with sp.Fori(0, B) as i:
                sp.wait_ge(ROUND["result_ready"], i + 1)
                sp.dma_start(out_v[:, bass.ds(i, 1), :, :].rearrange("p o t d -> p (o t) d"), fin[:, :, :]).then_inc(ROUND["result_stored"], 16)
            sp.wait_ge(ROUND["result_stored"], 16 * B)

        N_W, N_S, N_M = 6, 2 + 4 + 2 + 8, 5 + 5

        def quads(i, r):
            live, before = not (isinstance(i, int) and i == B), not (isinstance(i, int) and i == 0)
            return live, (before if r == 0 else live), (before if r <= 1 else live)

        def counted(n):
            return not isinstance(n, int) or n > 0

        N_2 = 9

        SCORES = {2: 1, 3: 1, 4: 1, 5: 1, 6: 1, 7: 1, 8: 1, 10: 1, 12: 1, 14: 1, 16: 1, 17: 1, 18: 1, 19: 1, 20: 1, 21: 1}

        @block.scalar
        def _(act):
            act.dma_start(cst[:, :], const_d).then_inc(consts_loaded, 16)
            g = A["L0_attn_gamma"].rearrange("h a d -> a (h d)")
            act.dma_start(gamB[:, :], g.broadcast_to([P, D])).then_inc(small_loaded, 16)
            act.dma_start(th[:, :], A["L0_attn_theta"].rearrange("h d a -> a (h d)").broadcast_to([P, D])).then_inc(small_loaded, 16)
            for hh in range(2):
                gr = A["L0_attn_gamma"].rearrange("(a h) o d -> h o a d", h=2)[hh]
                br = A["L0_attn_beta"].rearrange("(a h) o d -> h o a d", h=2)[hh]
                act.dma_start(gam[hh * 64:hh * 64 + 64, :], gr[0].rearrange("a d -> d a"), allow_slow_non_contiguous=True).then_inc(small_loaded, 16)
                act.dma_start(bet[hh * 64:hh * 64 + 64, :], br[0].rearrange("a d -> d a"), allow_slow_non_contiguous=True).then_inc(small_loaded, 16)
                tr = A["L0_attn_theta_bias"].rearrange("h o d -> o (h d)")
                act.dma_start(tb[hh * 64:hh * 64 + 64, :], tr.broadcast_to([64, H])).then_inc(small_loaded, 16)
                act.dma_start(alpha[hh * 64:hh * 64 + 64, :], A["L0_attn_alpha"].rearrange("(k o) -> k o", o=1)).then_inc(small_loaded, 16)
            act.wait_ge(norm_step, 1)
            act.activation(xsq[:, :, :], xn[:, :, :], ACT.Square).then_inc(squares_ready, 1)
            act.wait_ge(norm_step, 2)
            act.wait_ge(consts_loaded, 16)
            act.activation(st[:, 2, :], st[:, 1, :], ACT.Sqrt, bias=C("ln_eps"), scale=1.0 / P).then_inc(dev_ready, 1)
            for n in range(4):
                act.wait_ge(xn_turned, n + 1)
                act.activation(xnT[:, n * 512:(n + 1) * 512], bank[n][:, :], ACT.Copy).then_inc(xn_turned_taken, 1)
            act.wait_ge(xn_turned_taken, 4)
            act.activation(xch[:, :].rearrange("p (b c) -> p b c", b=B), xnT[:, :].rearrange("p (b s) -> p b s", b=B)[:, :, 0:K], ACT.Copy).then_inc(CHUNK["tokens_high"], 1)
            def evac(dst, m, n):
                act.wait_ge(CHUNK["proj_ready"], n)
                act.activation(dst, bank[2 + m % 2][:, :], ACT.Copy).then_inc(CHUNK["proj_taken"], 1)

            def tokens_of(i):
                act.activation(xch[:, :].rearrange("p (b c) -> p b c", b=B), xnT[:, :].rearrange("p (b s) -> p b s", b=B)[:, :, bass.ds(i * K, K)],
                               ACT.Copy).then_inc(CHUNK["tokens_high"], 1)

            def keys(n):
                for m in range(4):
                    evac(kT[:, 2 * m:2 * m + 2, :, :].rearrange("p a b c -> p (a b c)"), m, n + m + 1)

            keys(0)
            act.wait_ge(prep_pe, 1)
            for n in range(2):
                act.activation(wqT[:, 4 * n:4 * n + 4, :], bank[5 + n][:, :], ACT.Copy).then_inc(prep_act, 1)
            act.wait_ge(prep_pe, 2)
            act.activation(Wqo[:, :], bank[7][:, 0:P], ACT.Copy).then_inc(prep_act, 1)
            act.activation(bo0[:, :], bank[7][:, P:P + 1], ACT.Copy).then_inc(prep_act, 1)
            act.wait_ge(rates_biased, 1)
            act.activation(eta[:, :, :, :], eta[:, :, :, :], ACT.Sigmoid).then_inc(rates_sigmoid, 1)
            def chunk(i, live=True, before=True, more=True):
                j = i - 1

                def sqz_(u):
                    if live:
                        act.wait_ge(CHUNK["z_ready"], 4 * i + u + 1)
                        act.activation(sqz[:, u % 2, :], bank[u % 2][:, :], ACT.Square).then_inc(CHUNK["z_squared"], 1)

                def xku(u):
                    if live:
                        if u == 0 and before:
                            act.wait_ge(CHUNK["dw_ready"], 4 * i)
                        evac(XK[:, u, :], 0, 16 * i + 4 + 2 * u + 1)
                        evac(U[:, u, :], 1, 16 * i + 4 + 2 * u + 2)
                    if not before and u == 2:
                        act.wait_ge(choice_step, 2)
                        act.activation(rkp[:, 1, :], lgt[:, :], ACT.Exp, bias=es[:, 0:1], accum_out=es[:, 1:2]).then_inc(choice_exp, 1)

                def std(u):
                    if live:
                        act.wait_ge(CHUNK["z_sumsq"], 4 * i + u + 1)
                        act.activation(sm[:, u, 1, :], sm[:, u, 0, :], ACT.Sqrt, bias=C("ttt_eps"), scale=1.0 / HD).then_inc(CHUNK["z_dev"], 1)

                def zqs(u):
                    if before:
                        act.wait_ge(CHUNK["zq_ready"], 4 * j + u + 1)
                        if not live and u >= 2:
                            act.wait_ge(CHUNK["zq_sumsq"], 4 * j + u - 1)
                        act.activation(sq2[:, u % 2, :], bank[6 if live else u][:, :], ACT.Square).then_inc(CHUNK["zq_squared"], 1)

                def stdq(u):
                    if before:
                        act.wait_ge(CHUNK["zq_sumsq"], 4 * j + u + 1)
                        act.activation(rq[:, u, 1, :], rq[:, u, 0, :], ACT.Sqrt, bias=C("ttt_eps"), scale=1.0 / HD).then_inc(CHUNK["zq_dev"], 1)

                def turned(u):
                    if before:
                        act.wait_ge(CHUNK["normed_turned"], 4 * j + u + 1)
                        act.activation(AT[:, u % 2, :], bank[7][:, :], ACT.Copy).then_inc(CHUNK["turned_taken"], 1)

                def att(g):
                    if before:
                        act.wait_ge(CHUNK["att_ready"], 2 * j + g + 1)
                        act.activation(attnT[:, :].rearrange("p (b s) -> p b s", b=B)[:, 2 * g:2 * g + 2, bass.ds(j * K, K)],
                                       bank[7][:, 0:P].rearrange("p (b s) -> p b s", b=2), ACT.Identity, bias=bo0[:, :]).then_inc(CHUNK["att_taken"], 1)

                if not live:
                    zqs(0), stdq(0), zqs(1), stdq(1), zqs(2), stdq(2), zqs(3), stdq(3), turned(0), turned(1), att(0), turned(2), turned(3), att(1)
                    return
                sqz_(0), std(0), sqz_(1), std(1), xku(0), zqs(0), sqz_(2), stdq(0), std(2), xku(1), zqs(1), sqz_(3), stdq(1), std(3)
                xku(2), turned(0), zqs(2), stdq(2), xku(3), turned(1), att(0), zqs(3)
                if live:
                    for m in range(4):
                        if m == 2:
                            stdq(3)
                        evac(qT[:, 2 * m:2 * m + 2, :, :].rearrange("p a b c -> p (a b c)"), m, 16 * i + 12 + m + 1)
                turned(2)
                if more:
                    tokens_of(i + 1)
                turned(3), att(1)
                if not before:
                    act.wait_ge(ranks_turned, 1)
                    act.activation(rpT[:, :, :, :], bank[7][:, :].rearrange("p (k t r) -> p k t r", k=2, t=NT), ACT.Copy).then_inc(ranks_taken, 1)
                if more:
                    keys(16 * i + 16)

            chunk(0, before=False)
            with act.Fori(1, NC - 1) as i:
                chunk(i)
            chunk(NC - 1, more=False)
            chunk(NC, live=False, more=False)

            n = 0
            for b in range(B):
                act.wait_ge(job_done, n + 1)
                act.activation(tokT[:, b, :, :], bank[n % 4][:, :].rearrange("p (e k) -> p e k", e=E0), ACT.Copy).then_inc(job_taken, 1)
                n += 1
                for g in range(E0 // 4):
                    act.wait_ge(job_done, n + 1)
                    act.activation(WPT[:, b, g, :], bank[n % 4][:, :], ACT.Copy).then_inc(job_taken, 1)
                    n += 1
            for k, h in enumerate((h1, h2)):
                for g in range(E0 // 4):
                    act.wait_ge(job_done, n + 1)
                    for j in range(4):
                        last = act.activation(h[:, 4 * g + j, :], bank[n % 4][:, j * P:(j + 1) * P], ACT.Relu, bias=eb[:, k, 4 * g + j:4 * g + j + 1])
                    last.then_inc(job_taken, 1)
                    n += 1
            for g in range(E0 // 4):
                act.wait_ge(job_done, n + 1)
                act.activation(o3[:, g, :, :], bank[n % 4][:, :].rearrange("p (b d) -> p b d", b=B), ACT.Identity, bias=b3s[:, g:g + 1]).then_inc(job_taken, 1)
                n += 1


            for b in range(B):
                act.wait_ge(l2_norm_step, b + 1)
                act.activation(sq_2[:, b * NT:(b + 1) * NT, :], x2[:, b * NT:(b + 1) * NT, :], ACT.Square).then_inc(l2_squares, 1)
            act.wait_ge(l2_sumsq, B)
            act.activation(st2[:, 2, :], st2[:, 1, :], ACT.Sqrt, bias=C("ln_eps"), scale=1.0 / P).then_inc(l2_squares, 1)
            act.wait_ge(l2_w_turned, 1)
            act.activation(wT4[:, :, :], bank[0][:, :].rearrange("p (n c) -> p n c", n=4), ACT.Copy).then_inc(l2_w_taken, 1)
            act.activation(b1c[:, :], bank[1][:, 0:E1 * NF], ACT.Copy).then_inc(l2_w_taken, 1)
            for b in range(B):
                act.wait_ge(xn2_turned, b + 1)
                act.activation(xn2T[:, b * S:(b + 1) * S], bank[2 + b][:, :], ACT.Copy).then_inc(xn2_turned_taken, 1)
            act.wait_ge(xn2_turned_taken, B)

            def round_(i, r):
                live, has1, has2 = quads(i, r)

                def part(k):
                    act.wait_ge(ROUND["rows_ready"], 12 * i + 3 * r + k)
                    n = (3 * r + k + 1) % 2
                    if k == 1:
                        last = act.activation(hi[:, n, :], bank[5][:, :], ACT.Identity, bias=C("k_ones"))
                    else:
                        last = act.activation(hi[:, n, :], bank[5][:, :], ACT.Copy)
                    last.then_inc(ROUND["rows_high"], 1)

                def exps(n):
                    act.wait_ge(ROUND["turned_ready"], 64 * i + 16 * r - 16 + n + 1)
                    if counted(64 * i + 16 * r - 16 + n - 7):
                        act.wait_ge(ROUND["values_summed"], 64 * i + 16 * r - 16 + n - 7)
                    act.activation(ex[:, n % 8, :], bank[n % 2][:, :], ACT.Exp, scale=float(AD) ** -0.5).then_inc(ROUND["exps_ready"], 1)

                def gelu(n):
                    act.wait_ge(ROUND["hidden_ready"], 64 * i + 16 * r + n + 1)
                    if counted(64 * i + 16 * r + n - 7):
                        act.wait_ge(ROUND["outputs_ready"], 64 * i + 16 * r + n - 7)
                    act.activation(hd[:, n % 8, :], bank[n % 2][:, :], ACT.Gelu_apprx_tanh, bias=b1c[:, n:n + 1]).then_inc(ROUND["gelu_ready"], 1)

                if has2:
                    act.wait_ge(ROUND["values_summed"], 64 * i + 16 * r - 16)
                    act.activation(ob[:, :], bank[6][:, :], ACT.Copy).then_inc(ROUND["heads_taken"], 1)
                if live and r:
                    act.wait_ge(ROUND["cur_turned"], 3 * i + r)
                    act.activation(curT[:, :], bank[7][:, :], ACT.Copy).then_inc(ROUND["cur_taken"], 1)
                elif live:
                    act.activation(curT[:, :], xn2T[:, bass.ds(i * S, S)], ACT.Copy).then_inc(ROUND["cur_taken"], 1)
                if has1:
                    part(0)
                for n in range(8 if live else 0):
                    gelu(n)
                    if n == 2:
                        part(1)
                    if n == 5:
                        part(2)
                if live:
                    act.wait_ge(ROUND["logits_shifted"], 4 * i + r + 1)
                    act.activation(gt[:, 1, :], gt[:, 0, :], ACT.Exp).then_inc(ROUND["gate_exp"], 1)
                for n in range(8):
                    if has1:
                        exps(n)
                    if n == 3 and live:
                        act.wait_ge(ROUND["gates_turned"], 4 * i + r + 1)
                        act.activation(cwT[:, :], bank[7][0:E1, :], ACT.Copy).then_inc(ROUND["gates_taken"], 1)
                for n in range(8, 16):
                    if live:
                        gelu(n)
                    if n == 10 and r == 1 and has2:
                        act.wait_ge(ROUND["att_turned"], i)
                        act.activation(aT[:, :], bank[7][:, :], ACT.Copy).then_inc(ROUND["att_turned_taken"], 1)
                for n in range(8, 16 if has1 else 8):
                    exps(n)

            for r in range(R1):
                round_(0, r)
            with act.Fori(1, B) as i:
                for r in range(R1):
                    round_(i, r)
            for r in range(2):
                round_(B, r)

        @block.vector
        def _(dve):
            n = [0]

            def link(ins):
                n[0] += 1
                ins.then_inc(v_step, 1)
                dve.wait_ge(v_step, n[0])

            dve.wait_ge(x_loaded, 16)
            bc = lambda t: t.unsqueeze(2).broadcast_to([P, B * NT, P])
            link(dve.tensor_reduce(st[:, 0, :], x[:, :, :], AX_X, ALU.add))
            link(dve.tensor_scalar(st[:, 3, :], st[:, 0, :], 1.0 / P, None, ALU.mult))
            dve.tensor_tensor(xn[:, :, :], x[:, :, :], bc(st[:, 3, :]), ALU.subtract).then_inc(norm_step, 1)
            dve.memset(wrk[:, 1, :], 1.0)
            link(dve.memset(wgP[:, :, :], 0.0))
            dve.wait_ge(squares_ready, 1)
            dve.tensor_reduce(st[:, 1, :], xsq[:, :, :], AX_X, ALU.add).then_inc(norm_step, 1)
            dve.wait_ge(dev_ready, 1)
            link(dve.reciprocal(st[:, 3, :], st[:, 2, :]))
            for b in range(B):
                dve.tensor_tensor(xn[:, b * NT:(b + 1) * NT, :], xn[:, b * NT:(b + 1) * NT, :],
                                  st[:, 3, b * NT:(b + 1) * NT].unsqueeze(2).broadcast_to([P, NT, P]), ALU.mult).then_inc(norm_step, 1)
            dve.wait_ge(weights_loaded, 16 * N_W)
            dve.tensor_copy(wkh[:, :], wk[:, :])
            link(dve.tensor_copy(wqh[:, :], wq[:, :]))
            dve.tensor_tensor(wkl[:, :], wk[:, :], wkh[:, :], ALU.subtract).then_inc(prep_dve, 1)
            dve.wait_ge(CHUNK["tokens_high"], 1)
            dve.tensor_tensor(xcl[:, :].rearrange("p (b c) -> p b c", b=B), xnT[:, :].rearrange("p (b s) -> p b s", b=B)[:, :, 0:K],
                              xch[:, :].rearrange("p (b c) -> p b c", b=B), ALU.subtract).then_inc(CHUNK["tokens_low"], 1)
            dve.wait_ge(moe_loaded, 16 * N_M)
            for b in range(B):
                last = dve.tensor_copy(wgP[:, b, b * E0:(b + 1) * E0], wg0[:, :])
            last.then_inc(wg_ready, 1)
            for j in range(4):
                r = slice(32 * j, 32 * j + 32)
                dve.tensor_copy(b3s[r, :], eb[r, 2, :].rearrange("p (g j) -> p j g", j=4)[:, j, :])
            link(dve.tensor_reduce(m0[:, 0, 0:NP], W1s[:, :, :], AX_X, ALU.add))
            dve.tensor_scalar(m0[:, 1, 0:NP], m0[:, 0, 0:NP], 1.0 / HD, None, ALU.mult).then_inc(w_mean_ready, 1)
            dve.wait_ge(small_loaded, 16 * N_S)
            link(dve.tensor_tensor(th[:, :], th[:, :], wk[:, :], ALU.mult))
            dve.tensor_reduce(Th[:, :], th[:, :].rearrange("p (h c) -> p h c", h=H), AX_X, ALU.add).then_inc(prep_dve, 1)
            b0 = Bst[:, :, :].rearrange("p g (h c) -> p (g h) c", h=H)
            link(dve.tensor_reduce(mb[:, 0, :], b0, AX_X, ALU.add))
            link(dve.tensor_scalar(mb[:, 1, :], mb[:, 0, :], 1.0 / HD, None, ALU.mult))
            dve.tensor_tensor(b0, b0, mb[:, 1, :].unsqueeze(2).broadcast_to([2, 2 * H, HD]), ALU.subtract).then_inc(state_ready, 1)
            dve.wait_ge(zeros_ready, 2)
            dve.wait_ge(w_mean_ready, 1)
            for b in range(B):
                dve.tensor_tensor(Wbd[0:64, b, :, 0:64], W1s[0:64, :, :], m0[0:64, 1, 0:NP].unsqueeze(2).broadcast_to([64, NP, HD]),
                                  ALU.subtract).then_inc(state_ready, 1)
            link(dve.tensor_tensor(wu[:, :], wk[:, :], wv[:, :], ALU.subtract))
            link(dve.tensor_tensor(wu[:, :], wu[:, :], gamB[:, :], ALU.mult))
            link(dve.tensor_copy(wuh[:, :], wu[:, :]))
            dve.tensor_tensor(wul[:, :], wu[:, :], wuh[:, :], ALU.subtract)
            link(dve.tensor_scalar(ones[:, :], ident[0:64, :], 0.0, 1.0, ALU.mult, ALU.add))
            link(dve.tensor_tensor(gb2[:, 0, :], gb2[:, 0, :], gb2[:, 1, :], ALU.mult))
            link(dve.tensor_copy(gbr[:, :], gb2[:, 0, :]))
            dve.tensor_tensor(gbr[32:33, :], gb2[32:33, 0, :], gbr[32:33, :], ALU.subtract).then_inc(prep_dve, 1)
            link(dve.tensor_scalar(rate[:, :], alpha[:, :], C("token_rate"), 0.0, ALU.add, ALU.max))
            link(dve.tensor_scalar(rate[:, :], rate[:, :], 1.0 / HD, None, ALU.mult))
            dve.wait_ge(rates_raw, 1)
            dve.tensor_tensor(eta[:, :, :, :].rearrange("p i g h -> p (i g) h"), bank[4][:, 0:NC * 2 * H].rearrange("p (i h) -> p i h", h=H),
                              tb[:, :].unsqueeze(1).broadcast_to([P, NC * 2, H]), ALU.add).then_inc(rates_biased, 1)
            dve.tensor_tensor(wql[:, :], wq[:, :], wqh[:, :], ALU.subtract).then_inc(prep_dve, 1)
            dve.wait_ge(rates_sigmoid, 1)
            dve.tensor_scalar(eta[:, :, :, :], eta[:, :, :, :], rate[:, :], None, ALU.mult).then_inc(eta_ready, 1)
            dve.wait_ge(eta_ready, 1)

            def choice(step):
                if step == 0:
                    dve.wait_ge(choice_logits, 1)
                    dve.tensor_scalar(lgt[:, :], bank[7][0:BE, :], bg0[:, :], None, ALU.add).then_inc(choice_step, 1)
                    dve.wait_ge(choice_step, 1)
                elif step <= TOP0 // 8:
                    k = step - 1
                    left = lgt[:, :] if k == 0 else wrk[:, 0, :]
                    link(dve.max(m8[:, k, :], left))
                    if k == 0:
                        dve.tensor_scalar(es[:, 0:1], m8[:, 0, 0:1], -1.0, None, ALU.mult).then_inc(choice_step, 1)
                    link(dve.match_replace(wrk[:, 0, :], m8[:, k, :], left, -3.0e38))
                elif step == 5:
                    dve.wait_ge(choice_exp, 1)
                    link(dve.tensor_tensor(wrk[:, 0, :], lgt[:, :], wrk[:, 0, :], ALU.not_equal))
                    link(dve.tensor_tensor_scan(lgt[:, :], wrk[:, 1, :], wrk[:, 0, :], 0.0, ALU.mult, ALU.add))
                else:
                    dve.tensor_tensor(rkp[:, 0, :], lgt[:, :], wrk[:, 0, :], ALU.mult).then_inc(ranks_ready, 1)
                    link(dve.reciprocal(es[:, 2:3], es[:, 1:2]))
                    dve.tensor_scalar(rkp[:, 1, :], rkp[:, 1, :], es[:, 2:3], None, ALU.mult).then_inc(ranks_ready, 1)

            g3 = lambda t: t.rearrange("p (h c) -> p h c", h=8)
            per = lambda t: t.unsqueeze(2).broadcast_to([P, 8, HD])

            def chunk(i, live=True, before=True, more=True):
                j = i - 1

                def Xa(u):
                    if live:
                        dve.wait_ge(CHUNK["z_squared"], 4 * i + u + 1)
                        dve.tensor_reduce(sm[:, u, 0, :], g3(sqz[:, u % 2, :]), AX_X, ALU.add).then_inc(CHUNK["z_sumsq"], 1)

                def Xb(u):
                    if live:
                        n = 4 * i + u + 1
                        dve.wait_ge(CHUNK["z_dev"], n)
                        dve.reciprocal(sm[:, u, 2, :], sm[:, u, 1, :]).then_inc(CHUNK["z_rdev"], 1)
                        dve.wait_ge(CHUNK["z_rdev"], n)
                        dve.tensor_tensor(g3(xh[:, u, :]), g3(bank[u % 2][:, :]), per(sm[:, u, 2, :]), ALU.mult).then_inc(CHUNK["xhat_ready"], 1)

                def G(u):
                    if live:
                        n = 4 * i + u + 1
                        dve.wait_ge(CHUNK["scaled_ready"], n)
                        dve.wait_ge(CHUNK["proj_taken"], 16 * i + 4 + 2 * u + 2)
                        dve.tensor_tensor(gx[:, u, :], t1[:, u, :], U[:, u, :], ALU.add).then_inc(CHUNK["gx_ready"], 1)
                        rates = eta[:, bass.ds(i, 1), u // 2, :].rearrange("p o h -> p (o h)")[:, 8 * (u % 2):8 * (u % 2) + 8]
                        dve.tensor_tensor(sm[:, u, 3, :], rates, sm[:, u, 2, :], ALU.mult).then_inc(CHUNK["rate_ready"], 1)
                        dve.wait_ge(CHUNK["gx_ready"], n)
                        dve.tensor_reduce(sm[:, u, 4, :], g3(gx[:, u, :]), AX_X, ALU.add).then_inc(CHUNK["gx_centred"], 1)
                        dve.wait_ge(CHUNK["gx_centred"], 12 * i + 3 * u + 1)
                        dve.tensor_scalar(sm[:, u, 5, :], sm[:, u, 4, :], 1.0 / HD, None, ALU.mult).then_inc(CHUNK["gx_centred"], 1)
                        dve.wait_ge(CHUNK["gx_centred"], 12 * i + 3 * u + 2)
                        dve.tensor_tensor(g3(gw[:, u, :]), g3(gx[:, u, :]), per(sm[:, u, 5, :]), ALU.subtract).then_inc(CHUNK["gx_centred"], 1)

                def R(u):
                    if live:
                        n = 4 * i + u + 1
                        dve.wait_ge(CHUNK["gx_xhat"], n)
                        dve.tensor_reduce(sm[:, u, 6, :], g3(t1[:, u, :]), AX_X, ALU.add).then_inc(CHUNK["gx_xhat_sum"], 1)
                        dve.wait_ge(CHUNK["gx_xhat_sum"], n)
                        dve.tensor_scalar(sm[:, u, 4, :], sm[:, u, 6, :], 1.0 / HD, None, ALU.mult).then_inc(CHUNK["gx_xhat_mean"], 1)

                def Wd(u):
                    if live:
                        dve.wait_ge(CHUNK["xhat_part"], 4 * i + u + 1)
                        dve.wait_ge(CHUNK["gx_centred"], 12 * i + 3 * u + 3)
                        dve.tensor_tensor(gw[:, u, :], gw[:, u, :], t1[:, u, :], ALU.subtract).then_inc(CHUNK["grad_less"], 1)

                def up(u):
                    if live:
                        g, hf = u // 2, u % 2
                        dve.wait_ge(CHUNK["dw_ready"], 4 * i + u + 1)
                        for k in range(2):
                            for hh in range(2):
                                r = slice(64 * hh, 64 * hh + 64)
                                st_ = Wbd[r, 2 * g + k, 4 * hf:4 * hf + 4, r]
                                dve.tensor_tensor(st_, st_, bank[(4, 0)[u % 2] + k][r, :].rearrange("p (a c) -> p a c", a=4)[:, :, r], ALU.subtract)
                        bb = Bst[:, g, 512 * hf:512 * hf + 512]
                        dve.tensor_tensor(bb, bb, bank[6 + u % 2][0:2, :], ALU.subtract).then_inc(CHUNK["state_updated"], 1)

                def Qa(u):
                    if before:
                        dve.wait_ge(CHUNK["zq_squared"], 4 * j + u + 1)
                        dve.tensor_reduce(rq[:, u, 0, :], g3(sq2[:, u % 2, :]), AX_X, ALU.add).then_inc(CHUNK["zq_sumsq"], 1)

                def Qb(u):
                    if before:
                        dve.wait_ge(CHUNK["zq_dev"], 4 * j + u + 1)
                        dve.reciprocal(rq[:, u, 2, :], rq[:, u, 1, :]).then_inc(CHUNK["zq_rdev"], 1)
                        dve.wait_ge(CHUNK["zq_rdev"], 4 * j + u + 1)
                        if not live and u >= 2:
                            dve.wait_ge(CHUNK["normed_turned"], 4 * j + u - 1)
                        dve.tensor_tensor(g3(Am[:, u % 2, :]), g3(bank[6 if live else u][:, :]), per(rq[:, u, 2, :]), ALU.mult).then_inc(CHUNK["normed_ready"], 1)

                if not live:
                    Qa(0), Qb(0), Qa(1), Qb(1), Qa(2), Qa(3), Qb(2), Qb(3)
                    return
                step = (lambda n: None) if before else choice
                Xa(0), Xb(0), Xa(1), Xb(1), step(0), step(1), G(0), Qa(0), Xa(2), Qb(0), Xb(2), step(2), Qa(1), G(1), Xa(3), Qb(1), Xb(3)
                step(3), R(0), Qa(2), G(2), step(4), R(1), Qb(2), Wd(0), Qa(3), G(3), Qb(3), step(5), step(6)
                if more:
                    dve.wait_ge(CHUNK["tokens_high"], i + 2)
                    dve.tensor_tensor(xcl[:, :].rearrange("p (b c) -> p b c", b=B), xnT[:, :].rearrange("p (b s) -> p b s", b=B)[:, :, bass.ds((i + 1) * K, K)],
                                      xch[:, :].rearrange("p (b c) -> p b c", b=B), ALU.subtract).then_inc(CHUNK["tokens_low"], 1)
                R(2), Wd(1), R(3), up(0), Wd(2), Wd(3), up(1), up(2), up(3)

            chunk(0, before=False)
            with dve.Fori(1, NC - 1) as i:
                chunk(i)
            chunk(NC - 1, more=False)
            chunk(NC, live=False, more=False)
            for b in range(B):
                if b >= 2:
                    dve.wait_ge(job_done, 5 * (b - 2) + 1)
                for t in range(NT):
                    last = dve.tensor_tensor(OH[:, b % 2, t, :].rearrange("p (e k) -> p e k", e=E0),
                                             rpT[:, 0, t, b * E0:(b + 1) * E0].unsqueeze(2).broadcast_to([P, E0, TOP0]),
                                             C("slots").unsqueeze(1).broadcast_to([P, E0, TOP0]), ALU.is_equal)
                last.then_inc(onehot_ready, 1)
                dve.wait_ge(onehot_ready, b + 1)
                if b:
                    dve.wait_ge(job_done, 5 * b)
                for t in range(NT):
                    last = dve.tensor_tensor(WP[:, t, :].rearrange("p (e k) -> p e k", e=E0), OH[:, b % 2, t, :].rearrange("p (e k) -> p e k", e=E0),
                                             rpT[:, 1, t, b * E0:(b + 1) * E0].unsqueeze(2).broadcast_to([P, E0, TOP0]), ALU.mult)
                last.then_inc(weighted_ready, 1)
            dve.wait_ge(l2_loaded, 16 * N_2)
            tok = lambda t: t.unsqueeze(2).broadcast_to([P, NT, P])
            for b in range(B + 1):
                if b < B:
                    t4 = slice(b * NT, (b + 1) * NT)
                    dve.wait_ge(scattered, b + 1)
                    dve.tensor_tensor(x1[:, t4, :], bank[4 + b][:, :].rearrange("p (t d) -> p t d", t=NT), x[:, t4, :], ALU.add).then_inc(x1_ready, 1)
                    dve.wait_ge(x1_ready, b + 1)
                    link(dve.tensor_reduce(st2[:, 0, t4], x1[:, t4, :], AX_X, ALU.add))
                    link(dve.tensor_scalar(st2[:, 3, t4], st2[:, 0, t4], 1.0 / P, None, ALU.mult))
                    dve.tensor_tensor(x2[:, t4, :], x1[:, t4, :], tok(st2[:, 3, t4]), ALU.subtract).then_inc(l2_norm_step, 1)
                if b:
                    dve.wait_ge(l2_squares, b)
                    dve.tensor_reduce(st2[:, 1, (b - 1) * NT:b * NT], sq_2[:, (b - 1) * NT:b * NT, :], AX_X, ALU.add).then_inc(l2_sumsq, 1)
            dve.wait_ge(l2_squares, B + 1)
            link(dve.reciprocal(st2[:, 3, :], st2[:, 2, :]))
            for b in range(B):
                t4 = slice(b * NT, (b + 1) * NT)
                dve.tensor_tensor(xn2[:, t4, :], x2[:, t4, :], tok(st2[:, 3, t4]), ALU.mult).then_inc(l2_norm_step, 1)
            dve.wait_ge(w1_loaded, 16)
            dve.tensor_copy(W1h[:, :, :], W1r[:, :, :]).then_inc(l2_w_split, 1)
            dve.wait_ge(l2_pool_step, 3)
            dve.wait_ge(l2_w_taken, 2)
            for k in range(2):
                last = dve.tensor_copy(wr[:, k, :, :].rearrange("p q (j c) -> p (q j) c", c=32)[:, :, 0:24].rearrange("p h (c d) -> p h c d", d=AD),
                                       wT4[:, k, :].rearrange("p (h d) -> p h d", d=AD).unsqueeze(2).broadcast_to([P, AH, 3, AD]))
            link(last)
            link(dve.tensor_copy(wrh[:, :, :, :], wr[:, :, :, :]))
            dve.tensor_tensor(wrl[:, :, :, :], wr[:, :, :, :], wrh[:, :, :, :], ALU.subtract).then_inc(l2_w_split, 1)
            dve.memset(Vx[:, :, :, AD:AD + 1], 1.0).then_inc(l2_w_split, 1)
            dve.wait_ge(l2_w_split, 3)
            dve.wait_ge(l2_pool_step, 4)

            n1 = [0]

            def round_(i, r):
                live, has1, has2 = quads(i, r)
                at = V1 * i + V0 - V1 if not isinstance(i, int) else V0 * min(i, 1) + V1 * max(i - 1, 0)

                def link(ins):
                    n1[0] += 1
                    ins.then_inc(ROUND["own_step"], 1)
                    dve.wait_ge(ROUND["own_step"], at + n1[0])

                def part(k):
                    n = 12 * i + 3 * r + k
                    dve.wait_ge(ROUND["rows_high"], n)
                    h = hi[:, (3 * r + k + 1) % 2, :]
                    if k == 1:
                        dve.scalar_tensor_tensor(out=kx[:, r % 2, :], in0=h, scalar=C("k_minus"), in1=bank[5][:, :], op0=ALU.mult, op1=ALU.add).then_inc(ROUND["rows_taken"], 1)
                        return
                    if counted(8 * i + 2 * r - 1 + k // 2):
                        dve.wait_ge(ROUND["q_masked"], 8 * i + 2 * r - 1 + k // 2)
                    dve.scalar_tensor_tensor(out=qf[:, :], in0=h, scalar=C("q_minus"), in1=bank[5][:, :], op0=ALU.mult, op1=ALU.add).then_inc(ROUND["rows_taken"], 1)
                    q = qx if k else qm
                    dve.wait_ge(ROUND["rows_taken"], n)
                    dve.tensor_scalar(q[:, 0, :], qf[:, :], C("even"), None, ALU.mult)
                    dve.tensor_scalar(q[:, 1, :], qf[:, :], C("odd"), None, ALU.mult).then_inc(ROUND["q_masked"], 1)

                def smax():
                    n = s1[0]
                    s1[0] += 1
                    t, h = n // QH, n % QH
                    dve.wait_ge(ROUND["scores_ready"], 64 * i + 16 * r + n + 1)
                    dve.tensor_reduce(Mt[:, t, 32 * h + 24:32 * h + 25], bank[3][:, :], AX_X, ALU.max, negate=True).then_inc(ROUND["score_max"], 1)

                def maxima():
                    dve.wait_ge(ROUND["score_max"], 64 * i + 16 * (r + 1))
                    m = Mt[:, :, :].rearrange("p t (h c) -> p t h c", c=32)
                    dve.tensor_copy(m[:, :, :, 25:26], m[:, :, :, 24:25]).then_inc(ROUND["maxima_ready"], 1)

                n_g = 4 * i + r + 1
                other = lg[:, :, :].unsqueeze(2).broadcast_to([P, NT, E1, E1])
                own = lg[:, :, :].unsqueeze(3).broadcast_to([P, NT, E1, E1])
                sq = lambda k: lgx[:, k, :, :].rearrange("p t (e f) -> p t e f", e=E1)
                g2 = lambda k: gt[:, k, :]
                g3_ = lambda k: gt[:, k, :].rearrange("p (t e) -> p t e", e=E1)
                one = lambda k: gt[:, k, 0:NT]
                per = lambda k: gt[:, k, 0:NT].unsqueeze(2).broadcast_to([P, NT, E1])

                def best():
                    dve.wait_ge(ROUND["logits_ready"], n_g)
                    b16 = bank[7][:, 0:NT * E1].rearrange("p (t e) -> p t e", e=E1)
                    dve.tensor_tensor(lg[:, :, :], b16, bgB[:, r, :].unsqueeze(1).broadcast_to([P, NT, E1]), ALU.add).then_inc(ROUND["logits_taken"], 1)
                    dve.wait_ge(ROUND["logits_taken"], n_g)
                    dve.tensor_tensor(sq(0), other, own, ALU.is_gt)
                    dve.tensor_tensor(sq(1), other, own, ALU.is_equal)
                    link(dve.tensor_reduce(one(2), lg[:, :, :], AX_X, ALU.max))
                    dve.tensor_tensor(g3_(0), lg[:, :, :], per(2), ALU.subtract).then_inc(ROUND["logits_shifted"], 1)
                    link(dve.tensor_tensor(lgx[:, 2, :, :], lgx[:, 1, :, :], C("lower").unsqueeze(1).broadcast_to([P, NT, E1 * E1]), ALU.mult))
                    link(dve.tensor_tensor(lgx[:, 1, :, :], lgx[:, 0, :, :], lgx[:, 2, :, :], ALU.add))
                    link(dve.tensor_reduce(g3_(3), sq(1), AX_X, ALU.add))
                    link(dve.tensor_scalar(g2(4), g2(3), 2.0, None, ALU.is_lt))

                def weigh():
                    dve.wait_ge(ROUND["gate_exp"], n_g)
                    link(dve.tensor_tensor(g2(5), g2(1), g2(4), ALU.mult))
                    link(dve.tensor_reduce(one(6), g3_(5), AX_X, ALU.add))
                    link(dve.reciprocal(one(7), one(6)))
                    dve.tensor_tensor(cw[:, :, :], g3_(5), per(7), ALU.mult).then_inc(ROUND["gates_ready"], 1)

                def bias():
                    dve.wait_ge(ROUND["bias_ready"], n_g)
                    dve.wait_ge(ROUND["cur_set"], i + 1)
                    if r:
                        dve.wait_ge(ROUND["expert_added"], 16 * i + 4 * r)
                    dve.tensor_tensor(cur[:, :, :], bank[7][:, :].rearrange("p (t d) -> p t d", t=NT), cur[:, :, :], ALU.add).then_inc(ROUND["bias_added"], 1)

                def expert(e):
                    dve.wait_ge(ROUND["outputs_ready"], 64 * i + 16 * r + 4 * e + 4)
                    dve.wait_ge(ROUND["bias_added"], n_g)
                    if e:
                        dve.wait_ge(ROUND["expert_added"], 16 * i + 4 * r + e)
                    for t in range(NT):
                        last = dve.scalar_tensor_tensor(out=cur[:, t, :], in0=bank[2 + 2 * (e % 2)][:, t * P:(t + 1) * P], scalar=cw[:, t, e:e + 1],
                                                        in1=cur[:, t, :], op0=ALU.mult, op1=ALU.add)
                    last.then_inc(ROUND["expert_added"], 1)

                def outputs():
                    j = (r - 2) % 4
                    dve.wait_ge(ROUND["heads_turned"], 4 * i + r - 1)
                    o4 = bank[7][:, :].rearrange("p (t h c) -> p t h c", t=NT, c=32)
                    link(dve.tensor_scalar(den[:, 0, :, :], o4[:, :, :, AD:AD + 1].rearrange("p t h o -> p t (h o)"), 1e-8, None, ALU.add))
                    link(dve.reciprocal(den[:, 1, :, :], den[:, 0, :, :]))
                    dve.tensor_tensor(an[:, :, j * 32:(j + 1) * 32].rearrange("p t (h d) -> p t h d", d=AD), o4[:, :, :, 0:AD],
                                      den[:, 1, :, :].unsqueeze(3).broadcast_to([P, NT, QH, AD]), ALU.mult).then_inc(ROUND["heads_divided"], 1)

                s1 = [0]
                if live:
                    dve.wait_ge(ROUND["cur_taken"], n_g)
                    link(dve.tensor_copy(cH[:, :], curT[:, :]))
                    dve.tensor_tensor(cL[:, :], curT[:, :], cH[:, :], ALU.subtract).then_inc(ROUND["cur_split"], 1)
                if has1:
                    part(0)
                if r == 0 and has1:
                    dve.wait_ge(ROUND["expert_added"], 16 * i)
                    if counted(16 * i - 16):
                        dve.wait_ge(ROUND["result_stored"], 16 * i - 16)
                    link(dve.tensor_tensor(fin[:, :, :], cur[:, :, :], boB[:, :].unsqueeze(1).broadcast_to([P, NT, P]), ALU.add))
                    link(dve.tensor_tensor(fin[:, :, :], fin[:, :, :], x1[:, bass.ds(i * NT - NT, NT), :], ALU.add))
                if r == 0 and live:
                    dve.tensor_copy(cur[:, :, :], xn2[:, bass.ds(i * NT, NT), :]).then_inc(ROUND["cur_set"], 1)
                    dve.wait_ge(ROUND["cur_split"], n_g)
                    dve.tensor_copy(xH[:, :], cH[:, :])
                    dve.tensor_copy(xL[:, :], cL[:, :]).then_inc(ROUND["xn_split"], 1)
                if live:
                    best()
                    part(1)
                if has2:
                    outputs()
                if live:
                    part(2)
                if r == 0 and live:
                    dve.wait_ge(ROUND["v_ready"], i + 1)
                    dve.tensor_copy(Vs[:, :, :], bank[7][:, :].rearrange("p (t d) -> p t d", t=NT)).then_inc(ROUND["v_taken"], 1)
                if r == 1 and live:
                    if counted(64 * i):
                        dve.wait_ge(ROUND["values_summed"], 64 * i)
                    dve.wait_ge(ROUND["v_taken"], i + 1)
                    dve.tensor_copy(Vx[:, :, :, 0:AD], Vs[:, :, :].rearrange("p t (h d) -> p t h d", d=AD)).then_inc(ROUND["v_spread"], 1)
                if live:
                    weigh()
                for n in range(24 if live else 0):
                    k = n if n < 8 else n - 8 if n >= 16 else None
                    if k == 5:
                        bias()
                        expert(0)
                    if k is not None and k % NF == 3 and k > 3:
                        expert(k // NF)
                    for _ in range(SCORES.get(n, 0)):
                        smax()
                    if n == 22:
                        maxima()
                    if n == 13 and r == 1 and has2:
                        result(i, link)
                if not live and r == 1:
                    result(i, link)

            def result(i, link):
                dve.wait_ge(ROUND["att_out"], i)
                dve.tensor_tensor(fin[:, :, :], bank[7][:, :].rearrange("p (t d) -> p t d", t=NT), fin[:, :, :], ALU.add).then_inc(ROUND["result_ready"], 1)

            V0, V1 = 4 * (1 + 5 + 3) + 2 * 2, 4 * (1 + 5 + 3) + 4 * 2 + 2
            for r in range(R1):
                round_(0, r)
            assert n1[0] == V0, n1[0]
            n1[0] = 0
            with dve.Fori(1, B) as i:
                for r in range(R1):
                    round_(i, r)
            assert n1[0] == V1, n1[0]
            n1[0] = 0
            for r in range(2):
                round_(B, r)

        @block.gpsimd
        def _(pool):
            pool.memset(gb2[:, :, :], 0.0).then_inc(zeros_ready, 1)
            pool.memset(Wbd[:, :, :, :], 0.0).then_inc(zeros_ready, 1)
            pool.wait_ge(w_mean_ready, 1)
            pool.wait_ge(zeros_ready, 2)
            for b in range(B):
                pool.tensor_tensor(Wbd[64:128, b, :, 64:128], W1s[64:128, :, :], m0[64:128, 1, 0:NP].unsqueeze(2).broadcast_to([64, NP, HD]),
                                   ALU.subtract).then_inc(prep_pool, 1)
            pool.wait_ge(prep_pool, B)
            pool.wait_ge(small_loaded, 16 * N_S)
            pool.wait_ge(weights_loaded, 16 * N_W)
            pool.tensor_tensor(gg[:, :], gamB[:, :], gamB[:, :], ALU.mult).then_inc(prep_pool, 1)
            pool.tensor_tensor(wog[:, :, :], wo[:, :, :], gam[:, :].unsqueeze(2).broadcast_to([P, NP, P]), ALU.mult).then_inc(prep_pool, 1)
            pool.wait_ge(prep_pool, B + 1)
            g3 = lambda t: t.rearrange("p (h c) -> p h c", h=8)
            per = lambda t: t.unsqueeze(2).broadcast_to([P, 8, HD])

            def chunk(i):
                def t(u):
                    pool.wait_ge(CHUNK["xhat_ready"], 4 * i + u + 1)
                    pool.tensor_tensor(t1[:, u, :], xh[:, u, :], gg[:, 512 * (u % 2):512 * (u % 2) + 512], ALU.mult).then_inc(CHUNK["scaled_ready"], 1)

                def q(u):
                    pool.wait_ge(CHUNK["gx_ready"], 4 * i + u + 1)
                    pool.tensor_tensor(t1[:, u, :], gx[:, u, :], xh[:, u, :], ALU.mult).then_inc(CHUNK["gx_xhat"], 1)

                def v(u):
                    pool.wait_ge(CHUNK["gx_xhat_mean"], 4 * i + u + 1)
                    pool.tensor_tensor(g3(t1[:, u, :]), g3(xh[:, u, :]), per(sm[:, u, 4, :]), ALU.mult).then_inc(CHUNK["xhat_part"], 1)

                def wa(u):
                    pool.wait_ge(CHUNK["grad_less"], 4 * i + u + 1)
                    pool.tensor_tensor(g3(gw[:, u, :]), g3(gw[:, u, :]), per(sm[:, u, 3, :]), ALU.mult).then_inc(CHUNK["grad_ready"], 1)

                t(0), t(1), q(0), t(2), q(1), v(0), t(3), q(2), v(1), wa(0), q(3), v(2), wa(1), v(3), wa(2), wa(3)

            with pool.Fori(0, NC) as i:
                chunk(i)
            pool.wait_ge(x1_ready, B)
            pool.memset(wr[:, :, :, :], 0.0).then_inc(l2_pool_step, 1)
            pool.memset(Mt[:, :, :], 0.0).then_inc(l2_pool_step, 1)
            pool.memset(Vx[:, :, :, :], 0.0).then_inc(l2_pool_step, 1)
            pool.wait_ge(l2_w_split, 1)
            pool.tensor_tensor(W1l[:, :, :], W1r[:, :, :], W1h[:, :, :], ALU.subtract).then_inc(l2_pool_step, 1)

        @block.tensor
        def _(pe):
            pe.wait_ge(consts_loaded, 16)
            for b in range(B):
                pe.wait_ge(norm_step, 3 + b)
                for t in range(NT):
                    last = pe.transpose(bank[b][:, t * P:(t + 1) * P], xn[:, b * NT + t, :], ident)
                last.then_inc(xn_turned, 1)
            pe.wait_ge(xn_turned_taken, 4)
            def mm3(to, lh, ll, rh, rl, start=True, stop=True):
                pe.matmul(to, lh, rh, start=start, stop=False, skip_group_check=True)
                pe.matmul(to, ll, rh, start=False, stop=False, skip_group_check=True)
                return pe.matmul(to, lh, rl, start=False, stop=stop, skip_group_check=True)

            def features(m, n, wh, wl):
                if counted(n):
                    pe.wait_ge(CHUNK["proj_taken"], n)
                to = bank[2 + m % 2]
                for k in range(2):
                    a = slice((2 * m + k) * P, (2 * m + k + 1) * P)
                    last = mm3(to[:, k * 256:(k + 1) * 256], wh[:, a], wl[:, a], xch[:, :], xcl[:, :])
                last.then_inc(CHUNK["proj_ready"], 1)

            pe.wait_ge(prep_dve, 1)
            pe.wait_ge(CHUNK["tokens_low"], 1)
            for m in range(4):
                features(m, m - 1, wkh, wkl)
            pe.wait_ge(prep_dve, 2)
            for i in range(NC):
                for b in range(B):
                    last = pe.matmul(bank[4][b % 2 * 64:b % 2 * 64 + 64, (i * 2 + b // 2) * H:(i * 2 + b // 2 + 1) * H],
                                     xnT[:, b * S + i * K:b * S + (i + 1) * K], Th[:, :], start=True, stop=True, skip_group_check=True)
            last.then_inc(rates_raw, 1)
            pe.wait_ge(weights_loaded, 16 * N_W)
            pe.wait_ge(small_loaded, 16 * N_S)
            for a in range(NP):
                last = pe.transpose(bank[5 + a // 4][:, a % 4 * P:(a % 4 + 1) * P], wq[:, a * P:(a + 1) * P], ident)
            last.then_inc(prep_pe, 1)
            pe.wait_ge(prep_act, 2)
            for a in range(NP):
                pe.matmul(bank[7][:, 0:P], wqT[:, a, :], wo[:, a, :], start=(a == 0), stop=(a == NP - 1))
            for a in range(NP):
                last = pe.matmul(bank[7][:, P:P + 1], wo[:, a, :], bet[:, a:a + 1], start=(a == 0), stop=(a == NP - 1))
            last.then_inc(prep_pe, 1)
            pe.wait_ge(state_ready, B + 1)
            pe.wait_ge(prep_pool, B)

            def chunk(i, live=True, before=True, more=True):
                j = i - 1

                def through(u, T, to):
                    g, hf = u // 2, u % 2
                    pe.matmul(to[:, :], half, Bst[:, g, 512 * hf:512 * hf + 512], start=True, stop=False, skip_group_check=True)
                    for a in range(4):
                        for k in range(2):
                            last = pe.matmul(to[64 * k:64 * k + 64, a * P:(a + 1) * P], T[:, 4 * hf + a, 2 * g + k, :], Wbd[:, 2 * g + k, 4 * hf + a, :],
                                             start=False, stop=True, skip_group_check=True)
                    return last

                def Z(u):
                    if live:
                        if u == 0:
                            pe.wait_ge(CHUNK["proj_taken"], 16 * i + 4)
                        if before:
                            pe.wait_ge(CHUNK["state_updated"], 4 * i)
                        if counted(4 * i + u - 1):
                            pe.wait_ge(CHUNK["xhat_ready"], 4 * i + u - 1)
                        through(u, kT, bank[u % 2]).then_inc(CHUNK["z_ready"], 1)

                def Zq(u):
                    if before:
                        if u == 0:
                            pe.wait_ge(CHUNK["proj_taken"], 16 * j + 16)
                            pe.wait_ge(CHUNK["state_updated"], 4 * i)
                        elif live:
                            pe.wait_ge(CHUNK["normed_ready"], 4 * j + u)
                        through(u, qT, bank[6 if live else u]).then_inc(CHUNK["zq_ready"], 1)

                def xku(u):
                    if live:
                        g, hf = u // 2, u % 2
                        xs, ws = slice(g * P, (g + 1) * P), slice(hf * 512, (hf + 1) * 512)
                        pe.wait_ge(CHUNK["proj_taken"], 16 * i + 3 + 2 * u)
                        mm3(bank[2][:, :], xch[:, xs], xcl[:, xs], wkh[:, ws], wkl[:, ws]).then_inc(CHUNK["proj_ready"], 1)
                        pe.wait_ge(CHUNK["proj_taken"], 16 * i + 4 + 2 * u)
                        pe.matmul(bank[3][:, :], ones[:, :], gbr[:, ws], start=True, stop=False, skip_group_check=True)
                        mm3(bank[3][:, :], xch[:, xs], xcl[:, xs], wuh[:, ws], wul[:, ws], start=False).then_inc(CHUNK["proj_ready"], 1)

                def dW(u):
                    if live:
                        pe.wait_ge(CHUNK["grad_ready"], 4 * i + u + 1)
                        if counted(4 * i + u - 1):
                            pe.wait_ge(CHUNK["state_updated"], 4 * i + u - 1)
                        if before and u == 0:
                            pe.wait_ge(CHUNK["normed_ready"], 4 * i)
                        if u == 1:
                            pe.wait_ge(CHUNK["xhat_ready"], 4 * i + 4)
                            if before:
                                pe.wait_ge(CHUNK["att_taken"], 2 * i)
                            else:
                                pe.wait_ge(ranks_taken, 1)
                        pe.matmul(bank[6 + u % 2][0:2, :], half_t, gw[:, u, :], start=True, stop=True)
                        for a in range(4):
                            for k in range(2):
                                r, c = slice(64 * k, 64 * k + 64), slice(a * P, (a + 1) * P)
                                last = pe.matmul(bank[(4, 0)[u % 2] + k][:, c], XK[r, u, c], gw[r, u, c], start=True, stop=True, skip_group_check=True)
                        last.then_inc(CHUNK["dw_ready"], 1)

                def turn(u):
                    if before:
                        pe.wait_ge(CHUNK["normed_ready"], 4 * j + u + 1)
                        if u % 2:
                            pe.wait_ge(CHUNK["turned_taken"], 4 * j + u)
                        elif counted(2 * j + u // 2):
                            pe.wait_ge(CHUNK["att_taken"], 2 * j + u // 2)
                        for a in range(4):
                            last = pe.transpose(bank[7][:, a * P:(a + 1) * P], Am[:, u % 2, a * P:(a + 1) * P], ident)
                        last.then_inc(CHUNK["normed_turned"], 1)

                def att(g):
                    if before:
                        pe.wait_ge(CHUNK["turned_taken"], 4 * j + 2 * g + 2)
                        pe.wait_ge(prep_pool, B + 2)
                        pe.wait_ge(prep_act, 4)
                        to = bank[7][:, 0:P]
                        for a in range(NP):
                            pe.matmul(to, wog[:, a, :], AT[:, a // 4, a % 4 * P:(a % 4 + 1) * P], start=(a == 0), stop=False, skip_group_check=True)
                        pe.matmul(to, Wqo[:, :], xnT[:, :].rearrange("p (b s) -> p b s", b=B)[:, 2 * g:2 * g + 2, bass.ds(j * K, K)],
                                  start=False, stop=True, skip_group_check=True).then_inc(CHUNK["att_ready"], 1)

                if not live:
                    Zq(0), Zq(1), Zq(2), Zq(3), turn(0), turn(1), att(0), turn(2), turn(3), att(1)
                    return
                Z(0), Z(1)
                if not before:
                    pe.wait_ge(prep_act, 4)
                    pe.wait_ge(wg_ready, 1)
                    for b in range(B):
                        last = pe.matmul(bank[7][0:BE, :], wgP[:, b, :], xnT[:, b * S:(b + 1) * S], start=(b == 0), stop=(b == B - 1))
                    last.then_inc(choice_logits, 1)
                    pe.wait_ge(prep_dve, 3)
                xku(0), Zq(0), Z(2), xku(1), Zq(1), Z(3), xku(2), turn(0), Zq(2), xku(3), turn(1), att(0), Zq(3)
                if live:
                    if not before:
                        pe.wait_ge(prep_dve, 4)
                    for m in range(4):
                        features(m, 16 * i + 11 + m, wqh, wql)
                turn(2), turn(3), dW(0), att(1)
                if not before:
                    pe.wait_ge(ranks_ready, 2)
                    for k in range(2):
                        for t in range(NT):
                            last = pe.transpose(bank[7][:, (k * NT + t) * BE:(k * NT + t + 1) * BE], rkp[:, k, t * P:(t + 1) * P], ident[0:BE, 0:BE])
                    last.then_inc(ranks_turned, 1)
                if more:
                    pe.wait_ge(CHUNK["tokens_low"], i + 2)
                def key(m):
                    if more:
                        features(m, 16 * i + 15 + m, wkh, wkl)

                key(0), dW(1), dW(2), key(1), dW(3), key(2), key(3)

            chunk(0, before=False)
            with pe.Fori(1, NC - 1) as i:
                chunk(i)
            chunk(NC - 1, more=False)
            chunk(NC, live=False, more=False)

            jobs = [0]

            def job(parts):
                n = jobs[0]
                jobs[0] += 1
                if n >= 4:
                    pe.wait_ge(job_taken, n - 3)
                for dst, lhs, rhs, start, stop in parts:
                    last = pe.matmul(bank[n % 4][dst], lhs, rhs, start=start, stop=stop, skip_group_check=True)
                last.then_inc(job_done, 1)

            pe.wait_ge(CHUNK["att_taken"], 2 * NC)
            for b in range(B):
                pe.wait_ge(onehot_ready, b + 1)
                job([((slice(0, P), slice(0, S)), xn[:, b * NT + t, :], OH[:, b % 2, t, :], t == 0, t == NT - 1) for t in range(NT)])
                pe.wait_ge(weighted_ready, b + 1)
                for g in range(E0 // 4):
                    n = jobs[0]
                    jobs[0] += 1
                    if n >= 4:
                        pe.wait_ge(job_taken, n - 3)
                    for t in range(NT):
                        last = pe.transpose(bank[n % 4][:, t * P:(t + 1) * P], WP[:, t, g * P:(g + 1) * P], ident)
                    last.then_inc(job_done, 1)
            n0 = jobs[0]
            pe.wait_ge(moe_loaded, 16 * N_M)
            pe.wait_ge(job_taken, n0)
            for g in range(E0 // 4):
                job([((slice(0, P), slice(j * P, (j + 1) * P)), ew[0][:, 4 * g + j, :], tokT[:, :, 4 * g + j, :], True, True) for j in range(4)])
            for g in range(E0 // 4):
                pe.wait_ge(job_taken, n0 + g + 1)
                job([((slice(0, P), slice(j * P, (j + 1) * P)), ew[1][:, 4 * g + j, :], h1[:, 4 * g + j, :], True, True) for j in range(4)])
            pe.wait_ge(w3_loaded, 16)
            for g in range(E0 // 4):
                pe.wait_ge(job_taken, n0 + 4 + g + 1)
                job([((slice(32 * j, 32 * j + 32), slice(b * P, (b + 1) * P)), h2[:, 4 * g + j, b * 32:(b + 1) * 32], ew[2][:, 4 * g + j, :], True, True)
                     for b in range(B) for j in range(4)])
            pe.wait_ge(job_taken, n0 + 12)
            for b in range(B):
                for t in range(NT):
                    to = bank[4 + b][:, t * P:(t + 1) * P]
                    pe.matmul(to, attnT[:, b * S + t * P:b * S + (t + 1) * P], ident, start=True, stop=False, skip_group_check=True)
                    for g in range(E0 // 4):
                        last = pe.matmul(to, WPT[:, b, g, t * P:(t + 1) * P], o3[:, g, b, :], start=False, stop=(g == E0 // 4 - 1), skip_group_check=True)
                last.then_inc(scattered, 1)

            pe.wait_ge(l2_loaded, 16 * N_2)
            for n in range(4):
                pe.transpose(bank[0][:, n * P:(n + 1) * P], w4[:, n, :], ident)
            pe.transpose(bank[1][:, 0:E1 * NF], b1r[:, :], ident[0:E1 * NF, 0:E1 * NF]).then_inc(l2_w_turned, 1)
            for b in range(B):
                pe.wait_ge(l2_norm_step, B + 1 + b)
                for t in range(NT):
                    last = pe.transpose(bank[2 + b][:, t * P:(t + 1) * P], xn2[:, b * NT + t, :], ident)
                last.then_inc(xn2_turned, 1)
            pe.wait_ge(xn2_turned_taken, B)
            pe.wait_ge(l2_w_split, 3)
            pe.wait_ge(l2_pool_step, 4)
            pe.wait_ge(l2_w_taken, 2)

            pe.wait_ge(w2_loaded, 16)

            def round_(i, r):
                live, has1, has2 = quads(i, r)
                s1 = [0]

                def project(k):
                    n = 12 * i + 3 * r + k
                    if counted(n - 1):
                        pe.wait_ge(ROUND["rows_taken"], n - 1)
                    j = (r - 1) % 4 if k == 0 else r
                    if k and r == 0:
                        pe.wait_ge(ROUND["xn_split"], i + 1)
                    kind = 1 if k == 1 else 0
                    last = mm3(bank[5][:, :], wrh[:, kind, j, :], wrl[:, kind, j, :], xH[:, :], xL[:, :], stop=(k != 0))
                    if k == 0:
                        pe.wait_ge(ROUND["maxima_ready"], 4 * i + r)
                        for t in range(NT):
                            last = pe.matmul(bank[5][:, t * P:(t + 1) * P], Mt[:, t, :], ident, start=False, stop=True, skip_group_check=True)
                    last.then_inc(ROUND["rows_ready"], 1)

                def scores():
                    n = s1[0]
                    s1[0] += 1
                    t, h = n // QH, n % QH
                    rows = slice(64 * (h // 2), 64 * (h // 2) + 64)
                    if n == 0:
                        pe.wait_ge(ROUND["q_masked"], 8 * i + 2 * r + 1)
                    if counted(64 * i + 16 * r + n):
                        pe.wait_ge(ROUND["score_max"], 64 * i + 16 * r + n)
                    pe.matmul(bank[3][:, :], qx[rows, h % 2, t * P:(t + 1) * P], kx[rows, r % 2, :], start=True, stop=True).then_inc(ROUND["scores_ready"], 1)

                def turned_scores(n):
                    t, h = n // QH, n % QH
                    rows = slice(64 * (h // 2), 64 * (h // 2) + 64)
                    if n == 0:
                        pe.wait_ge(ROUND["q_masked"], 8 * i + 2 * r)
                    if n % 8 > 1:
                        pe.wait_ge(ROUND["exps_ready"], 64 * i + 16 * r - 16 + n - 1)
                    elif live:
                        pe.wait_ge(ROUND["gelu_ready"], 64 * i + 16 * r + n // 8 * 8 + 7 + n % 8)
                    elif counted(64 * i + 16 * r - 16 + n - 1):
                        pe.wait_ge(ROUND["exps_ready"], 64 * i + 16 * r - 16 + n - 1)
                    pe.matmul(bank[n % 2][:, :], kx[rows, (r - 1) % 2, t * P:(t + 1) * P], qm[rows, h % 2, :], start=True, stop=True).then_inc(ROUND["turned_ready"], 1)

                def values(c, t):
                    j = (r - c) % 4
                    if t == 0:
                        if r == 1 and c == 1:
                            pe.wait_ge(ROUND["v_spread"], i + 1)
                        if counted(4 * i + r - c):
                            pe.wait_ge(ROUND["heads_taken"], 4 * i + r - c)
                    pe.wait_ge(ROUND["exps_ready"], 64 * i + 16 * (r - c) + 4 * t + 4)
                    for h in range(QH):
                        pe.matmul(bank[6][32 * h:32 * h + 32, :], Vx[:, t, QH * j + h, :], ex[:, (4 * t + h) % 8, :], start=(t == 0), stop=(t == NT - 1),
                                  skip_group_check=True).then_inc(ROUND["values_summed"], 1)

                def hidden(n):
                    m = 64 * i + 16 * r + n
                    e, a = n // NF, n % NF
                    if n == 0:
                        pe.wait_ge(ROUND["cur_split"], 4 * i + r + 1)
                    if n % 8 > 1 or not has1 and counted(m - 1):
                        pe.wait_ge(ROUND["gelu_ready"], m - 1)
                    if n % 8 <= 1 and counted(64 * i + 16 * r - 16 + n // 8 * 8 - 1 + n % 8):
                        pe.wait_ge(ROUND["exps_ready"], 64 * i + 16 * r - 16 + n // 8 * 8 - 1 + n % 8)
                    c = slice(a * P, (a + 1) * P)
                    mm3(bank[n % 2][:, :], W1h[:, e, c], W1l[:, e, c], cH[:, :], cL[:, :]).then_inc(ROUND["hidden_ready"], 1)

                def outputs(n):
                    e, a = n // NF, n % NF
                    if a == 0 and counted(16 * i + 4 * r + e - 1):
                        pe.wait_ge(ROUND["expert_added"], 16 * i + 4 * r + e - 1)
                    pe.wait_ge(ROUND["gelu_ready"], 64 * i + 16 * r + n + 1)
                    to = bank[2 + 2 * (e % 2)]
                    for t in range(NT):
                        last = pe.matmul(to[:, t * P:(t + 1) * P], hd[:, n % 8, t * P:(t + 1) * P], W2[:, e, a, :],
                                         start=(a == 0 and t == 0), stop=(a == NF - 1), skip_group_check=True)
                    last.then_inc(ROUND["outputs_ready"], 1)

                def logits():
                    pe.wait_ge(ROUND["cur_taken"], 4 * i + r + 1)
                    if r == 0 and counted(4 * i + r):
                        pe.wait_ge(ROUND["bias_added"], 4 * i + r)
                    for t in range(NT):
                        last = pe.matmul(bank[7][:, t * E1:(t + 1) * E1],
                                         curT[:, t * P:(t + 1) * P], Wg1[:, r, :], start=True, stop=True, skip_group_check=True)
                    last.then_inc(ROUND["logits_ready"], 1)

                def turn_out():
                    pe.wait_ge(ROUND["heads_taken"], 4 * i + r - 1)
                    if live:
                        pe.wait_ge(ROUND["logits_taken"], 4 * i + r + 1)
                    elif r:
                        pe.wait_ge(ROUND["heads_divided"], 4 * i + r - 2)
                    else:
                        pe.wait_ge(ROUND["bias_added"], 4 * i)
                    for t in range(NT):
                        last = pe.transpose(bank[7][:, t * P:(t + 1) * P], ob[:, t * P:(t + 1) * P], ident)
                    last.then_inc(ROUND["heads_turned"], 1)

                def turn_weights():
                    pe.wait_ge(ROUND["gates_ready"], 4 * i + r + 1)
                    for t in range(NT):
                        last = pe.transpose(bank[7][0:E1, t * P:(t + 1) * P], cw[:, t, :], ident)
                    last.then_inc(ROUND["gates_turned"], 1)

                def biases():
                    pe.wait_ge(ROUND["gates_taken"], 4 * i + r + 1)
                    for t in range(NT):
                        last = pe.matmul(bank[7][:, t * P:(t + 1) * P], cwT[:, t * P:(t + 1) * P], b2r[:, :], start=True, stop=True, skip_group_check=True)
                    last.then_inc(ROUND["bias_ready"], 1)

                def turn_heads():
                    pe.wait_ge(ROUND["heads_divided"], 4 * i)
                    if live:
                        pe.wait_ge(ROUND["bias_added"], 4 * i + r + 1)
                    for t in range(NT):
                        last = pe.transpose(bank[7][:, t * P:(t + 1) * P], an[:, t, :], ident)
                    last.then_inc(ROUND["att_turned"], 1)

                def attention_out():
                    pe.wait_ge(ROUND["att_turned_taken"], i)
                    for t in range(NT):
                        last = pe.matmul(bank[7][:, t * P:(t + 1) * P], aT[:, t * P:(t + 1) * P], wT4[:, 3, :], start=True, stop=True, skip_group_check=True)
                    last.then_inc(ROUND["att_out"], 1)

                if has2:
                    values(2, 2)
                    values(2, 3)
                if live and r:
                    pe.wait_ge(ROUND["expert_added"], 16 * i + 4 * r)
                    if r == 2 and counted(i):
                        pe.wait_ge(ROUND["result_ready"], i)
                    for t in range(NT):
                        last = pe.transpose(bank[7][:, t * P:(t + 1) * P], cur[:, t, :], ident)
                    last.then_inc(ROUND["cur_turned"], 1)
                if has1:
                    project(0)
                for n in range(8 if live else 0):
                    hidden(n)
                    if n == 1:
                        logits()
                    if n == 2:
                        project(1)
                    if n == 4 and has2:
                        turn_out()
                    if n == 5:
                        project(2)
                    if n == 6 and r == 0:
                        pe.wait_ge(ROUND["heads_divided" if has2 else "logits_taken"], 4 * i + r - 1 if has2 else 1)
                        for t in range(NT):
                            last = pe.matmul(bank[7][:, t * P:(t + 1) * P], curT[:, t * P:(t + 1) * P], wT4[:, 2, :], start=True, stop=True, skip_group_check=True)
                        last.then_inc(ROUND["v_ready"], 1)
                if has2 and not live:
                    turn_out()
                for n in range(24):
                    k = n if n < 8 else n - 8 if n >= 16 else None
                    if k is not None and live:
                        outputs(k)
                    if k is not None and has1:
                        turned_scores(k)
                    if k is None and live:
                        hidden(n)
                    if n in (8, 9) and has1:
                        values(1, n - 8)
                    if live and n == 3:
                        if has2:
                            pe.wait_ge(ROUND["heads_divided"], 4 * i + r - 1)
                        if r == 0:
                            pe.wait_ge(ROUND["v_taken"], i + 1)
                        turn_weights()
                    if live and n == 5:
                        biases()
                    if live:
                        for _ in range(SCORES.get(n, 0)):
                            scores()
                    if n == 9 and r == 1 and has2:
                        turn_heads()
                    if n == 12 and r == 1 and has2:
                        attention_out()
                if live and r < 3 or has1:
                    pass

            for r in range(R1):
                round_(0, r)
            with pe.Fori(1, B) as i:
                for r in range(R1):
                    round_(i, r)
            for r in range(2):
                round_(B, r)


_INS = ["L0_attn_hidden_states", "L0_attn_wq", "L0_attn_wk", "L0_attn_wv", "L0_attn_wo", "L0_attn_W1", "L0_attn_b1", "L0_attn_theta",
        "L0_attn_theta_bias", "L0_attn_alpha", "L0_attn_gamma", "L0_attn_beta", "L0_ffn_Wg", "L0_ffn_bg", "L0_ffn_w1", "L0_ffn_b1",
        "L0_ffn_w2", "L0_ffn_b2", "L0_ffn_w3", "L0_ffn_b3", "L1_attn_Wq", "L1_attn_Wk", "L1_attn_Wv", "L1_attn_Wo", "L1_attn_bo",
        "L1_ffn_Wg", "L1_ffn_bg", "L1_ffn_W1", "L1_ffn_b1", "L1_ffn_W2", "L1_ffn_b2"]


def kernel(**inputs):
    import numpy as _np
    import concourse.bacc as _bacc
    from concourse import mybir as _mybir
    from concourse.bass_utils import run_bass_kernel_spmd as _run

    nc = _bacc.Bacc("TRN2", target_bir_lowering=False, num_devices=1)
    arrays, aps = {}, {}
    for name in _INS:
        a = _np.ascontiguousarray(inputs[name])
        arrays[f"in_{name}"] = a
        aps[name] = nc.dram_tensor(f"in_{name}", a.shape, _mybir.dt.from_np(a.dtype), kind="ExternalInput").ap()
    c = constants(_np)
    arrays["constants"] = c
    const_d = nc.dram_tensor("constants", c.shape, _mybir.dt.float32, kind="ExternalInput").ap()
    out = nc.dram_tensor("out_0", (B, S, P), _mybir.dt.float32, kind="ExternalOutput").ap()
    build(nc, aps, out, const_d)
    r = _run(nc, [arrays], core_ids=[0])
    return r.results[0]["out_0"]
```
